# Optimizing a Trainium2 kernel written in Bass

```python
import numpy as np
import jax
import jax.numpy as jnp

def _softmax(x, axis=-1):
    return jax.nn.softmax(x, axis=axis)

def _gelu(x):
    return jax.nn.gelu(x, approximate=True)

def _silu(x):
    return jax.nn.silu(x)

def _sigmoid(x):
    return jax.nn.sigmoid(x)

def _layernorm(x, axis=-1, eps=1e-05):
    m = jnp.mean(x, axis=axis, keepdims=True)
    v = jnp.var(x, axis=axis, keepdims=True)
    return (x - m) / jnp.sqrt(v + eps)

def _scatter_add(tgt, idx, src, axis=0):
    return tgt.at[idx].add(src)

def _segment_sum(src, seg, n):
    return jax.ops.segment_sum(src, seg, n)
kernel_name = 'mk_early_fusion_embed_d2_tok_img1024_r4_910a05'

def setup_inputs(seed: int=0):
    np.random.seed(seed)
    _w = jnp.asarray

    def _rec_inputs():
        import jax
        import jax.numpy as jnp
        _rk = jax.random.key(seed)
        x = -0.00016672 + 0.999947 * jax.random.normal(jax.random.fold_in(_rk, 1), (32, 3, 96, 96), jnp.float32)
        x_txt = jax.random.randint(jax.random.fold_in(_rk, 51), (32, 128), 0, 64, jnp.int32)
        return (x, x_txt)
    x, x_txt = _rec_inputs()

    def _L0_tok_setup():
        import jax, jax.numpy as jnp
        import numpy as np
        key = jax.random.key(seed)
        kx, kw, kpos = jax.random.split(key, 3)
        B, C, H, W = (64, 3, 96, 96)
        p, dim = (16, 256)
        n_patches = H // p * (W // p)
        x = jax.random.normal(kx, (B, C, H, W), dtype=jnp.float32)
        w = jax.random.normal(kw, (dim, C * p * p), dtype=jnp.float32) * 0.02
        b = jnp.zeros((dim,), dtype=jnp.float32)
        cls_token = jnp.ones((dim,), dtype=jnp.float32)
        pos = jax.random.uniform(kpos, (n_patches + 1, dim), dtype=jnp.float32)
        return {'x': x, 'w': w, 'b': b, 'cls_token': cls_token, 'pos': pos, 'patch_size': p}
    _L0_tok_all = _L0_tok_setup()
    _L0_tok_in = {k: v for k, v in _L0_tok_all.items() if k in ('w', 'b', 'cls_token', 'pos')}
    del _L0_tok_all

    def _L0_txt_setup():
        import jax, jax.numpy as jnp
        import numpy as np
        VOCAB = 64
        CHAR_DIM = 128
        N_FREQ = 4
        EMBED_DIM = 256
        BLOCK = 1024
        B, T = (8, 1024)
        key = jax.random.key(seed)
        k1, k2, k3, k4, k5 = jax.random.split(key, 5)
        raw_char_indices = jax.random.randint(k1, (B, T), 0, VOCAB, dtype=jnp.int32)
        emb_tables = jax.random.normal(k2, (N_FREQ, VOCAB, CHAR_DIM), dtype=jnp.float32) * 0.02
        W = jax.random.normal(k3, (N_FREQ * CHAR_DIM, EMBED_DIM), dtype=jnp.float32) * 0.02
        b = jnp.zeros((EMBED_DIM,), dtype=jnp.float32)
        pos_table = jax.random.normal(k4, (BLOCK, EMBED_DIM), dtype=jnp.float32) * 0.02
        return {'raw_char_indices': raw_char_indices, 'emb_tables': emb_tables, 'W': W, 'b': b, 'pos_table': pos_table}
    _L0_txt_all = _L0_txt_setup()
    _L0_txt_in = {k: v for k, v in _L0_txt_all.items() if k in ('emb_tables', 'W', 'b', 'pos_table')}
    del _L0_txt_all

    def _L0_attn_setup():
        import jax, jax.numpy as jnp
        import numpy as np
        LN_EPS = 1e-05
        NEG_INF = -1e+38

        def _layer_norm(x, g, b):
            mu = x.mean(-1, keepdims=True)
            var = ((x - mu) ** 2).mean(-1, keepdims=True)
            return (x - mu) * jax.lax.rsqrt(var + LN_EPS) * g + b

        def _wkv(w, u, k, v):
            B, T, C = k.shape
            kt = jnp.swapaxes(k, 0, 1)
            vt = jnp.swapaxes(v, 0, 1)
            aa0 = jnp.zeros((B, C), k.dtype)
            bb0 = jnp.zeros((B, C), k.dtype)
            pp0 = jnp.full((B, C), NEG_INF, k.dtype)

            def step(carry, inp):
                aa, bb, pp = carry
                kk, vv = inp
                p = jnp.maximum(pp, u + kk)
                e1 = jnp.exp(pp - p)
                e2 = jnp.exp(u + kk - p)
                y = (e1 * aa + e2 * vv) / (e1 + e2)
                p2 = jnp.maximum(pp + w, w + kk)
                e1u = jnp.exp(pp + w - p2)
                e2u = jnp.exp(w + kk - p2)
                aa2 = e1u * aa + e2u * vv
                bb2 = e1u + e2u
                pp2 = p2 + jnp.log(bb2)
                return ((aa2, bb2, pp2), y)
            _, ys = jax.lax.scan(step, (aa0, bb0, pp0), (kt, vt))
            return jnp.swapaxes(ys, 0, 1)

        def _shift(h):
            return jnp.pad(h[:, :-1, :], ((0, 0), (1, 0), (0, 0)))
        key = jax.random.key(seed)
        B, T, C = (8, 512, 256)
        ks = jax.random.split(key, 12)
        s = 0.02
        return {'x': jax.random.normal(ks[0], (B, T, C), jnp.float32), 'time_decay': jax.random.normal(ks[1], (C,), jnp.float32) * 0.01, 'time_first': jax.random.normal(ks[2], (C,), jnp.float32) * 0.01, 'w_tk': jax.random.normal(ks[3], (C, C), jnp.float32) * s, 'w_tv': jax.random.normal(ks[4], (C, C), jnp.float32) * s, 'w_tr': jax.random.normal(ks[5], (C, C), jnp.float32) * s, 'w_ck': jax.random.normal(ks[6], (C, 4 * C), jnp.float32) * s, 'w_cv': jax.random.normal(ks[7], (4 * C, C), jnp.float32) * s, 'w_cr': jax.random.normal(ks[8], (C, C), jnp.float32) * s, 'ln1_g': jnp.ones((C,), jnp.float32), 'ln1_b': jnp.zeros((C,), jnp.float32), 'ln2_g': jnp.ones((C,), jnp.float32), 'ln2_b': jnp.zeros((C,), jnp.float32), 'mix_k': jnp.ones((1, 1, C), jnp.float32), 'mix_v': jnp.ones((1, 1, C), jnp.float32), 'mix_r': jnp.ones((1, 1, C), jnp.float32), 'cmix_k': jnp.ones((1, 1, C), jnp.float32), 'cmix_r': jnp.ones((1, 1, C), jnp.float32)}
    _L0_attn_all = _L0_attn_setup()
    _L0_attn_in = {k: v for k, v in _L0_attn_all.items() if k in ('time_decay', 'time_first', 'w_tk', 'w_tv', 'w_tr', 'w_ck', 'w_cv', 'w_cr', 'ln1_g', 'ln1_b', 'ln2_g', 'ln2_b', 'mix_k', 'mix_v', 'mix_r', 'cmix_k', 'cmix_r')}
    del _L0_attn_all

    def _L0_ffn_setup():
        import jax, jax.numpy as jnp
        import numpy as np
        EMBED_DIM = 256
        MLP_RATIO = 4
        NUM_EXPERTS = 8
        CAPACITY = 1.0
        LN_EPS = 1e-05

        def _layernorm(y, gamma, beta):
            mu = jnp.mean(y, axis=-1, keepdims=True)
            var = jnp.mean(jnp.square(y - mu), axis=-1, keepdims=True)
            return (y - mu) * jax.lax.rsqrt(var + LN_EPS) * gamma + beta
        key = jax.random.key(seed)
        k0, k1, k2, k3, k4, k5 = jax.random.split(key, 6)
        d = EMBED_DIM
        dd = EMBED_DIM * MLP_RATIO
        n = NUM_EXPERTS
        x = jax.random.normal(k0, (4, 512, d), dtype=jnp.float32)
        gate_w = jax.random.normal(k1, (n, d), dtype=jnp.float32) * 0.02
        ln_gamma = jnp.ones((d,), dtype=jnp.float32)
        ln_beta = jnp.zeros((d,), dtype=jnp.float32)
        fc1s = jax.random.normal(k2, (n, dd, d), dtype=jnp.float32) * (1.0 / np.sqrt(d))
        b1s = jax.random.normal(k3, (n, dd), dtype=jnp.float32) * 0.02
        fc2s = jax.random.normal(k4, (n, d, dd), dtype=jnp.float32) * (1.0 / np.sqrt(dd))
        b2s = jax.random.normal(k5, (n, d), dtype=jnp.float32) * 0.02
        return {'x': x, 'gate_w': gate_w, 'ln_gamma': ln_gamma, 'ln_beta': ln_beta, 'fc1s': fc1s, 'b1s': b1s, 'fc2s': fc2s, 'b2s': b2s}
    _L0_ffn_all = _L0_ffn_setup()
    _L0_ffn_in = {k: v for k, v in _L0_ffn_all.items() if k in ('gate_w', 'ln_gamma', 'ln_beta', 'fc1s', 'b1s', 'fc2s', 'b2s')}
    del _L0_ffn_all

    def _L1_attn_setup():
        import jax, jax.numpy as jnp
        import numpy as np
        from jax import lax
        B, T, HID, NH = (4, 512, 256, 16)
        D = HID // NH
        LN_EPS = 1e-05
        NORM_EPS = 1e-06
        key = jax.random.key(seed)
        ks = jax.random.split(key, 3)
        s = 0.02
        return {'x': jax.random.normal(ks[0], (B, T, HID), jnp.float32), 'ln_g': jnp.ones((HID,), jnp.float32), 'ln_b': jnp.zeros((HID,), jnp.float32), 'w_qkvb': jax.random.normal(ks[1], (HID, 4 * HID), jnp.float32) * s, 'b_qkvb': jnp.zeros((4 * HID,), jnp.float32), 'w_out': jax.random.normal(ks[2], (HID, HID), jnp.float32) * s, 'b_out': jnp.zeros((HID,), jnp.float32)}
    _L1_attn_all = _L1_attn_setup()
    _L1_attn_in = {k: v for k, v in _L1_attn_all.items() if k in ('ln_g', 'ln_b', 'w_qkvb', 'b_qkvb', 'w_out', 'b_out')}
    del _L1_attn_all

    def _L1_ffn_setup():
        import jax, jax.numpy as jnp
        import numpy as np
        B, S, D, E = (2, 512, 256, 8)
        key = jax.random.key(seed)
        ks = jax.random.split(key, 5)
        x = jax.random.normal(ks[0], (B, S, D), dtype=jnp.float32)
        router_w = jax.random.normal(ks[1], (E, D), dtype=jnp.float32) * 0.02
        router_b = jnp.zeros((E,), dtype=jnp.float32)
        expert_w = jax.random.normal(ks[2], (E, D, D), dtype=jnp.float32) * 0.02
        expert_b = jnp.zeros((E, D), dtype=jnp.float32)
        return {'x': x, 'router_w': router_w, 'router_b': router_b, 'expert_w': expert_w, 'expert_b': expert_b}
    _L1_ffn_all = _L1_ffn_setup()
    _L1_ffn_in = {k: v for k, v in _L1_ffn_all.items() if k in ('router_w', 'router_b', 'expert_w', 'expert_b')}
    del _L1_ffn_all
    return {'x': x, 'x_txt': x_txt, 'L0_tok_w': _L0_tok_in['w'], 'L0_tok_b': _L0_tok_in['b'], 'L0_tok_cls_token': _L0_tok_in['cls_token'], 'L0_tok_pos': _L0_tok_in['pos'], 'L0_txt_emb_tables': _L0_txt_in['emb_tables'], 'L0_txt_W': _L0_txt_in['W'], 'L0_txt_b': _L0_txt_in['b'], 'L0_txt_pos_table': _L0_txt_in['pos_table'], 'L0_attn_time_decay': _L0_attn_in['time_decay'], 'L0_attn_time_first': _L0_attn_in['time_first'], 'L0_attn_w_tk': _L0_attn_in['w_tk'], 'L0_attn_w_tv': _L0_attn_in['w_tv'], 'L0_attn_w_tr': _L0_attn_in['w_tr'], 'L0_attn_w_ck': _L0_attn_in['w_ck'], 'L0_attn_w_cv': _L0_attn_in['w_cv'], 'L0_attn_w_cr': _L0_attn_in['w_cr'], 'L0_attn_ln1_g': _L0_attn_in['ln1_g'], 'L0_attn_ln1_b': _L0_attn_in['ln1_b'], 'L0_attn_ln2_g': _L0_attn_in['ln2_g'], 'L0_attn_ln2_b': _L0_attn_in['ln2_b'], 'L0_attn_mix_k': _L0_attn_in['mix_k'], 'L0_attn_mix_v': _L0_attn_in['mix_v'], 'L0_attn_mix_r': _L0_attn_in['mix_r'], 'L0_attn_cmix_k': _L0_attn_in['cmix_k'], 'L0_attn_cmix_r': _L0_attn_in['cmix_r'], 'L0_ffn_gate_w': _L0_ffn_in['gate_w'], 'L0_ffn_ln_gamma': _L0_ffn_in['ln_gamma'], 'L0_ffn_ln_beta': _L0_ffn_in['ln_beta'], 'L0_ffn_fc1s': _L0_ffn_in['fc1s'], 'L0_ffn_b1s': _L0_ffn_in['b1s'], 'L0_ffn_fc2s': _L0_ffn_in['fc2s'], 'L0_ffn_b2s': _L0_ffn_in['b2s'], 'L1_attn_ln_g': _L1_attn_in['ln_g'], 'L1_attn_ln_b': _L1_attn_in['ln_b'], 'L1_attn_w_qkvb': _L1_attn_in['w_qkvb'], 'L1_attn_b_qkvb': _L1_attn_in['b_qkvb'], 'L1_attn_w_out': _L1_attn_in['w_out'], 'L1_attn_b_out': _L1_attn_in['b_out'], 'L1_ffn_router_w': _L1_ffn_in['router_w'], 'L1_ffn_router_b': _L1_ffn_in['router_b'], 'L1_ffn_expert_w': _L1_ffn_in['expert_w'], 'L1_ffn_expert_b': _L1_ffn_in['expert_b']}

def reference(x, x_txt, L0_tok_w, L0_tok_b, L0_tok_cls_token, L0_tok_pos, L0_txt_emb_tables, L0_txt_W, L0_txt_b, L0_txt_pos_table, L0_attn_time_decay, L0_attn_time_first, L0_attn_w_tk, L0_attn_w_tv, L0_attn_w_tr, L0_attn_w_ck, L0_attn_w_cv, L0_attn_w_cr, L0_attn_ln1_g, L0_attn_ln1_b, L0_attn_ln2_g, L0_attn_ln2_b, L0_attn_mix_k, L0_attn_mix_v, L0_attn_mix_r, L0_attn_cmix_k, L0_attn_cmix_r, L0_ffn_gate_w, L0_ffn_ln_gamma, L0_ffn_ln_beta, L0_ffn_fc1s, L0_ffn_b1s, L0_ffn_fc2s, L0_ffn_b2s, L1_attn_ln_g, L1_attn_ln_b, L1_attn_w_qkvb, L1_attn_b_qkvb, L1_attn_w_out, L1_attn_b_out, L1_ffn_router_w, L1_ffn_router_b, L1_ffn_expert_w, L1_ffn_expert_b):
    import jax
    import jax.numpy as jnp

    def _L0_tok_ref(x, w, b, cls_token, pos, patch_size):
        import jax, jax.numpy as jnp
        import numpy as np
        B, C, H, W = x.shape
        p = patch_size
        Hp, Wp = (H // p, W // p)
        dim = w.shape[0]
        patches = x.reshape(B, C, Hp, p, Wp, p).transpose(0, 2, 4, 1, 3, 5).reshape(B, Hp * Wp, C * p * p)
        tokens = jnp.einsum('bnf,df->bnd', patches, w) + b
        cls = jnp.broadcast_to(cls_token, (B, 1, dim))
        emb = jnp.concatenate([cls, tokens], axis=1)
        return emb + pos

    def _L0_txt_ref(raw_char_indices, emb_tables, W, b, pos_table):
        import jax, jax.numpy as jnp
        import numpy as np
        VOCAB = 64
        CHAR_DIM = 128
        N_FREQ = 4
        EMBED_DIM = 256
        BLOCK = 1024
        B, T = (8, 1024)
        g = emb_tables[:, raw_char_indices]
        x = jnp.transpose(g, (1, 2, 0, 3)).reshape(g.shape[1], g.shape[2], -1)
        x = jnp.einsum('btk,ke->bte', x, W) + b
        Tlen = raw_char_indices.shape[1]
        x = x + pos_table[:Tlen]
        return x

    def _L0_attn_ref(x, time_decay, time_first, w_tk, w_tv, w_tr, w_ck, w_cv, w_cr, ln1_g, ln1_b, ln2_g, ln2_b, mix_k, mix_v, mix_r, cmix_k, cmix_r):
        import jax, jax.numpy as jnp
        import numpy as np
        LN_EPS = 1e-05
        NEG_INF = -1e+38

        def _layer_norm(x, g, b):
            mu = x.mean(-1, keepdims=True)
            var = ((x - mu) ** 2).mean(-1, keepdims=True)
            return (x - mu) * jax.lax.rsqrt(var + LN_EPS) * g + b

        def _wkv(w, u, k, v):
            B, T, C = k.shape
            kt = jnp.swapaxes(k, 0, 1)
            vt = jnp.swapaxes(v, 0, 1)
            aa0 = jnp.zeros((B, C), k.dtype)
            bb0 = jnp.zeros((B, C), k.dtype)
            pp0 = jnp.full((B, C), NEG_INF, k.dtype)

            def step(carry, inp):
                aa, bb, pp = carry
                kk, vv = inp
                p = jnp.maximum(pp, u + kk)
                e1 = jnp.exp(pp - p)
                e2 = jnp.exp(u + kk - p)
                y = (e1 * aa + e2 * vv) / (e1 + e2)
                p2 = jnp.maximum(pp + w, w + kk)
                e1u = jnp.exp(pp + w - p2)
                e2u = jnp.exp(w + kk - p2)
                aa2 = e1u * aa + e2u * vv
                bb2 = e1u + e2u
                pp2 = p2 + jnp.log(bb2)
                return ((aa2, bb2, pp2), y)
            _, ys = jax.lax.scan(step, (aa0, bb0, pp0), (kt, vt))
            return jnp.swapaxes(ys, 0, 1)

        def _shift(h):
            return jnp.pad(h[:, :-1, :], ((0, 0), (1, 0), (0, 0)))
        h = _layer_norm(x, ln1_g, ln1_b)
        hp = _shift(h)
        xk = h * mix_k + hp * (1.0 - mix_k)
        xv = h * mix_v + hp * (1.0 - mix_v)
        xr = h * mix_r + hp * (1.0 - mix_r)
        k = xk @ w_tk
        v = xv @ w_tv
        r = jax.nn.sigmoid(xr @ w_tr)
        y = _wkv(time_decay, time_first, k, v)
        x = x + r * y
        h2 = _layer_norm(x, ln2_g, ln2_b)
        hp2 = _shift(h2)
        ck = h2 * cmix_k + hp2 * (1.0 - cmix_k)
        cr = h2 * cmix_r + hp2 * (1.0 - cmix_r)
        kk = jnp.square(jax.nn.relu(ck @ w_ck))
        x = x + jax.nn.sigmoid(cr @ w_cr) * (kk @ w_cv)
        return x

    def _L0_ffn_ref(x, gate_w, ln_gamma, ln_beta, fc1s, b1s, fc2s, b2s):
        import jax, jax.numpy as jnp
        import numpy as np
        EMBED_DIM = 256
        MLP_RATIO = 4
        NUM_EXPERTS = 8
        CAPACITY = 1.0
        LN_EPS = 1e-05

        def _layernorm(y, gamma, beta):
            mu = jnp.mean(y, axis=-1, keepdims=True)
            var = jnp.mean(jnp.square(y - mu), axis=-1, keepdims=True)
            return (y - mu) * jax.lax.rsqrt(var + LN_EPS) * gamma + beta
        og_shape = x.shape
        d = og_shape[-1]
        xf = x.reshape(-1, d)
        bs = xf.shape[0]
        n = gate_w.shape[0]
        k = int(bs * CAPACITY) // n
        scores = xf @ gate_w.T
        scores = (jnp.tanh(scores) + 1.0) * 0.5
        vals, idx = jax.lax.top_k(scores.T, k)
        kept_w = vals.T
        flat_idx = idx.T.reshape(-1)
        y = xf[flat_idx].reshape(k, n, d)
        y = _layernorm(y, ln_gamma, ln_beta)
        h = jnp.einsum('knd,nfd->knf', y, fc1s) + b1s
        h = jax.nn.gelu(h, approximate=True)
        o = jnp.einsum('knf,ndf->knd', h, fc2s) + b2s
        o = o * kept_w[:, :, None]
        out = xf.at[flat_idx].add(o.reshape(k * n, d))
        return out.reshape(og_shape)

    def _L1_attn_ref(x, ln_g, ln_b, w_qkvb, b_qkvb, w_out, b_out):
        import jax, jax.numpy as jnp
        import numpy as np
        from jax import lax
        B, T, HID, NH = (4, 512, 256, 16)
        D = HID // NH
        LN_EPS = 1e-05
        NORM_EPS = 1e-06
        b, t = x.shape[:2]
        mu = jnp.mean(x, axis=-1, keepdims=True)
        var = jnp.mean((x - mu) ** 2, axis=-1, keepdims=True)
        normed = (x - mu) * lax.rsqrt(var + LN_EPS) * ln_g + ln_b
        proj = normed @ w_qkvb + b_qkvb
        q, k, v, beta_pre = jnp.split(proj, 4, axis=-1)
        beta = jax.nn.sigmoid(beta_pre)

        def heads(a):
            return a.reshape(b, t, NH, D).transpose(1, 0, 2, 3)
        q, k, v, beta = (heads(q), heads(k), heads(v), heads(beta))
        k = k / jnp.maximum(jnp.linalg.norm(k, axis=-1, keepdims=True), NORM_EPS)
        S0 = jnp.zeros((b, NH, D, D), x.dtype)

        def step(S, inp):
            q_t, k_t, v_t, beta_t = inp
            retrieval = jnp.einsum('bhij,bhj->bhi', S, k_t)
            S = S + jnp.einsum('bhi,bhj->bhij', beta_t * (v_t - retrieval), k_t)
            o_t = jnp.einsum('bhij,bhj->bhi', S, q_t)
            return (S, o_t)
        _, out_t = lax.scan(step, S0, (q, k, v, beta))
        scan_out = out_t.transpose(1, 0, 2, 3).reshape(b, t, NH * D)
        return x + scan_out @ w_out + b_out

    def _L1_ffn_ref(x, router_w, router_b, expert_w, expert_b):
        import jax, jax.numpy as jnp
        import numpy as np
        B, S, D, E = (2, 512, 256, 8)
        logits = jnp.einsum('bsd,ed->bse', x, router_w) + router_b
        probs = jax.nn.softmax(logits, axis=-1)
        weights = jnp.max(probs, axis=-1)
        top1 = jnp.argmax(probs, axis=-1)
        y_all = jnp.einsum('bsd,eod->bseo', x, expert_w) + expert_b
        y = jnp.take_along_axis(y_all, top1[:, :, None, None], axis=2)[:, :, 0, :]
        out = y * weights[:, :, None]
        return out
    h = _L0_tok_ref(x, L0_tok_w, L0_tok_b, L0_tok_cls_token, L0_tok_pos, 16)
    h = jnp.concatenate([h, _L0_txt_ref(x_txt, L0_txt_emb_tables, L0_txt_W, L0_txt_b, L0_txt_pos_table)], axis=1)
    h = h + _L0_attn_ref(_layernorm(h, axis=-1), L0_attn_time_decay, L0_attn_time_first, L0_attn_w_tk, L0_attn_w_tv, L0_attn_w_tr, L0_attn_w_ck, L0_attn_w_cv, L0_attn_w_cr, L0_attn_ln1_g, L0_attn_ln1_b, L0_attn_ln2_g, L0_attn_ln2_b, L0_attn_mix_k, L0_attn_mix_v, L0_attn_mix_r, L0_attn_cmix_k, L0_attn_cmix_r)
    h = h + _L0_ffn_ref(_layernorm(h, axis=-1), L0_ffn_gate_w, L0_ffn_ln_gamma, L0_ffn_ln_beta, L0_ffn_fc1s, L0_ffn_b1s, L0_ffn_fc2s, L0_ffn_b2s)
    h = h + _L1_attn_ref(_layernorm(h, axis=-1), L1_attn_ln_g, L1_attn_ln_b, L1_attn_w_qkvb, L1_attn_b_qkvb, L1_attn_w_out, L1_attn_b_out)
    h = h + _L1_ffn_ref(_layernorm(h, axis=-1), L1_ffn_router_w, L1_ffn_router_b, L1_ffn_expert_w, L1_ffn_expert_b)
    return h

_drawn_inputs = setup_inputs


def setup_inputs(seed=0):
    import zlib

    import numpy as np

    out = dict(_drawn_inputs(seed))
    spreads = {'L0_tok_b': (0.0, 0.1),
     'L0_tok_cls_token': (1.0, 0.2),
     'L0_txt_b': (0.0, 0.1),
     'L0_attn_ln1_g': (1.0, 0.2),
     'L0_attn_ln1_b': (0.0, 0.1),
     'L0_attn_ln2_g': (1.0, 0.6),
     'L0_attn_ln2_b': (0.0, 0.659),
     'L0_attn_mix_k': (1.0, 0.2),
     'L0_attn_mix_v': (1.0, 0.2),
     'L0_attn_mix_r': (1.0, 0.6),
     'L0_attn_cmix_k': (1.0, 0.6),
     'L0_attn_cmix_r': (1.0, 0.6),
     'L0_ffn_ln_gamma': (1.0, 0.2),
     'L0_ffn_ln_beta': (0.0, 0.435),
     'L1_attn_ln_g': (1.0, 0.6),
     'L1_attn_ln_b': (0.0, 0.8),
     'L1_attn_b_qkvb': (0.0, 0.635),
     'L1_attn_b_out': (0.0, 0.1),
     'L1_ffn_router_b': (0.0, 0.644),
     'L1_ffn_expert_b': (0.0, 0.8)}
    factors = {'L0_attn_time_first': 178.4,
     'L0_attn_w_cr': 3.91,
     'L0_ffn_b1s': 8.0,
     'L0_ffn_b2s': 8.0,
     'L1_ffn_router_w': 3.129,
     'L1_ffn_expert_w': 3.531}
    for name, (base, spread) in spreads.items():
        noise = np.random.default_rng([zlib.crc32(name.encode()), seed]).standard_normal(out[name].shape)
        drawn = base * np.exp(spread * noise) if base else spread * noise
        out[name] = jnp.asarray(drawn.astype(out[name].dtype))
    for name, factor in factors.items():
        out[name] = (out[name] * factor).astype(out[name].dtype)
    return out
```

```python
import numpy as np
import concourse.bass as bass
from concourse import mybir
from contextlib import ExitStack

fp32 = mybir.dt.float32
bf16 = mybir.dt.bfloat16
i32 = mybir.dt.int32
ALU = mybir.AluOpType
ACT = mybir.ActivationFunctionType
AX = mybir.AxisListType

B, T, C = 32, 165, 256
CT = C // 128
NIMG, NTXT = 36, 128
NTOK = B * T
TD = 168
NROW = B * TD
PAIRS = B // 2
NP = 2 * T
TP = T + 1
W4 = CT * 2 * TP
WC = CT * NP
VOCAB, NFREQ = 64, 4
PK = 6
F1 = 4 * C
FT = F1 // 128
E8 = 8
K_TOP = NTOK // E8
ROWT = 110
RT = NP // ROWT
EPS = 1e-5
NEG = -1e38


def one_act_table(nc):
    nc.scalar.add_instruction(mybir.InstLoadActFuncSet(
        name=nc.get_next_instruction_name(), act_func_set_id=6, engine=nc.scalar.engine))


class Chain:

    def __init__(self, eng, sem, per_turn=0, turn=None, base=0):
        self.eng, self.sem, self.n, self.per, self.turn, self.base = eng, sem, 0, per_turn, turn, base

    def mark(self, ins):
        self.n += 1
        ins.then_inc(self.sem, 1)
        return self.n

    def wait(self, n=None):
        n = self.base + (self.n if n is None else n)
        self.eng.wait_ge(self.sem, n if self.turn is None else self.turn * self.per + n)

    def then(self, ins):
        self.mark(ins)
        self.wait()


def phase_tokens(nc, A, z_rows, acc_rows, score_rows):
    ctx = ExitStack()
    with ctx:
        def sb(name, shape, dt=fp32):
            return ctx.enter_context(nc.sbuf_tensor(name, shape, dt))

        def sem(name):
            return ctx.enter_context(nc.semaphore(name))

        wtok = sb("wtok", [128, PK, C])
        wtk, wtv, wtr, wcr = (sb(n, [128, CT, C]) for n in ("wtk", "wtv", "wtr", "wcr"))
        wck = sb("wck", [128, CT, F1])
        wcv = sb("wcv", [128, FT, C])
        wgate = sb("wgate", [128, CT, E8])
        table = sb("table", [VOCAB + 1, C])
        pos = sb("pos", [128, CT, T])
        ident = sb("ident", [128, 128])
        mean_w = sb("mean_w", [128, 128])
        rowid = sb("rowid", [VOCAB, 1])
        epsc = sb("epsc", [128, 3])
        prm = sb("prm", [128, 13, CT])
        (TOKB, TXTB, DECAY, FIRST, G1, B1, G2, B2, MK, MV, MR, CK, CR) = range(13)
        wdec = sb("wdec", [128, W4])
        emb = sb("emb", [128, NFREQ, VOCAB])
        wtxt = sb("wtxt", [128, NFREQ, C])

        names = ["h0", "xc", "sq", "xa", "hh", "dd", "m0", "m1", "m2", "kk", "vv", "mm", "al", "be",
                 "pp", "ca", "cv", "aa"]
        tl = [{n: sb(f"{n}{s}", [128, W4]) for n in names} for s in range(2)]
        tmp = [sb(f"tmp{s}", [128, 4 * W4]) for s in range(2)]
        half = [sb(f"half{s}", [128, 2, NP]) for s in range(2)]
        patch = [sb(f"patch{s}", [128, PK, 2 * NIMG]) for s in range(2)]
        ids = [sb(f"ids{s}", [VOCAB, 2, NTXT], i32) for s in range(2)]
        hot = [sb(f"hot{s}", [VOCAB + 1, 2, T]) for s in range(2)]
        rows = [sb(f"rows{s}", [ROWT, RT, 2, C]) for s in range(2)]
        scs = [sb(f"scs{s}", [E8, NP]) for s in range(2)]
        ps = [ctx.enter_context(nc.psum_tensor(f"ps{s}", [128, 4, 512], fp32)) for s in range(2)]

        zero = sb("zero", [B * (TD - T), C])

        s_ld, s_ld2, s_fill = sem("loads"), sem("table_loads"), sem("filled")
        s_in = [sem(f"pair_in{s}") for s in range(2)]
        s_out = [sem(f"rows_out{s}") for s in range(2)]
        s_const, s_v, s_a, s_p = sem("consts"), sem("dve_chain"), sem("act_chain"), sem("pool_chain")
        s_tabp, s_tab, s_hot = sem("table_psum"), sem("table_ready"), sem("onehot_ready")
        s_emb, s_h0, s_mean, s_xc, s_sq, s_var = (sem(n) for n in (
            "embedded", "h0_ready", "mean_done", "centred", "squared", "var_done"))
        s_rs, s_hc, s_h = sem("rstd_ready"), sem("normed"), sem("h_ready")
        s_dd, s_mixk, s_mixv, s_mixr = sem("diff_ready"), sem("mixk"), sem("mixv"), sem("mixr")
        s_km, s_vm, s_rm = sem("k_done"), sem("v_done"), sem("r_done")
        s_ke, s_ve, s_re = sem("k_evac"), sem("v_evac"), sem("r_evac")
        s_t1, s_ab, s_pp, s_lp, s_s, s_cc, s_e12, s_den, s_lden, s_sg, s_gate = (sem(n) for n in (
            "t1", "alpha_beta", "p_scan", "log_p", "s_ready", "ca_cb", "e1_e2", "den", "log_den",
            "gate_log", "gate_exp"))
        s_x1, s_mixc, s_mixcr = sem("x1_ready"), sem("mix_ck"), sem("mix_cr")
        s_crm, s_cre = sem("cr_done"), sem("cr_evac")
        s_ck, s_relu, s_kk2, s_cv = sem("ck_done"), sem("relu_done"), sem("squares"), sem("cv_done")
        s_cg, s_cge, s_crm2 = sem("cgate_softplus"), sem("cgate_log"), sem("cgate_exp")
        s_h1, s_xf, s_zz, s_hx = sem("h1_ready"), sem("xf_ready"), sem("z_ready"), sem("hx_ready")
        s_scm, s_sce, s_tr, s_tre = sem("score_done"), sem("score_evac"), sem("rows_done"), sem("rows_evac")

        def grid(x):
            return x[:, 0:W4].rearrange("p (c s t) -> p c s t", c=CT, s=2)

        def real(x):
            return grid(x)[:, :, :, 1:TP]

        def prev(x):
            return grid(x)[:, :, :, 0:T]

        def real4(x):
            return x[:, 0:W4].rearrange("p (r t) -> p r t", t=TP)[:, :, 1:TP]

        def prev4(x):
            return x[:, 0:W4].rearrange("p (r t) -> p r t", t=TP)[:, :, 0:T]

        def pads(x):
            return x[:, 0:W4].rearrange("p (r t) -> p r t", t=TP)[:, :, 0:1]

        def realc(x, c):
            return grid(x)[:, c, :, 1:TP]

        def prevc(x, c):
            return grid(x)[:, c, :, 0:T]

        def comp(x):
            return x[:, 0:WC].rearrange("p (c s t) -> p c s t", c=CT, s=2)

        def comp4(x):
            return x[:, 0:WC].rearrange("p (r t) -> p r t", t=T)

        def compc(x, c):
            return comp(x)[:, c, :, :]

        def both(x):
            return x.rearrange("p (s t) -> p s t", s=2).unsqueeze(1).broadcast_to([128, CT, 2, T])

        def bank2(s, b0):
            return ps[s][:, b0:b0 + 2, 0:NP].rearrange("p c (s t) -> p c s t", s=2)

        def scratch(s, n):
            return tmp[s][:, n * W4:(n + 1) * W4]

        def hidden(s, f):
            return tmp[s][:, f * NP:(f + 1) * NP]

        def vec(i, c):
            return prm[:, i, c:c + 1]

        OUTS = 16 * 9
        block = ctx.enter_context(nc.Block())

        @block.sync
        def _(sp):
            sp.dma_start(emb[:], A["emb_t"]).then_inc(s_ld2, 16)
            sp.dma_start(wtxt[:], A["L0_txt_W"].rearrange("(f p) e -> p f e", p=128)).then_inc(s_ld2, 16)
            sp.dma_start(table[VOCAB:VOCAB + 1, :], A["L0_tok_cls_token"].rearrange("(a n) -> a n", a=1)).then_inc(s_ld2, 16)
            sp.dma_start(prm[:], A["prm"]).then_inc(s_ld, 16)
            sp.dma_start(pos[:], A["pos_t"]).then_inc(s_ld, 16)
            sp.dma_start(ident[:], A["ident"]).then_inc(s_ld, 16)
            sp.dma_start(rowid[:], A["rowid"]).then_inc(s_ld, 16)
            sp.dma_start(wtok[:], A["wtok_t"]).then_inc(s_ld, 16)

            def load_pair(i, s):
                sp.dma_start(patch[s][:], A["patches"][bass.ds(i, 1)].rearrange("a p k n -> (a p) k n")).then_inc(s_in[s], 16)
                src = A["x_txt"][bass.ds(2 * i, 2), :].unsqueeze(0).broadcast_to([VOCAB, 2, NTXT])
                sp.dma_start(ids[s][:], src).then_inc(s_in[s], 16)

            for s in range(2):
                load_pair(s, s)
            for w, n in ((wtk, "w_tk"), (wtv, "w_tv"), (wtr, "w_tr"), (wcr, "w_cr"), (wck, "w_ck")):
                sp.dma_start(w[:], A["L0_attn_" + n].rearrange("(a p) n -> p a n", p=128)).then_inc(s_ld, 16)
            sp.dma_start(wcv[:], A["L0_attn_w_cv"].rearrange("(a p) n -> p a n", p=128)).then_inc(s_ld, 16)
            sp.dma_start(wgate[:], A["gate_t"]).then_inc(s_ld, 16)

            sp.wait_ge(s_const, 5)
            for dst in (z_rows, acc_rows):
                sp.dma_start(dst.rearrange("(b t) c -> b t c", t=TD)[:, T:TD, :], zero[:]).then_inc(s_fill, 16)
            sp.dma_start(score_rows.rearrange("e (b t) -> e b t", t=TD)[:, :, T:TD],
                         zero[0:E8, 0:B * (TD - T)].rearrange("e (b t) -> e b t", b=B)).then_inc(s_fill, 16)

            def store_rows(it):
                for s in range(2):
                    first = (it * 2 + s) * (2 * TD)
                    seam = T - ROWT
                    sp.wait_ge(s_sce, it * 2 + (s + 3))
                    sp.dma_start(score_rows[:, bass.ds(first, 2 * TD)].rearrange("e (s t) -> e s t", s=2)[:, :, 0:T],
                                 scs[s][:].rearrange("e (s t) -> e s t", s=2)).then_inc(s_out[s], 16)
                    sp.wait_ge(s_tre, it * 6 + (3 * s + 9))
                    for m, dst in enumerate((z_rows, acc_rows)):
                        for j, p0, n, row in ((0, 0, ROWT, 0), (1, 0, seam, ROWT), (1, seam, ROWT - seam, TD), (2, 0, ROWT, TD + ROWT - seam)):
                            sp.dma_start(dst[bass.ds(first + row, n), :], rows[s][p0:p0 + n, j, m, :]).then_inc(s_out[s], 16)

            with sp.Fori(0, PAIRS // 2 - 1) as it:
                for s in range(2):
                    sp.wait_ge(s_hot, it * 2 + (s + 1))
                    sp.wait_ge(s_emb, it * 2 + (s + 1))
                    load_pair(it * 2 + (2 + s), s)
                store_rows(it)
            store_rows(PAIRS // 2 - 1)
            sp.wait_ge(s_fill, 48)
            for s in range(2):
                sp.wait_ge(s_out[s], 1 + OUTS * (PAIRS // 2))
                sp.wait_ge(s_in[s], 32 * (PAIRS // 2))

        @block.gpsimd
        def _(pool):
            V = nc.gpsimd
            V.memset(mean_w[:], 1.0 / C).then_inc(s_const, 1)
            for n, v in enumerate((EPS, EPS * EPS, 1.0)):
                V.memset(epsc[:, n:n + 1], v).then_inc(s_const, 1)
            V.memset(zero[:], 0.0).then_inc(s_const, 1)
            for s in range(2):
                pool.sem_inc(s_out[s], 1)
            with pool.Fori(0, PAIRS // 2) as it:
                for s in range(2):
                    for f in range(FT):
                        pool.wait_ge(s_relu, it * (2 * FT) + FT * s + f + 1)
                        V.tensor_tensor(hidden(s, f), hidden(s, f), hidden(s, f), ALU.mult).then_inc(s_kk2, 1)

        @block.tensor
        def _(pe):
            V = nc.tensor
            pe.wait_ge(s_ld2, 48)
            for f in range(NFREQ):
                last = V.matmul(ps[0][0:VOCAB, 0, 0:C], emb[:, f, :], wtxt[:, f, :], start=f == 0, stop=f == NFREQ - 1)
            last.then_inc(s_tabp, 1)
            pe.wait_ge(s_ld, 16 * 12)
            pe.wait_ge(s_tab, 1)
            pe.wait_ge(s_const, 4)

            def sums(s, b, x, done, compact):
                for c in range(CT):
                    last = V.matmul(ps[s][:, b, 0:NP], mean_w[:], (compc if compact else realc)(x, c),
                                    start=c == 0, stop=c == CT - 1)
                last.then_inc(done, 1)

            def project(s, b, w, x, done):
                for m in range(CT):
                    for c in range(CT):
                        last = V.matmul(ps[s][:, b + m, 0:NP], w[:, c, m * 128:(m + 1) * 128], compc(x, c),
                                        start=c == 0, stop=c == CT - 1)
                last.then_inc(done, 1)

            with pe.Fori(0, PAIRS // 2) as it:
                def turn(s, k=1):
                    return it * 2 + (s + k)

                for s in range(2):
                    pe.wait_ge(s_hot, turn(s))
                    pe.wait_ge(s_in[s], it * 32 + 32)
                    pe.wait_ge(s_tre, it * 6 + (3 * s + 1))
                    pe.wait_ge(s_sce, turn(s))
                    for m in range(CT):
                        V.matmul(ps[s][:, m, 0:NP], table[:, m * 128:(m + 1) * 128], hot[s][:].rearrange("p s t -> p (s t)"),
                                 start=True, stop=False)
                        out = ps[s][:, m, 0:NP].rearrange("p (s t) -> p s t", s=2)[:, :, 1:1 + NIMG]
                        for k in range(PK):
                            last = V.matmul(out, wtok[:, k, m * 128:(m + 1) * 128],
                                            patch[s][:, k, :].rearrange("p (s t) -> p s t", s=2),
                                            start=False, stop=k == PK - 1)
                    last.then_inc(s_emb, 1)
                for s in range(2):
                    pe.wait_ge(s_h0, turn(s))
                    pe.wait_ge(s_tre, it * 6 + (3 * s + 2))
                    sums(s, 2, tl[s]["h0"], s_mean, False)
                for s in range(2):
                    pe.wait_ge(s_sq, it * 6 + (s + 1))
                    pe.wait_ge(s_tre, it * 6 + (3 * s + 3))
                    sums(s, 3, tl[s]["sq"], s_var, True)
                for s in range(2):
                    pe.wait_ge(s_mixk, turn(s))
                    project(s, 0, wtk, tl[s]["m0"], s_km)
                for s in range(2):
                    pe.wait_ge(s_mixv, turn(s))
                    project(s, 2, wtv, tl[s]["m1"], s_vm)
                for s in range(2):
                    pe.wait_ge(s_mixr, turn(s))
                    pe.wait_ge(s_ke, turn(s))
                    project(s, 0, wtr, tl[s]["m2"], s_rm)
                for s in range(2):
                    pe.wait_ge(s_x1, turn(s))
                    sums(s, 2, tl[s]["xa"], s_mean, True)
                for s in range(2):
                    pe.wait_ge(s_sq, it * 6 + (s + 3))
                    sums(s, 3, tl[s]["sq"], s_var, True)
                for s in range(2):
                    pe.wait_ge(s_mixcr, turn(s))
                    project(s, 0, wcr, tl[s]["m1"], s_crm)
                for s in range(2):
                    pe.wait_ge(s_mixc, turn(s))
                    base = it * (2 * FT) + FT * s

                    def up(f):
                        if f >= 2:
                            pe.wait_ge(s_relu, base + (f - 1))
                        for c in range(CT):
                            last = V.matmul(ps[s][:, 2 + f % 2, 0:NP], wck[:, c, f * 128:(f + 1) * 128],
                                            compc(tl[s]["m0"], c), start=c == 0, stop=c == CT - 1)
                        last.then_inc(s_ck, 1)

                    def down(f):
                        if f == 0:
                            pe.wait_ge(s_cre, turn(s))
                        pe.wait_ge(s_kk2, base + (f + 1))
                        for m in range(CT):
                            last = V.matmul(ps[s][:, m, 0:NP], wcv[:, f, m * 128:(m + 1) * 128], hidden(s, f),
                                            start=f == 0, stop=f == FT - 1)
                        if f == FT - 1:
                            last.then_inc(s_cv, 1)

                    for f in range(FT + 3):
                        if f < FT:
                            up(f)
                        if f >= 3:
                            down(f - 3)
                for s in range(2):
                    pe.wait_ge(s_h1, turn(s))
                    sums(s, 2, tl[s]["xa"], s_mean, True)
                for s in range(2):
                    pe.wait_ge(s_sq, it * 6 + (s + 5))
                    sums(s, 3, tl[s]["sq"], s_var, True)
                for s in range(2):
                    pe.wait_ge(s_xf, turn(s))
                    for c in range(CT):
                        last = V.matmul(ps[s][0:E8, 0, 0:NP], wgate[:, c, :], compc(tl[s]["m0"], c), start=c == 0, stop=c == CT - 1)
                    last.then_inc(s_scm, 1)
                for s in range(2):
                    pe.wait_ge(s_hx, turn(s))
                    for j in range(RT):
                        for m, x in enumerate((tl[s]["m1"], tl[s]["m2"])):
                            for c in range(CT):
                                src = comp(x)[:, c, :, :].rearrange("p s t -> p (s t)")[:, j * ROWT:(j + 1) * ROWT]
                                last = V.transpose(ps[s][0:ROWT, 1 + j, m * C + c * 128:m * C + (c + 1) * 128], src, ident[:])
                        last.then_inc(s_tr, 1)

        @block.scalar
        def _(act):
            V = nc.scalar
            one_act_table(nc)
            act.wait_ge(s_tabp, 1)
            V.activation(table[0:VOCAB, :], ps[0][0:VOCAB, 0, 0:C], ACT.Copy).then_inc(s_tab, 1)
            act.wait_ge(s_const, 4)
            act.wait_ge(s_ld, 16 * 12)
            act.sem_inc(s_sce, 2)
            act.sem_inc(s_tre, 6)
            CHAIN = 2 * 9
            with act.Fori(0, PAIRS // 2) as it:
                ch = Chain(act, s_a, CHAIN, it)

                def turn(s, k=1):
                    return it * 2 + (s + k)

                def sqr(s, k):
                    act.wait_ge(s_xc, it * 6 + (k * 2 + s + 1))
                    V.activation(tl[s]["sq"][:, 0:WC], tl[s]["xc"][:, 0:WC], ACT.Square).then_inc(s_sq, 1)

                def rstd(s, k):
                    act.wait_ge(s_var, it * 6 + (k * 2 + s + 1))
                    ch.mark(V.activation(half[s][:, 0, :], ps[s][:, 3, 0:NP], ACT.Ln, bias=epsc[:, 0:1]))
                    n1 = ch.n
                    if k != 1:
                        ch.mark(V.activation(half[s][:, 1, :], ps[s][:, 3, 0:NP], ACT.Ln, bias=epsc[:, 1:2], scale=1.0 + EPS))
                        n1 = ch.n
                    ch.wait(n1)
                    m = 1 if k == 1 else 2
                    V.activation(half[s][:, 0:m, :], half[s][:, 0:m, :], ACT.Exp, scale=-0.5).then_inc(s_rs, 1)

                def affine(s, src, g, b, k):
                    act.wait_ge(s_hc, it * 4 + (k * 2 + s + 1))
                    for c in range(CT):
                        last = V.activation(realc(tl[s]["hh"], c), compc(src, c), ACT.Identity, bias=vec(b, c), scale=vec(g, c))
                    last.then_inc(s_h, 1)

                for s in range(2):
                    sqr(s, 0)
                for s in range(2):
                    rstd(s, 0)
                for s in range(2):
                    affine(s, tl[s]["m0"], G1, B1, 0)
                for s in range(2):
                    act.wait_ge(s_km, turn(s))
                    V.activation(real(tl[s]["kk"]), bank2(s, 0), ACT.Copy).then_inc(s_ke, 1)
                for s in range(2):
                    act.wait_ge(s_t1, turn(s))
                    V.activation(real(tl[s]["al"]), comp(scratch(s, 0)), ACT.Exp)
                    V.activation(real(tl[s]["be"]), comp(scratch(s, 1)), ACT.Exp, scale=-1.0).then_inc(s_ab, 1)
                for s in range(2):
                    act.wait_ge(s_vm, turn(s))
                    V.activation(comp(tl[s]["vv"]), bank2(s, 2), ACT.Copy).then_inc(s_ve, 1)
                for s in range(2):
                    act.wait_ge(s_pp, turn(s))
                    V.activation(comp(scratch(s, 0)), prev(tl[s]["pp"]), ACT.Ln).then_inc(s_lp, 1)
                for s in range(2):
                    act.wait_ge(s_rm, turn(s))
                    V.activation(comp(tl[s]["m2"]), bank2(s, 0), ACT.Copy).then_inc(s_re, 1)
                    act.wait_ge(s_re, turn(s))
                    ch.then(V.activation(tl[s]["m0"][:, 0:WC], tl[s]["m2"][:, 0:WC], ACT.Abs))
                    ch.mark(V.activation(tl[s]["m0"][:, 0:WC], tl[s]["m0"][:, 0:WC], ACT.Exp, scale=-1.0))
                    ch.wait()
                    V.activation(tl[s]["m0"][:, 0:WC], tl[s]["m0"][:, 0:WC], ACT.Ln, bias=epsc[:, 2:3]).then_inc(s_sg, 1)
                for s in range(2):
                    act.wait_ge(s_s, turn(s))
                    V.activation(real(tl[s]["ca"]), comp(scratch(s, 0)), ACT.Exp)
                    V.activation(comp(scratch(s, 1)), comp(scratch(s, 1)), ACT.Exp, scale=-1.0)
                    V.activation(scratch(s, 2)[:, 0:WC], scratch(s, 2)[:, 0:WC], ACT.Exp)
                    V.activation(scratch(s, 3)[:, 0:WC], scratch(s, 3)[:, 0:WC], ACT.Exp, scale=-1.0).then_inc(s_cc, 1)
                for s in range(2):
                    act.wait_ge(s_den, turn(s))
                    V.activation(scratch(s, 0)[:, 0:WC], scratch(s, 0)[:, 0:WC], ACT.Ln).then_inc(s_lden, 1)
                for s in range(2):
                    act.wait_ge(s_gate, turn(s))
                    V.activation(tl[s]["m0"][:, 0:WC], tl[s]["m0"][:, 0:WC], ACT.Exp).then_inc(s_e12, 1)
                for s in range(2):
                    sqr(s, 1)
                for s in range(2):
                    rstd(s, 1)
                for s in range(2):
                    affine(s, tl[s]["m2"], G2, B2, 1)
                for s in range(2):
                    act.wait_ge(s_crm, turn(s))
                    V.activation(comp(tl[s]["m2"]), bank2(s, 0), ACT.Copy).then_inc(s_cre, 1)
                    act.wait_ge(s_cre, turn(s))
                    ch.then(V.activation(tl[s]["aa"][:, 0:WC], tl[s]["m2"][:, 0:WC], ACT.Abs))
                    ch.mark(V.activation(tl[s]["aa"][:, 0:WC], tl[s]["aa"][:, 0:WC], ACT.Exp, scale=-1.0))
                    ch.wait()
                    V.activation(tl[s]["aa"][:, 0:WC], tl[s]["aa"][:, 0:WC], ACT.Ln, bias=epsc[:, 2:3]).then_inc(s_cg, 1)
                for s in range(2):
                    for f in range(FT):
                        act.wait_ge(s_ck, it * (2 * FT) + (FT * s + f + 1))
                        V.activation(hidden(s, f), ps[s][:, 2 + f % 2, 0:NP], ACT.Relu).then_inc(s_relu, 1)
                    if s == 0:
                        for q in range(2):
                            act.wait_ge(s_cge, turn(q))
                            V.activation(tl[q]["aa"][:, 0:WC], tl[q]["aa"][:, 0:WC], ACT.Exp).then_inc(s_crm2, 1)
                for s in range(2):
                    sqr(s, 2)
                for s in range(2):
                    rstd(s, 2)
                for s in range(2):
                    act.wait_ge(s_scm, turn(s))
                    act.wait_ge(s_out[s], it * OUTS + 1)
                    V.activation(scs[s][:], ps[s][0:E8, 0, 0:NP], ACT.Copy).then_inc(s_sce, 1)
                for s in range(2):
                    for j in range(RT):
                        act.wait_ge(s_tr, it * 6 + (3 * s + j + 1))
                        V.activation(rows[s][:, j, :, :].rearrange("p m c -> p (m c)"), ps[s][0:ROWT, 1 + j, :], ACT.Copy).then_inc(s_tre, 1)
                assert ch.n == CHAIN

        @block.vector
        def _(dve):
            V = nc.vector
            dve.wait_ge(s_ld, 16 * 12)
            for c in range(CT):
                V.tensor_scalar(pos[:, c, 1:1 + NIMG], pos[:, c, 1:1 + NIMG], vec(TOKB, c), None, ALU.add)
                V.tensor_scalar(pos[:, c, 1 + NIMG:T], pos[:, c, 1 + NIMG:T], vec(TXTB, c), None, ALU.add)
            pre = Chain(dve, s_v)
            pre.then(V.memset(wdec[:], 0.0))
            for c in range(CT):
                pre.then(V.tensor_scalar(wdec[:, c * 2 * TP:(c + 1) * 2 * TP], wdec[:, c * 2 * TP:(c + 1) * 2 * TP],
                                         vec(DECAY, c), None, ALU.add))
            pre.then(V.memset(pads(wdec), NEG))
            for s in range(2):
                V.memset(pads(tl[s]["hh"]), 0.0)
                V.memset(pads(tl[s]["kk"]), NEG)
                V.memset(pads(tl[s]["al"]), 0.0)
                V.memset(pads(tl[s]["be"]), 1.0)
                V.memset(pads(tl[s]["ca"]), 0.0)
                V.memset(pads(tl[s]["cv"]), 0.0)
                pre.then(V.memset(hot[s][:], 0.0))
                pre.then(V.memset(hot[s][VOCAB:VOCAB + 1, :, 0:1], 1.0))
            CHAIN = 2 * 14
            with dve.Fori(0, PAIRS // 2) as it:
                ch = Chain(dve, s_v, CHAIN, it, base=pre.n)

                def turn(s, k=1):
                    return it * 2 + (s + k)

                def centre(s, x, k, compact=True):
                    dve.wait_ge(s_mean, it * 6 + (k * 2 + s + 1))
                    V.tensor_tensor(comp(tl[s]["xc"]), (comp if compact else real)(x), both(ps[s][:, 2, 0:NP]), ALU.subtract).then_inc(s_xc, 1)
                    dve.wait_ge(s_xc, it * 6 + (k * 2 + s + 1))

                def mix(s, out, i, done):
                    for c in range(CT):
                        last = V.scalar_tensor_tensor(compc(out, c), compc(tl[s]["dd"], c), vec(i, c), prevc(tl[s]["hh"], c), ALU.mult, ALU.add)
                    last.then_inc(done, 1)

                for s in range(2):
                    dve.wait_ge(s_in[s], it * 32 + 32)
                    V.tensor_scalar(hot[s][0:VOCAB, :, 1 + NIMG:T], ids[s][:], rowid[:, 0:1], None, ALU.is_equal).then_inc(s_hot, 1)
                for s in range(2):
                    dve.wait_ge(s_emb, turn(s))
                    V.tensor_tensor(real(tl[s]["h0"]), bank2(s, 0), pos[:].unsqueeze(2).broadcast_to([128, CT, 2, T]), ALU.add).then_inc(s_h0, 1)
                    dve.wait_ge(s_h0, turn(s))
                for s in range(2):
                    centre(s, tl[s]["h0"], 0, False)
                for s in range(2):
                    dve.wait_ge(s_rs, it * 6 + (s + 1))
                    V.tensor_tensor(comp(tl[s]["m0"]), comp(tl[s]["xc"]), both(half[s][:, 1, :]), ALU.mult).then_inc(s_hc, 1)
                    V.tensor_tensor(comp(tl[s]["xa"]), comp(tl[s]["xc"]), both(half[s][:, 0, :]), ALU.mult)
                for s in range(2):
                    dve.wait_ge(s_h, it * 4 + (s + 1))
                    ch.then(V.tensor_tensor(comp(tl[s]["dd"]), real(tl[s]["hh"]), prev(tl[s]["hh"]), ALU.subtract))
                    mix(s, tl[s]["m0"], MK, s_mixk)
                    mix(s, tl[s]["m1"], MV, s_mixv)
                    mix(s, tl[s]["m2"], MR, s_mixr)
                for s in range(2):
                    dve.wait_ge(s_ke, turn(s))
                    ch.then(V.tensor_tensor_scan(tl[s]["mm"][:], tl[s]["kk"][:], wdec[:], NEG, ALU.max, ALU.add))
                    ch.then(V.tensor_tensor(comp(tl[s]["dd"]), prev(tl[s]["mm"]), real(tl[s]["kk"]), ALU.subtract))
                    V.tensor_scalar(scratch(s, 0)[:, 0:WC], tl[s]["dd"][:, 0:WC], 0.0, None, ALU.min)
                    V.tensor_scalar(scratch(s, 1)[:, 0:WC], tl[s]["dd"][:, 0:WC], 0.0, None, ALU.max).then_inc(s_t1, 1)
                for s in range(2):
                    dve.wait_ge(s_ab, turn(s))
                    V.tensor_tensor_scan(tl[s]["pp"][:], tl[s]["al"][:], tl[s]["be"][:], 1.0, ALU.mult, ALU.add).then_inc(s_pp, 1)
                for s in range(2):
                    dve.wait_ge(s_lp, turn(s))
                    ch.then(V.tensor_tensor(tl[s]["dd"][:, 0:WC], tl[s]["dd"][:, 0:WC], scratch(s, 0)[:, 0:WC], ALU.add))
                    V.tensor_scalar(scratch(s, 0)[:, 0:WC], tl[s]["dd"][:, 0:WC], 0.0, None, ALU.min)
                    V.tensor_scalar(scratch(s, 1)[:, 0:WC], tl[s]["dd"][:, 0:WC], 0.0, None, ALU.max)
                    for c in range(CT):
                        V.tensor_scalar(compc(scratch(s, 2), c), compc(tl[s]["dd"], c), vec(FIRST, c), 0.0, ALU.subtract, ALU.min)
                        last = V.tensor_scalar(compc(scratch(s, 3), c), compc(tl[s]["dd"], c), vec(FIRST, c), 0.0, ALU.subtract, ALU.max)
                    last.then_inc(s_s, 1)
                for s in range(2):
                    dve.wait_ge(s_cc, turn(s))
                    dve.wait_ge(s_ve, turn(s))
                    ch.then(V.tensor_tensor(real(tl[s]["cv"]), comp(scratch(s, 1)), comp(tl[s]["vv"]), ALU.mult))
                    V.tensor_tensor_scan(tl[s]["aa"][:], tl[s]["ca"][:], tl[s]["cv"][:], 0.0, ALU.mult, ALU.add)
                    ch.then(V.tensor_tensor(scratch(s, 0)[:, 0:WC], scratch(s, 2)[:, 0:WC], scratch(s, 3)[:, 0:WC], ALU.add))
                    dve.sem_inc(s_den, 1)
                    ch.then(V.tensor_tensor(comp(tl[s]["m1"]), comp(scratch(s, 3)), comp(tl[s]["vv"]), ALU.mult))
                    ch.then(V.tensor_tensor(comp(tl[s]["dd"]), comp(scratch(s, 2)), prev(tl[s]["aa"]), ALU.mult))
                    ch.mark(V.tensor_tensor(tl[s]["m1"][:, 0:WC], tl[s]["m1"][:, 0:WC], tl[s]["dd"][:, 0:WC], ALU.add))
                for s in range(2):
                    dve.wait_ge(s_sg, turn(s))
                    ch.then(V.scalar_tensor_tensor(tl[s]["m2"][:, 0:WC], tl[s]["m2"][:, 0:WC], 0.0, tl[s]["m0"][:, 0:WC], ALU.min, ALU.subtract))
                    dve.wait_ge(s_lden, turn(s))
                    V.tensor_tensor(tl[s]["m0"][:, 0:WC], tl[s]["m2"][:, 0:WC], scratch(s, 0)[:, 0:WC], ALU.subtract).then_inc(s_gate, 1)
                for s in range(2):
                    dve.wait_ge(s_e12, turn(s))
                    ch.then(V.tensor_tensor(tl[s]["m1"][:, 0:WC], tl[s]["m1"][:, 0:WC], tl[s]["m0"][:, 0:WC], ALU.mult))
                    V.tensor_tensor(tl[s]["xa"][:, 0:WC], tl[s]["xa"][:, 0:WC], tl[s]["m1"][:, 0:WC], ALU.add).then_inc(s_x1, 1)
                    dve.wait_ge(s_x1, turn(s))
                for s in range(2):
                    centre(s, tl[s]["xa"], 1)
                for s in range(2):
                    dve.wait_ge(s_rs, it * 6 + (s + 3))
                    V.tensor_tensor(comp(tl[s]["m2"]), comp(tl[s]["xc"]), both(half[s][:, 0, :]), ALU.mult).then_inc(s_hc, 1)
                for s in range(2):
                    dve.wait_ge(s_h, it * 4 + (s + 3))
                    ch.then(V.tensor_tensor(comp(tl[s]["dd"]), real(tl[s]["hh"]), prev(tl[s]["hh"]), ALU.subtract))
                    mix(s, tl[s]["m1"], CR, s_mixcr)
                    mix(s, tl[s]["m0"], CK, s_mixc)
                for s in range(2):
                    dve.wait_ge(s_cg, turn(s))
                    V.scalar_tensor_tensor(tl[s]["aa"][:, 0:WC], tl[s]["m2"][:, 0:WC], 0.0, tl[s]["aa"][:, 0:WC], ALU.min, ALU.subtract).then_inc(s_cge, 1)
                for s in range(2):
                    dve.wait_ge(s_cv, turn(s))
                    dve.wait_ge(s_crm2, turn(s))
                    ch.then(V.tensor_tensor(comp(tl[s]["m2"]), bank2(s, 0), comp(tl[s]["aa"]), ALU.mult))
                    ch.then(V.tensor_tensor(tl[s]["m2"][:, 0:WC], tl[s]["m2"][:, 0:WC], tl[s]["xa"][:, 0:WC], ALU.add))
                    V.tensor_tensor(comp(tl[s]["xa"]), comp(tl[s]["m2"]), real(tl[s]["h0"]), ALU.add).then_inc(s_h1, 1)
                    dve.wait_ge(s_h1, turn(s))
                for s in range(2):
                    centre(s, tl[s]["xa"], 2)
                for s in range(2):
                    dve.wait_ge(s_rs, it * 6 + (s + 5))
                    V.tensor_tensor(comp(tl[s]["m0"]), comp(tl[s]["xc"]), both(half[s][:, 0, :]), ALU.mult).then_inc(s_xf, 1)
                    V.tensor_tensor(comp(tl[s]["m1"]), comp(tl[s]["xc"]), both(half[s][:, 1, :]), ALU.mult)
                    dve.wait_ge(s_xf, turn(s))
                    V.tensor_tensor(comp(tl[s]["m2"]), comp(tl[s]["xa"]), comp(tl[s]["m0"]), ALU.add).then_inc(s_hx, 1)
                    dve.wait_ge(s_hx, turn(s))
                assert ch.n == CHAIN

u32 = mybir.dt.uint32
SP_P, SP_C = 128, NROW // 128
JT = K_TOP // ROWT
GT = JT // RT
SCORE_BITS = 26


def phase_experts(nc, A, z_rows, acc_rows, score_rows):
    ctx = ExitStack()
    with ctx:
        def sb(name, shape, dt=fp32):
            return ctx.enter_context(nc.sbuf_tensor("e_" + name, shape, dt))

        def sem(name):
            return ctx.enter_context(nc.semaphore("e_" + name))

        score = sb("score", [SP_P, E8, SP_C])
        thr, step, cand = sb("thr", [SP_P, E8]), sb("step", [SP_P, E8]), sb("cand", [SP_P, E8])
        flag = sb("flag", [SP_P, E8, SP_C])
        eq = sb("eq", [SP_P, E8, SP_C])
        rank = sb("rank", [SP_P, E8, SP_C])
        cnt, upd, need = sb("cnt", [SP_P, E8]), sb("upd", [SP_P, E8]), sb("need", [SP_P, E8])
        carry = sb("carry", [SP_P, E8, SP_C])
        ones, tri = sb("ones", [SP_P, SP_P]), sb("tri", [SP_P, SP_P])
        ge = sb("ge", [SP_P, E8 * SP_C, JT + 1])
        tile1 = sb("tile1", [SP_P, E8 * SP_C, JT])
        parts = sb("parts", [SP_P, E8 * SP_C, 5, JT], bf16)
        sp3 = sb("sp3", [SP_P, 3, E8, SP_C], bf16)
        rest = sb("rest", [SP_P, 2, E8, SP_C])
        limit = sb("limit", [SP_P, SP_C])
        tokp, tokc = sb("tokp", [SP_P, 1]), sb("tokc", [SP_P, SP_C])
        lo = sb("lo", [SP_P, E8, SP_C])
        lane = sb("lane", [SP_P, ROWT])
        hotlo = [sb(f"hotlo{s}", [SP_P, SP_C, ROWT], bf16) for s in range(2)]
        found = sb("found", [ROWT, E8, 5, JT])
        idxf = sb("idxf", [ROWT, E8, JT])
        idx = sb("idx", [ROWT, E8, JT], u32)
        kept = sb("kept", [ROWT, E8, JT])

        lnv = sb("lnv", [128, 2, CT])
        w1 = [sb(f"w1{s}", [128, CT * F1 + FT]) for s in range(2)]
        w2 = [sb(f"w2{s}", [128, FT, C]) for s in range(2)]
        b2 = [sb(f"b2{s}", [1, C]) for s in range(2)]
        one_row = sb("one_row", [1, ROWT])
        eye = sb("eye", [128, 128])
        cidx = [sb(f"cidx{s}", [ROWT, JT], u32) for s in range(2)]
        ckept = [sb(f"ckept{s}", [ROWT, JT]) for s in range(2)]
        gz = [sb(f"gz{s}", [ROWT, JT, C]) for s in range(2)]
        yt = [sb(f"yt{s}", [128, CT, K_TOP]) for s in range(2)]
        hid = [sb(f"hid{g}", [128, FT, NP]) for g in range(GT)]
        oo = [sb(f"oo{s}", [ROWT, JT, C]) for s in range(2)]
        pt = ctx.enter_context(nc.psum_tensor("e_pt", [128, 2, 512], fp32))
        pu = ctx.enter_context(nc.psum_tensor("e_pu", [128, 3, 512], fp32))
        pd = ctx.enter_context(nc.psum_tensor("e_pd", [128, 3, 512], fp32))

        s_ld, s_v, s_cnt, s_sum = sem("loads"), sem("dve_chain"), sem("counted"), sem("summed")
        s_tanh, s_hl, s_fd = sem("tanh"), sem("onehots"), sem("found")
        s_w = [sem(f"weights{s}") for s in range(2)]
        s_ci, s_g, s_tr, s_yt = sem("indices"), [sem(f"gathered{s}") for s in range(2)], sem("transposed"), sem("y_ready")
        s_up, s_hid, s_dn, s_oo, s_sc = sem("up_done"), sem("hidden_ready"), sem("down_done"), sem("out_ready"), sem("scattered")
        s_cst, s_turn = sem("consts"), sem("turn")
        block = ctx.enter_context(nc.Block())
        LOADS = 7

        @block.sync
        def _(sp):
            sp.dma_start(score[:], score_rows.rearrange("e (p c) -> p e c", c=SP_C)).then_inc(s_ld, 16)
            sp.dma_start(tri[:], A["tri"]).then_inc(s_ld, 16)
            sp.dma_start(limit[:], A["limit"]).then_inc(s_ld, 16)
            sp.dma_start(tokp[:], A["tokp"]).then_inc(s_ld, 16)
            sp.dma_start(tokc[:], A["iota"][0:1, 0:SP_C].broadcast_to([SP_P, SP_C])).then_inc(s_ld, 16)
            sp.dma_start(lane[:], A["iota"][0:1, 0:ROWT].broadcast_to([SP_P, ROWT])).then_inc(s_ld, 16)
            sp.dma_start(eye[:], A["ident"]).then_inc(s_ld, 16)
            sp.dma_start(lnv[:], A["ffn_ln"]).then_inc(s_cst, 16)

            def load_expert(e, s):
                sp.dma_start(w1[s][:], A["w1"][bass.ds(e, 1)].rearrange("a p n -> (a p) n")).then_inc(s_w[s], 16)
                sp.dma_start(w2[s][:], A["w2"][bass.ds(e, 1)].rearrange("a p f n -> (a p) f n")).then_inc(s_w[s], 16)
                sp.dma_start(b2[s][:], A["b2"][bass.ds(e, 1), :]).then_inc(s_w[s], 16)

            for s in range(2):
                load_expert(s, s)
            with sp.Fori(0, E8 // 2 - 1) as it:
                for s in range(2):
                    sp.wait_ge(s_dn, it * 12 + (6 * s + 6))
                    sp.sem_inc(s_turn, 1)
                    sp.wait_ge(s_hid, it * 32 + (16 * s + 16))
                    sp.sem_inc(s_turn, 1)
                    load_expert(it * 2 + (2 + s), s)

        @block.gpsimd
        def _(pool):

            def gather(s, n):
                pool.wait_ge(s_ci, n)
                pool.sem_inc(s_turn, 1)
                for j in range(JT):
                    pool.indirect_dma_start(gz[s][:, j, :], None, z_rows[:, :],
                                            bass.IndirectOffsetOnAxis(ap=cidx[s][:, j:j + 1], axis=0),
                                            bounds_check=NROW - 1).then_inc(s_g[s], 16)

            def scatter(s, n, before):
                pool.wait_ge(s_oo, n * JT)
                if before is not None:
                    pool.wait_ge(s_sc, before)
                pool.sem_inc(s_turn, 1)
                for j in range(JT):
                    pool.indirect_dma_start(acc_rows[:, :], bass.IndirectOffsetOnAxis(ap=cidx[s][:, j:j + 1], axis=0),
                                            oo[s][:, j, :], None, bounds_check=NROW - 1,
                                            compute_op=ALU.add).then_inc(s_sc, 16)

            def pair(it, before):
                gather(1, it * 2 + 2)
                scatter(0, it * 2 + 1, before)
                gather(0, it * 2 + 3)
                scatter(1, it * 2 + 2, it * (32 * JT) + 16 * JT)

            gather(0, 1)
            pair(0, None)
            with pool.Fori(1, E8 // 2 - 1) as it:
                pair(it, it * (32 * JT))
            last = E8 // 2 - 1
            gather(1, E8)
            scatter(0, E8 - 1, last * 32 * JT)
            scatter(1, E8, last * 32 * JT + 16 * JT)
            pool.wait_ge(s_sc, E8 * JT * 16)

        @block.scalar
        def _(act):
            V = nc.scalar
            act.wait_ge(s_ld, 16 * LOADS)
            V.activation(flag[:], score[:], ACT.Tanh).then_inc(s_tanh, 1)
            act.wait_ge(s_cst, 16)

            def norm_affine(s, n0):
                for g in range(GT):
                    act.wait_ge(s_tr, n0 + (g + 1))
                    for c in range(CT):
                        last = V.activation(yt[s][:, c, g * NP:(g + 1) * NP], pt[:, c, 0:NP], ACT.Identity,
                                            scale=lnv[:, 0, c:c + 1], bias=lnv[:, 1, c:c + 1])
                    last.then_inc(s_yt, 1)

            def hidden(s, g, n0):
                for f in range(FT):
                    k = g * FT + f
                    act.wait_ge(s_up, n0 + (k + 1))
                    V.activation(hid[g][:, f, :], pu[:, k % 3, 0:NP], ACT.Gelu_apprx_tanh,
                                 bias=w1[s][:, CT * F1 + f:CT * F1 + f + 1]).then_inc(s_hid, 1)

            def expert(s, it, more):
                for g in range(GT):
                    if g == 0:
                        act.wait_ge(s_w[s], it * 48 + 48)
                    hidden(s, g, it * (4 * FT) + s * 2 * FT)
                if more:
                    norm_affine(1 - s, it * 4 + (2 * s + 2))

            norm_affine(0, 0)
            with act.Fori(0, E8 // 2 - 1) as it:
                for s in range(2):
                    expert(s, it, True)
            for s in range(2):
                expert(s, E8 // 2 - 1, s == 0)

        @block.tensor
        def _(pe):
            V = nc.tensor
            pe.wait_ge(s_ld, 16 * LOADS)
            with pe.Fori(0, SCORE_BITS + 1) as it:
                pe.wait_ge(s_cnt, it + 1)
                V.matmul(pt[0:SP_P, 0, 0:E8], ones[:], cnt[:], start=True, stop=True).then_inc(s_sum, 1)
            for n in range(2):
                pe.wait_ge(s_cnt, SCORE_BITS + 2 + n)
                V.matmul(pt[0:SP_P, 0, 0:E8], tri[:], cnt[:], start=True, stop=True).then_inc(s_sum, 1)
            for e in range(E8):
                pe.wait_ge(s_hl, e + 1)
                for c in range(SP_C):
                    last = V.matmul(pt[0:ROWT, 1, e * 5 * JT:(e + 1) * 5 * JT], hotlo[e % 2][:, c, :],
                                    parts[:, e * SP_C + c, :, :].rearrange("p a b -> p (a b)"),
                                    start=c == 0, stop=c == SP_C - 1)
                last.then_inc(s_fd, 1)
            pe.wait_ge(s_ci, 1)

            def transposes(s, n, yt_before, gathered):
                pe.wait_ge(s_g[s], gathered)
                for g in range(GT):
                    if yt_before is not None or g:
                        pe.wait_ge(s_yt, g if yt_before is None else yt_before + g)
                    for c in range(CT):
                        for j in range(RT):
                            last = V.transpose(pt[:, c, j * ROWT:(j + 1) * ROWT], gz[s][:, g * RT + j, c * 128:(c + 1) * 128],
                                               eye[0:ROWT, 0:ROWT])
                    last.then_inc(s_tr, 1)

            def up(s, g, it, first):
                n0 = it * (4 * FT) + s * 2 * FT
                for f in range(FT):
                    k = g * FT + f
                    if not (first and k < 3):
                        pe.wait_ge(s_hid, n0 + (k - 2))
                    for c in range(CT):
                        last = V.matmul(pu[:, k % 3, 0:NP], w1[s][:, c * F1 + f * 128:c * F1 + (f + 1) * 128],
                                        yt[s][:, c, g * NP:(g + 1) * NP], start=c == 0, stop=c == CT - 1)
                    last.then_inc(s_up, 1)

            def down(s, g, it, first):
                n0 = it * (4 * FT) + s * 2 * FT
                m0 = it * (2 * JT) + s * JT
                pe.wait_ge(s_hid, n0 + (g + 1) * FT)
                for j in range(RT):
                    if not (first and g == 0):
                        pe.wait_ge(s_oo, m0 + (g * RT + j - RT + 1))
                    V.matmul(pd[0:ROWT, j, 0:C], one_row[:], b2[s][:], start=True, stop=False)
                    for f in range(FT):
                        last = V.matmul(pd[0:ROWT, j, 0:C], hid[g][:, f, j * ROWT:(j + 1) * ROWT], w2[s][:, f, :],
                                        start=False, stop=f == FT - 1)
                    last.then_inc(s_dn, 1)

            def expert(s, it, first, more):
                pe.wait_ge(s_w[s], it * 48 + 48)
                n = it * 4 + (2 * s + 1)
                pe.wait_ge(s_yt, n)
                up(s, 0, it, first)
                pe.wait_ge(s_yt, n + 1)
                up(s, 1, it, False)
                down(s, 0, it, first)
                if more:
                    transposes(1 - s, None, it * 4 + (2 * s + 2), (it + s) * (16 * JT) + 16 * JT)
                down(s, 1, it, False)

            transposes(0, 0, None, 16 * JT)
            for s in range(2):
                expert(s, 0, s == 0, True)
            with pe.Fori(1, E8 // 2 - 1) as it:
                for s in range(2):
                    expert(s, it, False, True)
            for s in range(2):
                expert(s, E8 // 2 - 1, False, s == 0)

        @block.vector
        def _(dve):
            V = nc.vector
            V.memset(ones[:], 1.0)
            V.memset(one_row[:], 1.0)
            pre = Chain(dve, s_v)
            pre.then(V.memset(carry[:], 1.0))
            pre.mark(V.memset(thr[:], 0.0))
            pre.mark(V.memset(step[:], 1.0))
            pre.then(V.memset(carry[:, :, 0:1], 0.0))

            dve.wait_ge(s_ld, 16 * LOADS)
            dve.wait_ge(s_tanh, 1)
            pre.then(V.tensor_scalar(score[:], flag[:], 1.0, 0.5, ALU.add, ALU.mult))
            pre.then(V.tensor_tensor(score[:], score[:], limit[:].unsqueeze(1).broadcast_to([SP_P, E8, SP_C]), ALU.min))

            def over(x):
                return x.unsqueeze(2).broadcast_to([SP_P, E8, SP_C])

            CHAIN = 4
            with dve.Fori(0, SCORE_BITS) as it:
                ch = Chain(dve, s_v, CHAIN, it, base=pre.n)
                ch.then(V.tensor_tensor(cand[:], thr[:], step[:], ALU.add))
                ch.then(V.tensor_tensor(flag[:], score[:], over(cand[:]), ALU.is_ge))
                V.tensor_reduce(cnt[:], flag[:], AX.X, ALU.add).then_inc(s_cnt, 1)
                dve.wait_ge(s_sum, it + 1)
                ch.then(V.scalar_tensor_tensor(upd[:], pt[0:SP_P, 0, 0:E8], float(K_TOP), step[:], ALU.is_ge, ALU.mult))
                V.tensor_scalar(step[:], step[:], 0.5, None, ALU.mult)
                ch.then(V.tensor_tensor(thr[:], thr[:], upd[:], ALU.add))
                assert ch.n == CHAIN
            po = Chain(dve, s_v, base=pre.n + CHAIN * SCORE_BITS)
            po.then(V.tensor_tensor(flag[:], score[:], over(thr[:]), ALU.is_gt))
            V.tensor_reduce(cnt[:], flag[:], AX.X, ALU.add).then_inc(s_cnt, 1)
            V.tensor_tensor(eq[:], score[:], over(thr[:]), ALU.is_equal)
            dve.wait_ge(s_sum, SCORE_BITS + 1)
            po.then(V.tensor_scalar(need[:], pt[0:SP_P, 0, 0:E8], -1.0, float(K_TOP), ALU.mult, ALU.add))

            def flat(x):
                return x.rearrange("p e c -> p (e c)")

            def ranks(x, n):
                po.then(V.tensor_tensor_scan(flat(rank[:]), flat(carry[:]), flat(x[:]), 0.0, ALU.mult, ALU.add))
                V.tensor_copy(cnt[:].unsqueeze(2), rank[:, :, SP_C - 1:SP_C]).then_inc(s_cnt, 1)
                dve.wait_ge(s_sum, n)
                po.then(V.tensor_copy(upd[:], pt[0:SP_P, 0, 0:E8]))
                po.then(V.tensor_tensor(rank[:], rank[:], over(upd[:]), ALU.add))

            ranks(eq, SCORE_BITS + 2)
            po.then(V.tensor_tensor(rank[:], rank[:], over(need[:]), ALU.is_le))
            po.then(V.tensor_tensor(eq[:], eq[:], rank[:], ALU.mult))
            po.then(V.tensor_tensor(flag[:], flag[:], eq[:], ALU.add))
            ranks(flag, SCORE_BITS + 3)
            po.then(V.tensor_scalar(flag[:], flag[:], -2.0 * NTOK, 2.0 * NTOK - 1.0, ALU.mult, ALU.add))
            po.then(V.tensor_tensor(rank[:], rank[:], flag[:], ALU.add))
            for j in range(JT + 1):
                last = V.tensor_scalar(ge[:, :, j], flat(rank[:]), float(ROWT * j), None, ALU.is_ge)
            po.then(last)
            po.mark(V.tensor_tensor(tile1[:], ge[:, :, 0:JT], ge[:, :, 1:JT + 1], ALU.subtract))
            po.then(V.tensor_reduce(flat(lo[:]), ge[:, :, 1:JT], AX.X, ALU.add))
            po.then(V.scalar_tensor_tensor(lo[:], lo[:], -float(ROWT), rank[:], ALU.mult, ALU.add))
            po.then(V.tensor_copy(sp3[:, 0], score[:]))
            po.then(V.tensor_tensor(rest[:, 0], score[:], sp3[:, 0], ALU.subtract))
            po.then(V.tensor_copy(sp3[:, 1], rest[:, 0]))
            po.then(V.tensor_tensor(rest[:, 1], rest[:, 0], sp3[:, 1], ALU.subtract))
            po.then(V.tensor_copy(sp3[:, 2], rest[:, 1]))
            V.tensor_scalar(parts[:, :, 0, :], tile1[:], tokp[:, 0:1], None, ALU.mult)
            t4 = tile1[:].rearrange("p (e c) j -> p e c j", e=E8)
            p4 = parts[:].rearrange("p (e c) a j -> p e c a j", e=E8)
            for e in range(E8):
                last = V.tensor_tensor(p4[:, e, :, 1, :], t4[:, e, :, :], tokc[:].unsqueeze(2).broadcast_to([SP_P, SP_C, JT]), ALU.mult)
            for n in range(3):
                last = V.tensor_tensor(parts[:, :, 2 + n, :], tile1[:], sp3[:, n].rearrange("p e c -> p (e c)").unsqueeze(2).broadcast_to([SP_P, E8 * SP_C, JT]), ALU.mult)
            po.then(last)
            for e in range(E8):
                if e >= 2:
                    dve.wait_ge(s_fd, e - 1)
                V.tensor_tensor(hotlo[e % 2][:], lo[:, e, :].unsqueeze(2).broadcast_to([SP_P, SP_C, ROWT]),
                                lane[:].unsqueeze(1).broadcast_to([SP_P, SP_C, ROWT]), ALU.is_equal).then_inc(s_hl, 1)
            dve.wait_ge(s_fd, E8)
            po.then(V.tensor_copy(found[:].rearrange("p e a j -> p (e a j)"), pt[0:ROWT, 1, 0:E8 * 5 * JT]))
            po.then(V.scalar_tensor_tensor(idxf[:], found[:, :, 0, :], float(SP_C), found[:, :, 1, :], ALU.mult, ALU.add))
            po.then(V.tensor_copy(idx[:], idxf[:]))
            po.then(V.tensor_tensor(kept[:], found[:, :, 2, :], found[:, :, 3, :], ALU.add))
            po.then(V.tensor_tensor(kept[:], kept[:], found[:, :, 4, :], ALU.add))

            def take(s, e):
                V.tensor_copy(ckept[s][:], kept[:, bass.ds(e, 1), :].rearrange("p a j -> p (a j)"))
                V.tensor_copy(cidx[s][:], idx[:, bass.ds(e, 1), :].rearrange("p a j -> p (a j)")).then_inc(s_ci, 1)

            def weigh(s, it):
                m0 = it * (2 * JT) + s * JT
                for j in range(JT):
                    dve.wait_ge(s_dn, m0 + (j + 1))
                    V.tensor_scalar(oo[s][:, j, :], pd[0:ROWT, j % RT, 0:C], ckept[s][:, j:j + 1], None, ALU.mult).then_inc(s_oo, 1)

            for s in range(2):
                take(s, s)
            with dve.Fori(0, E8 // 2 - 1) as it:
                for s in range(2):
                    dve.wait_ge(s_ci, it * 2 + (s + 1))
                    weigh(s, it)
                    dve.wait_ge(s_sc, it * (32 * JT) + 16 * JT * (s + 1))
                    take(s, it * 2 + (s + 2))
            dve.wait_ge(s_ci, E8)
            for s in range(2):
                weigh(s, E8 // 2 - 1)

CH = 12
NCH = TD // CH
TT = 4
NT3 = CH // TT
HG, HH, DH = 4, 4, 16
HD = HH * DH


class Turn:

    def __init__(self, off, it=None):
        self.off, self.it = off, it

    def __add__(self, k):
        return Turn(self.off + k, self.it)

    @property
    def par(self):
        return self.off % 2

    def of(self, k, m):
        return self.off * k + m if self.it is None else self.it * (2 * k) + (self.off * k + m)

    def half(self, k, m):
        return self.off // 2 * k + m if self.it is None else self.it * k + (self.off // 2 * k + m)


def wait(eng, sem, v):
    if not isinstance(v, int) or v > 0:
        eng.wait_ge(sem, v)


def phase_delta(nc, A, acc_rows, proj_rows, o_rows, out):
    ctx = ExitStack()
    with ctx:
        def sb(name, shape, dt=fp32):
            return ctx.enter_context(nc.sbuf_tensor("d_" + name, shape, dt))

        def sem(name):
            return ctx.enter_context(nc.semaphore("d_" + name))

        def pb(name, shape):
            return ctx.enter_context(nc.psum_tensor("d_" + name, shape, fp32))

        NB = 4 * C + C + E8
        (B_QKVB, B_OUT, B_RT) = (0, 4 * C, 5 * C)
        wqkvb = sb("wqkvb", [128, CT, 4 * C])
        wout = sb("wout", [128, CT, C])
        wrt = sb("wrt", [128, CT, E8])
        wex = sb("wex", [128, CT, E8 * C])
        bias = sb("bias", [3, NB])
        bpart = [sb(f"bpart{n}", [3, NB], bf16) for n in range(3)]
        brest = [sb(f"brest{n}", [3, NB]) for n in range(2)]
        brow = sb("brow", [3, NB], bf16)
        ones3 = sb("ones3", [3, 128], bf16)
        ident = sb("ident", [128, 128])
        lnp = sb("lnp", [128, 2, CT])
        epsc = sb("epsc", [128, 3])
        rev = sb("rev", [128, E8])

        h2 = [sb(f"h2{p}", [128, NT3, C]) for p in range(2)]
        st1, mv1, st3, mv3 = sb("st1", [128, NT3, 6]), sb("mv1", [128, NT3, 2]), sb("st3", [128, NT3, 6]), sb("mv3", [128, NT3, 2])
        rs1, rs3 = sb("rs1", [128, 2, NT3]), sb("rs3", [128, NT3])
        onep, nmb = sb("onep", [128, NT3]), sb("nmb", [128, NT3])
        hn = sb("hn", [128, NT3, C])
        ntile = [sb(f"nt{i}", [128, CT, 128]) for i in range(NT3)]
        pr = [sb(f"pr{i}", [128, 4 * C]) for i in range(NT3)]
        base = [sb(f"base{p}", [128, NT3, C]) for p in range(2)]
        D = [sb(f"qkvb{p}", [128, CH, 4 * HD]) for p in range(2)]
        O = [sb(f"o{p}", [128, CH, HD]) for p in range(2)]
        ksq, bab = sb("ksq", [128, CH, HD]), sb("bab", [128, CH, HD])
        ss, inv = sb("ss", [128, CH * HH]), sb("inv", [128, CH * HH])
        S, mk, mq, ou = (sb(n, [128, HD * DH]) for n in ("state", "mk", "mq", "outer"))
        rk, u1, u = sb("rk", [128, HD]), sb("u1", [128, HD]), sb("u", [128, HD])
        otm = sb("otm", [128, NT3, C])
        ott = [sb(f"ot{i}", [128, CT, 128]) for i in range(NT3)]
        wo = sb("wo", [128, NT3, C])
        h3 = [sb(f"h3{p}", [128, NT3, C]) for p in range(2)]
        dd = [sb(f"dd{p}", [128, NT3, C]) for p in range(2)]
        eb = sb("eb", [E8, C])
        wt = sb("wt", [E8, NT3, 128])
        dtile = [sb(f"dt{i}", [128, CT, 128]) for i in range(NT3)]
        mx, lgs, ex, sm, rc = sb("mx", [128, NT3]), sb("lgs", [128, NT3, E8]), sb("ex", [128, NT3, E8]), sb("sm", [128, NT3]), sb("rc", [128, NT3])
        mask, mr, wm = sb("mask", [128, NT3, E8]), sb("mr", [128, NT3]), sb("wm", [128, NT3, E8])
        xw = [sb(f"xw{n}", [128, E8, C]) for n in range(2)]
        xt = [sb(f"xt{n}", [128, 2, CT, 128]) for n in range(2)]
        outb = sb("outb", [128, NT3, C])

        pt = [pb(f"pt{n}", [128, 512]) for n in range(2)]
        pj = pb("pj", [128, 1024])
        pf = [pb(f"pf{n}", [128, 512]) for n in range(2)]
        py, pw = pb("py", [128, 512]), pb("pw", [128, 512])

        s_ld, s_cst, s_bias, s_v, s_a = sem("loads"), sem("consts"), sem("bias_rows"), sem("dve_chain"), sem("act_chain")
        s_h2 = [sem(f"h2_in{p}") for p in range(2)]
        s_dl = [sem(f"qkvb_in{p}") for p in range(2)]
        s_st1, s_rs1, s_hn, s_nb = sem("stats1"), sem("rstd1"), sem("hn_ready"), sem("base_coeffs")
        s_ntt, s_nte, s_pj, s_pre, s_base = sem("nt_done"), sem("nt_evac"), sem("proj_done"), sem("proj_evac"), sem("base_ready")
        s_pst, s_sq, s_sp, s_ss, s_bl, s_inv, s_beta, s_kn = (sem(n) for n in (
            "proj_stored", "k_squares", "softplus", "k_sums", "beta_log", "k_inv", "beta_ready", "k_ready"))
        s_dd, s_ost, s_otl = sem("delta_done"), sem("o_stored"), sem("o_in")
        s_ott, s_ote, s_wo, s_woe = sem("ot_done"), sem("ot_evac"), sem("wout_done"), sem("wout_evac")
        s_h3, s_st3, s_rs3, s_ddn, s_dtt, s_dte = (sem(n) for n in ("h3_ready", "stats3", "rstd3", "d_ready", "dt_done", "dt_evac"))
        s_lg, s_ls, s_ex, s_wm = sem("logits"), sem("logits_less_max"), sem("exps"), sem("expert_weights")
        s_xw, s_f, s_fe, s_yd, s_oe, s_od = (sem(n) for n in (
            "weighted", "xt_done", "xt_evac", "out_summed", "out_evac", "out_stored"))

        s_turn = sem("turn")
        s_l1, s_l3, s_lstep, s_lrt, s_lkb, s_st, s_mq, s_a2 = (sem(n) for n in (
            "stats1_chain", "stats3_chain", "step_chain", "router_chain", "k_chain", "state_ready", "mq_ready", "rstd3_chain"))

        BANKS = 1 + NT3 * E8 // 2
        assert BANKS % 2 == 1
        acc_t = acc_rows.rearrange("(b t) c -> t b c", t=TD)
        out_t = out.rearrange("b t c -> t b c")
        block = ctx.enter_context(nc.Block())

        def schedule(eng, body, prologue):
            prologue()
            for c in range(3):
                body(Turn(c), True, True, c >= 1, c >= 2)
            with eng.Fori(0, (NCH - 1 - 3) // 2) as it:
                for k in range(2):
                    body(Turn(3 + k, it), True, True, True, True)
            body(Turn(NCH - 1), False, True, True, True)
            body(Turn(NCH), False, False, True, True)
            body(Turn(NCH + 1), False, False, False, True)

        assert (NCH - 4) % 2 == 0

        @block.sync
        def _(sp):
            sp.dma_start(bias[:], A["b_row"].broadcast_to([3, NB])).then_inc(s_ld, 16)
            sp.dma_start(ident[:], A["ident"]).then_inc(s_ld, 16)
            sp.dma_start(lnp[:], A["l1_ln"]).then_inc(s_ld, 16)
            sp.dma_start(rev[:], A["rev"].broadcast_to([128, E8])).then_inc(s_ld, 16)

            def load_h2(k):
                wait(sp, s_base, k.of(1, -1))
                sp.sem_inc(s_turn, 1)
                for i in range(NT3):
                    sp.dma_start(h2[k.par][:, i, :], acc_t[bass.ds(k.of(CH, TT * i), TT)]).then_inc(s_h2[k.par], 16)

            def prologue():
                load_h2(Turn(0))
                sp.dma_start(wqkvb[:], A["wqkvb"]).then_inc(s_ld, 16)
                sp.dma_start(wout[:], A["L1_attn_w_out"].rearrange("(a p) n -> p a n", p=128)).then_inc(s_ld, 16)
                sp.dma_start(wrt[:], A["wrt"]).then_inc(s_ld, 16)
                sp.dma_start(wex[:], A["wex"]).then_inc(s_ld, 16)
                sp.dma_start(eb[:], A["L1_ffn_expert_b"]).then_inc(s_ld, 16)
                project_io(Turn(0))

            def project_io(k):
                for i in range(NT3):
                    sp.wait_ge(s_pre, k.of(NT3, i + 1))
                    sp.sem_inc(s_turn, 1)
                    sp.dma_start(proj_rows[bass.ds(k.of(CH, TT * i), TT)].rearrange("t b n -> (t b) n"), pr[i][:]).then_inc(s_pst, 16)
                sp.wait_ge(s_pst, k.of(16 * NT3, 16 * NT3))
                sp.sem_inc(s_turn, 1)
                wait(sp, s_dd, k.of(1, -1))
                sp.sem_inc(s_turn, 1)
                for g in range(HG):
                    sp.dma_start(D[k.par][32 * g:32 * g + 32, :, :],
                                 proj_rows[bass.ds(k.of(CH, 0), CH), :, g * 4 * HD:(g + 1) * 4 * HD].rearrange("t b n -> b t n")).then_inc(s_dl[k.par], 16)

            def body(c, prep, delta, post, routed):
                if prep:
                    load_h2(c + 1)
                if post:
                    k = c + (-1)
                    sp.wait_ge(s_ost, k.of(16 * HG, 16 * HG))
                    sp.sem_inc(s_turn, 1)
                    wait(sp, s_ott, k.of(NT3, 0))
                    sp.sem_inc(s_turn, 1)
                    for i in range(NT3):
                        sp.dma_start(otm[:, i, :], o_rows[bass.ds(k.of(CH, TT * i), TT)].rearrange("t b n -> (t b) n")).then_inc(s_otl, 16)
                if prep:
                    project_io(c + 1)
                if delta:
                    sp.wait_ge(s_dd, c.of(1, 1))
                    sp.sem_inc(s_turn, 1)
                    for g in range(HG):
                        sp.dma_start(o_rows[bass.ds(c.of(CH, 0), CH), :, g * HD:(g + 1) * HD].rearrange("t b n -> b t n"),
                                     O[c.par][32 * g:32 * g + 32, :, :]).then_inc(s_ost, 16)

            schedule(sp, body, prologue)
            sp.wait_ge(s_pst, 16 * NT3 * NCH)
            sp.wait_ge(s_ost, 16 * HG * NCH)
            sp.wait_ge(s_od, 16 * NT3 * NCH)

        @block.gpsimd
        def _(pool):
            V = nc.gpsimd
            for n, v in enumerate((EPS, EPS * EPS, 1.0)):
                V.memset(epsc[:, n:n + 1], v).then_inc(s_cst, 1)
            V.memset(ones3[:], 1.0).then_inc(s_cst, 1)
            V.memset(S[:], 0.0).then_inc(s_cst, 1)

            def body(c, prep, delta, post, routed):
                if routed:
                    k = c + (-2)
                    pool.wait_ge(s_wm, k.of(1, 1))
                    for i in range(NT3):
                        wait(pool, s_yd, k.of(NT3, i - 1))
                        pool.sem_inc(s_turn, 1)
                        for e in range(E8):
                            last = V.tensor_scalar(xw[(k.par + i) % 2][:, e, :], dd[k.par][:, i, :],
                                                   wm[:, i, e:e + 1], None, ALU.mult)
                        last.then_inc(s_xw, 1)

            schedule(pool, body, lambda: None)

        @block.tensor
        def _(pe):
            V = nc.tensor
            pe.wait_ge(s_ld, 16 * 9)
            pe.wait_ge(s_bias, 1)

            def transposes(bank, src, done):
                for c in range(CT):
                    last = V.transpose(bank[:, c * 128:(c + 1) * 128], src[:, c * 128:(c + 1) * 128], ident[:])
                last.then_inc(done, 1)

            def product(out, x, w, b, n):
                V.matmul(out, ones3[:], brow[:, b:b + n], start=True, stop=False)
                for c in range(CT):
                    last = V.matmul(out, x[:, c, :], w[:, c, :], start=False, stop=c == CT - 1)
                return last

            def prep_chunk(k, after_post):
                for i in range(NT3):
                    if i < 2:
                        if after_post:
                            pe.wait_ge(s_ote, k.of(NT3, -2 * NT3 + 2 + i))
                        elif k.off > 0 and i == 0:
                            pe.wait_ge(s_nte, k.of(NT3, 0))
                    else:
                        pe.wait_ge(s_nte, k.of(NT3, 1))
                    pe.wait_ge(s_hn, k.of(NT3, i + 1))
                    transposes(pt[(i + 1) % 2], hn[:, i, :], s_ntt)
                    pe.wait_ge(s_nte, k.of(NT3, i + 1))
                    wait(pe, s_pre, k.of(NT3, i))
                    for n in range(2):
                        last = product(pj[:, n * 512:(n + 1) * 512], ntile[i], wqkvb[:, :, n * 512:(n + 1) * 512], B_QKVB + n * 512, 512)
                    last.then_inc(s_pj, 1)

            def post_a(k):
                pe.wait_ge(s_otl, k.of(16 * NT3, 16 * NT3))
                for i in range(NT3):
                    if i < 2:
                        if k.it is None and k.off == 0:
                            pe.wait_ge(s_nte, 2 * NT3)
                        else:
                            pe.wait_ge(s_dte, k.of(NT3, 0))
                    else:
                        pe.wait_ge(s_ote, k.of(NT3, 1))
                    transposes(pt[i % 2], otm[:, i, :], s_ott)
                    pe.wait_ge(s_ote, k.of(NT3, i + 1))
                    wait(pe, s_woe, k.of(NT3, i))
                    if i == 0:
                        wait(pe, s_ls, k.of(1, 0))
                    product(pw[:, 0:C], ott[i], wout, B_OUT, C).then_inc(s_wo, 1)

            def post_b(k, prep):
                for i in range(NT3):
                    if i < 2:
                        if prep:
                            pe.wait_ge(s_nte, k.of(NT3, 2 * NT3 + 2 + i))
                        else:
                            pe.wait_ge(s_ote, k.of(NT3, NT3))
                    else:
                        pe.wait_ge(s_dte, k.of(NT3, 1))
                    pe.wait_ge(s_ddn, k.of(NT3, i + 1))
                    transposes(pt[i % 2], dd[k.par][:, i, :], s_dtt)
                    pe.wait_ge(s_dte, k.of(NT3, i + 1))
                    if i == 0:
                        pe.wait_ge(s_woe, k.of(NT3, NT3))
                    last = product(pw[:, C + i * E8:C + (i + 1) * E8], dtile[i], wrt, B_RT, E8)
                last.then_inc(s_lg, 1)

            def weights(k):
                pe.wait_ge(s_wm, k.of(1, 1))
                wait(pe, s_fe, k.of(BANKS, -1))
                for i in range(NT3):
                    last = V.transpose(pf[k.par][0:E8, i * 128:(i + 1) * 128], wm[:, i, :], ident[:])
                last.then_inc(s_f, 1)

            def routed_tile(k, i):
                n0 = 1 + i * E8 // 2
                src = xw[(k.par + i) % 2]

                def turn_pair(q):
                    wait(pe, s_fe, k.of(BANKS, n0 + q - 1))
                    for n in range(2 * CT):
                        e, c = 2 * q + n // CT, n % CT
                        last = V.transpose(pf[(k.par + n0 + q) % 2][:, n * 128:(n + 1) * 128], src[:, e, c * 128:(c + 1) * 128], ident[:])
                    last.then_inc(s_f, 1)

                def multiply_pair(q):
                    pe.wait_ge(s_fe, k.of(BANKS, n0 + q + 1))
                    for n in range(2 * CT):
                        e, c = 2 * q + n // CT, n % CT
                        last = V.matmul(py[:, 0:C], xt[q % 2][:, n // CT, c, :], wex[:, c, e * C:(e + 1) * C],
                                        start=False, stop=q == 3 and n == 2 * CT - 1)
                    return last

                pe.wait_ge(s_xw, k.of(NT3, i + 1))
                turn_pair(0)
                turn_pair(1)
                wait(pe, s_oe, k.of(NT3, i))
                V.matmul(py[:, 0:C], ident[:], h3[k.par][:, i, :], start=True, stop=False)
                pe.wait_ge(s_fe, k.of(BANKS, 1))
                V.matmul(py[:, 0:C], wt[:, i, :], eb[:], start=False, stop=False)
                multiply_pair(0)
                turn_pair(2)
                multiply_pair(1)
                turn_pair(3)
                multiply_pair(2)
                multiply_pair(3).then_inc(s_yd, 1)

            def body(c, prep, delta, post, routed):
                if post:
                    post_a(c + (-1))
                if routed:
                    pe.wait_ge(s_h3, c.of(1, -1))
                    weights(c + (-2))
                    routed_tile(c + (-2), 0)
                    routed_tile(c + (-2), 1)
                if prep:
                    prep_chunk(c + 1, post)
                if routed:
                    routed_tile(c + (-2), 2)
                if post:
                    post_b(c + (-1), prep)

            schedule(pe, body, lambda: prep_chunk(Turn(0), False))

        @block.scalar
        def _(act):
            V = nc.scalar
            one_act_table(nc)
            act.wait_ge(s_cst, 5)
            act.wait_ge(s_ld, 16 * 9)

            def rstd(k):
                act.wait_ge(s_st1, k.of(1, 1))
                var = mv1[:, :, 1]
                V.activation(rs1[:, 0, :], var, ACT.Ln, bias=epsc[:, 0:1]).then_inc(s_a, 1)
                V.activation(rs1[:, 1, :], var, ACT.Ln, bias=epsc[:, 1:2], scale=1.0 + EPS).then_inc(s_a, 1)
                act.wait_ge(s_a, k.of(5, 2))
                V.activation(rs1[:], rs1[:], ACT.Exp, scale=-0.5).then_inc(s_rs1, 1)

            def prep_chunk(k):
                for i in range(NT3):
                    act.wait_ge(s_ntt, k.of(NT3, i + 1))
                    for c in range(CT):
                        last = V.activation(ntile[i][:, c, :], pt[(i + 1) % 2][:, c * 128:(c + 1) * 128], ACT.Identity,
                                            scale=lnp[:, 0, c:c + 1], bias=lnp[:, 1, c:c + 1])
                    last.then_inc(s_nte, 1)
                    act.wait_ge(s_pj, k.of(NT3, i + 1))
                    wait(act, s_pst, k.of(16 * NT3, 0))
                    V.activation(pr[i][:], pj[:], ACT.Copy).then_inc(s_pre, 1)
                act.wait_ge(s_nb, k.of(1, 1))
                wait(act, s_h3, k.of(1, -1))
                for i in range(NT3):
                    last = V.activation(base[k.par][:, i, :], h2[k.par][:, i, :], ACT.Identity,
                                        scale=onep[:, i:i + 1], bias=nmb[:, i:i + 1])
                last.then_inc(s_base, 1)

            def keys_and_betas(k):
                d = D[k.par]
                act.wait_ge(s_dl[k.par], k.half(16 * HG, 16 * HG))
                V.activation(ksq[:], d[:, :, HD:2 * HD], ACT.Square).then_inc(s_sq, 1)
                V.activation(bab[:], d[:, :, 3 * HD:4 * HD], ACT.Abs).then_inc(s_a, 1)
                act.wait_ge(s_a, k.of(5, 3))
                V.activation(bab[:], bab[:], ACT.Exp, scale=-1.0).then_inc(s_a, 1)
                act.wait_ge(s_a, k.of(5, 4))
                V.activation(bab[:], bab[:], ACT.Ln, bias=epsc[:, 2:3]).then_inc(s_sp, 1)

            def keys_and_betas_end(k):
                d = D[k.par]
                act.wait_ge(s_ss, k.of(1, 1))
                V.activation(inv[:], ss[:], ACT.Ln).then_inc(s_a, 1)
                act.wait_ge(s_a, k.of(5, 5))
                V.activation(inv[:], inv[:], ACT.Exp, scale=-0.5).then_inc(s_inv, 1)
                act.wait_ge(s_bl, k.of(1, 1))
                V.activation(d[:, :, 3 * HD:4 * HD], d[:, :, 3 * HD:4 * HD], ACT.Exp).then_inc(s_beta, 1)

            def attention_rows(k):
                for i in range(NT3):
                    act.wait_ge(s_ott, k.of(NT3, i + 1))
                    V.activation(ott[i][:].rearrange("p c n -> p (c n)"), pt[i % 2][:, 0:C], ACT.Copy).then_inc(s_ote, 1)
                    act.wait_ge(s_wo, k.of(NT3, i + 1))
                    if i == 0:
                        wait(act, s_h3, k.of(1, 0))
                    V.activation(wo[:, i, :], pw[:, 0:C], ACT.Copy).then_inc(s_woe, 1)

            def weights(k):
                act.wait_ge(s_f, k.of(BANKS, 1))
                V.activation(wt[:].rearrange("p i n -> p (i n)"), pf[k.par][0:E8, 0:NT3 * 128], ACT.Copy).then_inc(s_fe, 1)

            def routed_tile(k, i):
                n0 = 1 + i * E8 // 2
                for q in range(E8 // 2):
                    act.wait_ge(s_f, k.of(BANKS, n0 + q + 1))
                    V.activation(xt[q % 2][:].rearrange("p e c n -> p (e c n)"), pf[(k.par + n0 + q) % 2][:], ACT.Copy).then_inc(s_fe, 1)
                act.wait_ge(s_yd, k.of(NT3, i + 1))
                wait(act, s_od, k.of(16 * NT3, 0))
                V.activation(outb[:, i, :], py[:, 0:C], ACT.Copy).then_inc(s_oe, 1)
                act.wait_ge(s_oe, k.of(NT3, i + 1))
                if k.it is None and k.off == NCH - 1 and i == NT3 - 1:
                    n = T - (NCH * CH - TT)
                    act.dma_start(out_t[T - n:T], outb[0:32 * n, i, :]).then_inc(s_od, 16)
                else:
                    act.dma_start(out_t[bass.ds(k.of(CH, TT * i), TT)], outb[:, i, :]).then_inc(s_od, 16)

            def body(c, prep, delta, post, routed):
                if post:
                    attention_rows(c + (-1))
                if prep:
                    rstd(c + 1)
                if routed:
                    weights(c + (-2))
                    routed_tile(c + (-2), 0)
                    routed_tile(c + (-2), 1)
                if prep:
                    prep_chunk(c + 1)
                if routed:
                    routed_tile(c + (-2), 2)
                if post:
                    k = c + (-1)
                    act.wait_ge(s_st3, k.of(1, 1))
                    V.activation(rs3[:], mv3[:, :, 1], ACT.Ln, bias=epsc[:, 0:1]).then_inc(s_a2, 1)
                    act.wait_ge(s_a2, k.of(1, 1))
                    V.activation(rs3[:], rs3[:], ACT.Exp, scale=-0.5).then_inc(s_rs3, 1)
                    for i in range(NT3):
                        act.wait_ge(s_dtt, k.of(NT3, i + 1))
                        V.activation(dtile[i][:].rearrange("p c n -> p (c n)"), pt[i % 2][:, 0:C], ACT.Copy).then_inc(s_dte, 1)
                if prep:
                    keys_and_betas(c + 1)
                if post:
                    act.wait_ge(s_ls, (c + (-1)).of(1, 1))
                    V.activation(ex[:], lgs[:], ACT.Exp).then_inc(s_ex, 1)
                if prep:
                    keys_and_betas_end(c + 1)

            def prologue():
                rstd(Turn(0))
                prep_chunk(Turn(0))
                keys_and_betas(Turn(0))
                keys_and_betas_end(Turn(0))

            schedule(act, body, prologue)

        @block.vector
        def _(dve):
            V = nc.vector
            pre = Chain(dve, s_v)
            dve.wait_ge(s_ld, 16 * 9)
            dve.wait_ge(s_cst, 5)
            pre.then(V.tensor_copy(bpart[0][:], bias[:]))
            pre.then(V.tensor_tensor(brest[0][:], bias[:], bpart[0][:], ALU.subtract))
            pre.then(V.tensor_copy(bpart[1][:], brest[0][:]))
            pre.then(V.tensor_tensor(brest[1][:], brest[0][:], bpart[1][:], ALU.subtract))
            pre.then(V.tensor_copy(bpart[2][:], brest[1][:]))
            pre.then(V.tensor_scalar(brest[0][:], bpart[0][:], ident[0:3, 0:1], None, ALU.mult))
            pre.then(V.scalar_tensor_tensor(brest[1][:], bpart[1][:], ident[0:3, 1:2], brest[0][:], ALU.mult, ALU.add))
            V.scalar_tensor_tensor(brow[:], bpart[2][:], ident[0:3, 2:3], brest[1][:], ALU.mult, ALU.add).then_inc(s_bias, 1)

            class Link:

                def __init__(self, sem_, per):
                    self.sem, self.per = sem_, per

                def start(self, k):
                    self.k, self.n = k, 0

                def then(self, ins):
                    self.n += 1
                    ins.then_inc(self.sem, 1)
                    dve.wait_ge(self.sem, self.k.of(self.per, self.n))

                def end(self):
                    assert self.n == self.per, (self.n, self.per)

            l_st1, l_st3, l_step, l_rt, l_kb = Link(s_l1, 1), Link(s_l3, 1), Link(s_lstep, 5 * CH), Link(s_lrt, 7), Link(s_lkb, 1)

            def stats(k, x, st, mv, link, done):
                link.start(k)
                for i in range(NT3):
                    last = V.bn_stats(st[:, i, :], x[:, i, :])
                link.then(last)
                dve.sem_inc(s_turn, 1)
                for i in range(NT3):
                    last = V.bn_aggr(mv[:, i, :], st[:, i, :])
                last.then_inc(done, 1)
                link.end()

            def norm_rows(k):
                dve.wait_ge(s_rs1, k.of(1, 1))
                for i in range(NT3):
                    V.tensor_scalar(hn[:, i, :], h2[k.par][:, i, :], mv1[:, i, 0:1], rs1[:, 1, i:i + 1], ALU.subtract, ALU.mult).then_inc(s_hn, 1)
                wait(dve, s_base, k.of(1, 0))
                V.tensor_scalar(onep[:], rs1[:, 0, :], 1.0, None, ALU.add)
                V.scalar_tensor_tensor(nmb[:], mv1[:, :, 0], -1.0, rs1[:, 0, :], ALU.mult, ALU.mult).then_inc(s_nb, 1)

            def step(c, t):
                d, s4 = D[c.par], S[:].rearrange("p (h i j) -> p h i j", h=HH, i=DH)

                def col(n):
                    return d[:, t, n * HD:(n + 1) * HD]

                def along_i(x):
                    return x.rearrange("p (h j) -> p h j", h=HH).unsqueeze(2).broadcast_to([128, HH, DH, DH])

                def heads(x):
                    return x[:].rearrange("p (h i j) -> p h i j", h=HH, i=DH)

                def rows(x):
                    return x[:].rearrange("p (r j) -> p r j", j=DH)

                q, k, v, b = (col(n) for n in range(4))
                l_step.then(V.tensor_tensor(heads(mk), s4, along_i(k), ALU.mult))
                l_step.then(V.tensor_reduce(rk[:], rows(mk), AX.X, ALU.add))
                l_step.then(V.tensor_tensor(u1[:], v, rk[:], ALU.subtract))
                l_step.then(V.tensor_tensor(u[:], u1[:], b, ALU.mult))
                l_step.then(V.tensor_tensor(heads(ou), u[:].unsqueeze(2).broadcast_to([128, HD, DH]).rearrange("p (h i) j -> p h i j", h=HH), along_i(k), ALU.mult))
                ins = V.tensor_tensor(S[:], S[:], ou[:], ALU.add)
                ins.then_inc(s_st, 1)
                dve.wait_ge(s_st, c.of(CH, t + 1))
                ins = V.tensor_tensor(heads(mq), s4, along_i(q), ALU.mult)
                ins.then_inc(s_mq, 1)
                dve.wait_ge(s_mq, c.of(CH, t + 1))
                last = V.tensor_reduce(O[c.par][:, t, :], rows(mq), AX.X, ALU.add)
                if t == CH - 1:
                    last.then_inc(s_dd, 1)

            def steps(c, t0, t1):
                if t0 == 0:
                    dve.wait_ge(s_kn, c.of(1, 1))
                    dve.wait_ge(s_beta, c.of(1, 1))
                    wait(dve, s_ost, c.of(16 * HG, -16 * HG))
                    l_step.start(c)
                for t in range(t0, t1):
                    step(c, t)
                if t1 == CH:
                    l_step.end()

            def keys_sums(k):
                l_kb.start(k)
                dve.wait_ge(s_sq, k.of(1, 1))
                l_kb.then(V.tensor_reduce(ss[:], ksq[:].rearrange("p t (h j) -> p (t h) j", h=HH), AX.X, ALU.add))
                V.tensor_scalar(ss[:], ss[:], 1e-12, None, ALU.max).then_inc(s_ss, 1)
                dve.wait_ge(s_sp, k.of(1, 1))
                b = D[k.par][:, :, 3 * HD:4 * HD]
                V.scalar_tensor_tensor(b, b, 0.0, bab[:], ALU.min, ALU.subtract).then_inc(s_bl, 1)
                l_kb.end()

            def keys_end(k):
                dve.wait_ge(s_inv, k.of(1, 1))
                kk = D[k.par][:, :, HD:2 * HD].rearrange("p t (h j) -> p t h j", h=HH)
                V.tensor_tensor(kk, kk, inv[:].rearrange("p (t h) -> p t h", h=HH).unsqueeze(3).broadcast_to([128, CH, HH, DH]), ALU.mult).then_inc(s_kn, 1)

            def add_base(k):
                dve.wait_ge(s_woe, k.of(NT3, NT3))
                dve.wait_ge(s_base, k.of(1, 1))
                wait(dve, s_yd, k.of(NT3, -NT3))
                V.tensor_tensor(h3[k.par][:], wo[:], base[k.par][:], ALU.add).then_inc(s_h3, 1)
                dve.wait_ge(s_h3, k.of(1, 1))
                stats(k, h3[k.par], st3, mv3, l_st3, s_st3)

            def norm_d(k):
                dve.wait_ge(s_rs3, k.of(1, 1))
                for i in range(NT3):
                    V.tensor_scalar(dd[k.par][:, i, :], h3[k.par][:, i, :], mv3[:, i, 0:1], rs3[:, i:i + 1], ALU.subtract, ALU.mult).then_inc(s_ddn, 1)

            def over8(x):
                return x.unsqueeze(2).broadcast_to([128, NT3, E8])

            def router_a(k):
                l_rt.start(k)
                lg = pw[:, C:C + NT3 * E8].rearrange("p (i e) -> p i e", e=E8)
                dve.wait_ge(s_lg, k.of(1, 1))
                l_rt.then(V.tensor_reduce(mx[:], lg, AX.X, ALU.max))
                V.tensor_tensor(lgs[:], lg, over8(mx[:]), ALU.subtract).then_inc(s_ls, 1)

            def router_b(k):
                dve.wait_ge(s_ex, k.of(1, 1))
                l_rt.then(V.tensor_reduce(sm[:], ex[:], AX.X, ALU.add))
                l_rt.then(V.reciprocal(rc[:], sm[:]))
                dve.wait_ge(s_ls, k.of(1, 1))
                l_rt.then(V.tensor_scalar(mask[:], lgs[:], 0.0, None, ALU.is_equal))
                l_rt.then(V.tensor_tensor(mask[:], mask[:], rev[:].unsqueeze(1).broadcast_to([128, NT3, E8]), ALU.mult))
                l_rt.then(V.tensor_reduce(mr[:], mask[:], AX.X, ALU.max))
                l_rt.then(V.tensor_tensor(mask[:], mask[:], over8(mr[:]), ALU.is_equal))
                wait(dve, s_yd, k.of(NT3, 0))
                V.tensor_tensor(wm[:], mask[:], over8(rc[:]), ALU.mult).then_inc(s_wm, 1)
                l_rt.end()

            def stats1(k):
                dve.wait_ge(s_h2[k.par], k.half(16 * NT3, 16 * NT3))
                stats(k, h2[k.par], st1, mv1, l_st1, s_st1)

            def body(c, prep, delta, post, routed):
                if delta:
                    steps(c, 0, 2)
                if prep:
                    stats1(c + 1)
                if delta:
                    steps(c, 2, 4)
                if prep:
                    norm_rows(c + 1)
                if delta:
                    steps(c, 4, 6)
                if post:
                    add_base(c + (-1))
                if delta:
                    steps(c, 6, 8)
                if post:
                    norm_d(c + (-1))
                if delta:
                    steps(c, 8, CH)
                if post:
                    router_a(c + (-1))
                if prep:
                    keys_sums(c + 1)
                    keys_end(c + 1)
                if post:
                    router_b(c + (-1))

            def prologue():
                stats1(Turn(0))
                norm_rows(Turn(0))
                keys_sums(Turn(0))
                keys_end(Turn(0))

            schedule(dve, body, prologue)


def build(nc, A, out):
    def scratch(name, shape):
        return nc.dram_tensor(name, shape, fp32, kind="Internal").ap()

    z_rows, acc_rows = scratch("z_rows", (NROW, C)), scratch("acc_rows", (NROW, C))
    score_rows = scratch("score_rows", (E8, NROW))
    phase_tokens(nc, A, z_rows, acc_rows, score_rows)
    phase_experts(nc, A, z_rows, acc_rows, score_rows)
    phase_delta(nc, A, acc_rows, scratch("proj_rows", (TD, B, 4 * C)), scratch("o_rows", (TD, B, C)), out)


def layouts(i):
    def slices(w, n=128):
        return w.reshape(-1, n, *w.shape[1:]).swapaxes(0, 1)

    def by_group(w):
        return w.reshape(*w.shape[:-1], 4, HG, HD).swapaxes(-3, -2).reshape(*w.shape[:-1], 4 * C)

    a, f = "L0_attn_", "L0_ffn_"
    d = {n: i[n] for n in ("x_txt", "L0_txt_W", "L0_tok_cls_token", "L0_attn_w_tk", "L0_attn_w_tv", "L0_attn_w_tr",
                           "L0_attn_w_ck", "L0_attn_w_cv", "L0_attn_w_cr", "L1_attn_w_out", "L1_ffn_expert_b")}
    p = i["x"].reshape(PAIRS, 2, 3, 6, 16, 6, 16).transpose(0, 2, 4, 6, 1, 3, 5).reshape(PAIRS, PK, 128, 2 * NIMG)
    d["patches"] = p.transpose(0, 2, 1, 3)
    d["wtok_t"] = slices(i["L0_tok_w"].T)
    d["emb_t"] = i["L0_txt_emb_tables"].transpose(2, 0, 1)
    d["pos_t"] = slices(np.concatenate([i["L0_tok_pos"], i["L0_txt_pos_table"][:NTXT]], 0).T)
    vectors = [i["L0_tok_b"], i["L0_txt_b"]] + [i[a + n].reshape(-1) for n in (
        "time_decay", "time_first", "ln1_g", "ln1_b", "ln2_g", "ln2_b", "mix_k", "mix_v", "mix_r", "cmix_k", "cmix_r")]
    d["prm"] = np.stack(vectors).reshape(len(vectors), CT, 128).transpose(2, 0, 1)
    d["gate_t"] = slices(i[f + "gate_w"].T)
    w1 = i[f + "fc1s"].transpose(0, 2, 1).reshape(E8, CT, 128, F1).transpose(0, 2, 1, 3).reshape(E8, 128, CT * F1)
    d["w1"] = np.concatenate([w1, i[f + "b1s"].reshape(E8, FT, 128).transpose(0, 2, 1)], 2)
    d["w2"] = i[f + "fc2s"].transpose(0, 2, 1).reshape(E8, FT, 128, C).transpose(0, 2, 1, 3)
    d["b2"] = i[f + "b2s"]
    d["ffn_ln"] = np.stack([i[f + "ln_gamma"], i[f + "ln_beta"]]).reshape(2, CT, 128).transpose(2, 0, 1)
    d["wqkvb"] = slices(by_group(i["L1_attn_w_qkvb"]))
    d["wrt"] = slices(i["L1_ffn_router_w"].T)
    d["wex"] = slices(i["L1_ffn_expert_w"].transpose(2, 0, 1).reshape(C, E8 * C))
    d["b_row"] = np.concatenate([by_group(i["L1_attn_b_qkvb"]), i["L1_attn_b_out"], i["L1_ffn_router_b"]])[None]
    d["l1_ln"] = np.stack([i["L1_attn_ln_g"], i["L1_attn_ln_b"]]).reshape(2, CT, 128).transpose(2, 0, 1)
    f4 = np.float32
    d["ident"], d["tri"] = np.eye(128, dtype=f4), np.triu(np.ones((SP_P, SP_P), f4), 1)
    d["rowid"], d["tokp"] = np.arange(VOCAB, dtype=f4)[:, None], np.arange(SP_P, dtype=f4)[:, None]
    d["iota"], d["rev"] = np.arange(128, dtype=f4)[None], np.arange(E8, 0, -1, dtype=f4)[None]
    d["limit"] = np.where(np.arange(NROW) % TD < T, 2.0, -1.0).astype(f4).reshape(SP_P, SP_C)
    return {n: np.ascontiguousarray(v) for n, v in d.items()}


def kernel(**inputs):
    from concourse.bass_utils import run_bass_kernel_spmd
    import concourse.bacc as bacc

    data = layouts({n: np.asarray(v) for n, v in inputs.items()})
    nc = bacc.Bacc("TRN2", target_bir_lowering=False, num_devices=1)
    A = {n: nc.dram_tensor("in_" + n, v.shape, mybir.dt.from_np(v.dtype), kind="ExternalInput").ap() for n, v in data.items()}
    out = nc.dram_tensor("out_0_dram", (B, T, C), fp32, kind="ExternalOutput").ap()
    build(nc, A, out)
    r = run_bass_kernel_spmd(nc, [{"in_" + n: v for n, v in data.items()}], core_ids=[0])
    return r.results[0]["out_0_dram"]
```

```python
import numpy as np
import concourse.bass as bass
from concourse import mybir
from contextlib import ExitStack

fp32 = mybir.dt.float32
bf16 = mybir.dt.bfloat16
i32 = mybir.dt.int32
ALU = mybir.AluOpType
ACT = mybir.ActivationFunctionType
AX = mybir.AxisListType

B, T, C = 32, 165, 256
CT = C // 128
NIMG, NTXT = 36, 128
NTOK = B * T
TD = 168
NROW = B * TD
PAIRS = B // 2
NP = 2 * T
TP = T + 1
W4 = CT * 2 * TP
WC = CT * NP
VOCAB, NFREQ = 64, 4
PK = 6
F1 = 4 * C
FT = F1 // 128
E8 = 8
K_TOP = NTOK // E8
ROWT = 110
RT = NP // ROWT
EPS = 1e-5
NEG = -1e38


def one_act_table(nc):
    nc.scalar.add_instruction(mybir.InstLoadActFuncSet(
        name=nc.get_next_instruction_name(), act_func_set_id=6, engine=nc.scalar.engine))


class Chain:

    def __init__(self, eng, sem, per_turn=0, turn=None, base=0):
        self.eng, self.sem, self.n, self.per, self.turn, self.base = eng, sem, 0, per_turn, turn, base

    def mark(self, ins):
        self.n += 1
        ins.then_inc(self.sem, 1)
        return self.n

    def wait(self, n=None):
        n = self.base + (self.n if n is None else n)
        self.eng.wait_ge(self.sem, n if self.turn is None else self.turn * self.per + n)

    def then(self, ins):
        self.mark(ins)
        self.wait()


def phase_tokens(nc, A, s_turn, z_rows, acc_rows, score_rows):
    ctx = ExitStack()
    sems = []
    with ctx:
        def sb(name, shape, dt=fp32):
            return ctx.enter_context(nc.sbuf_tensor(name, shape, dt))

        def sem(name):
            sems.append(nc.alloc_semaphore(name=name))
            return sems[-1]

        wtok = sb("wtok", [128, PK, C])
        wtk, wtv, wtr, wcr = (sb(n, [128, CT, C]) for n in ("wtk", "wtv", "wtr", "wcr"))
        wck = sb("wck", [128, CT, F1])
        wcv = sb("wcv", [128, FT, C])
        wgate = sb("wgate", [128, CT, E8])
        table = sb("table", [VOCAB + 1, C])
        pos = sb("pos", [128, CT, T])
        ident = sb("ident", [128, 128])
        mean_w = sb("mean_w", [128, 128])
        rowid = sb("rowid", [VOCAB, 1])
        epsc = sb("epsc", [128, 3])
        prm = sb("prm", [128, 13, CT])
        (TOKB, TXTB, DECAY, FIRST, G1, B1, G2, B2, MK, MV, MR, CK, CR) = range(13)
        wdec = sb("wdec", [128, W4])
        emb = sb("emb", [128, NFREQ, VOCAB])
        wtxt = sb("wtxt", [128, NFREQ, C])

        names = ["h0", "xc", "sq", "xa", "hh", "dd", "m0", "m1", "m2", "kk", "vv", "mm", "al", "be",
                 "pp", "ca", "cv", "aa"]
        tl = [{n: sb(f"{n}{s}", [128, W4]) for n in names} for s in range(2)]
        tmp = [sb(f"tmp{s}", [128, 4 * W4]) for s in range(2)]
        half = [sb(f"half{s}", [128, 2, NP]) for s in range(2)]
        patch = [sb(f"patch{s}", [128, PK, 2 * NIMG]) for s in range(2)]
        ids = [sb(f"ids{s}", [VOCAB, 2, NTXT], i32) for s in range(2)]
        hot = [sb(f"hot{s}", [VOCAB + 1, 2, T]) for s in range(2)]
        rows = [sb(f"rows{s}", [ROWT, RT, 2, C]) for s in range(2)]
        scs = [sb(f"scs{s}", [E8, NP]) for s in range(2)]
        ps = [ctx.enter_context(nc.psum_tensor(f"ps{s}", [128, 4, 512], fp32)) for s in range(2)]

        zero = sb("zero", [B * (TD - T), C])

        s_ld, s_ld2, s_fill = sem("loads"), sem("table_loads"), sem("filled")
        s_in = [sem(f"pair_in{s}") for s in range(2)]
        s_out = [sem(f"rows_out{s}") for s in range(2)]
        s_const, s_pre = sem("consts"), sem("dve_consts")
        s_tabp, s_tab = sem("table_psum"), sem("table_ready")

        def both_streams(name):
            return [sem(f"{name}{s}") for s in range(2)]

        s_v, s_a, s_hot = (both_streams(n) for n in ("dve_chain", "act_chain", "onehot_ready"))
        s_emb, s_h0, s_mean, s_xc, s_sq, s_var = (both_streams(n) for n in (
            "embedded", "h0_ready", "mean_done", "centred", "squared", "var_done"))
        s_rs, s_hc, s_h = (both_streams(n) for n in ("rstd_ready", "normed", "h_ready"))
        s_mix, s_proj, s_pev = (both_streams(n) for n in ("mixed", "projected", "projection_evac"))
        s_t1, s_ab, s_pp, s_lp, s_s, s_cc, s_e12, s_den, s_lden, s_sg, s_gate = (both_streams(n) for n in (
            "t1", "alpha_beta", "p_scan", "log_p", "s_ready", "ca_cb", "gate_exp", "den", "log_den",
            "gate_log", "gate_sum"))
        s_x1 = both_streams("x1_ready")
        s_ck, s_relu, s_kk2, s_cv = (both_streams(n) for n in ("ck_done", "relu_done", "squares", "cv_done"))
        s_cg, s_cge, s_crm2 = (both_streams(n) for n in ("cgate_softplus", "cgate_log", "cgate_exp"))
        s_h1, s_xf, s_hx = (both_streams(n) for n in ("h1_ready", "xf_ready", "hx_ready"))
        s_scm, s_sce, s_tr, s_tre = (both_streams(n) for n in ("score_done", "score_evac", "rows_done", "rows_evac"))

        def grid(x):
            return x[:, 0:W4].rearrange("p (c s t) -> p c s t", c=CT, s=2)

        def real(x):
            return grid(x)[:, :, :, 1:TP]

        def prev(x):
            return grid(x)[:, :, :, 0:T]

        def real4(x):
            return x[:, 0:W4].rearrange("p (r t) -> p r t", t=TP)[:, :, 1:TP]

        def prev4(x):
            return x[:, 0:W4].rearrange("p (r t) -> p r t", t=TP)[:, :, 0:T]

        def pads(x):
            return x[:, 0:W4].rearrange("p (r t) -> p r t", t=TP)[:, :, 0:1]

        def realc(x, c):
            return grid(x)[:, c, :, 1:TP]

        def prevc(x, c):
            return grid(x)[:, c, :, 0:T]

        def comp(x):
            return x[:, 0:WC].rearrange("p (c s t) -> p c s t", c=CT, s=2)

        def comp4(x):
            return x[:, 0:WC].rearrange("p (r t) -> p r t", t=T)

        def compc(x, c):
            return comp(x)[:, c, :, :]

        def both(x):
            return x.rearrange("p (s t) -> p s t", s=2).unsqueeze(1).broadcast_to([128, CT, 2, T])

        def bank2(s, b0):
            return ps[s][:, b0:b0 + 2, 0:NP].rearrange("p c (s t) -> p c s t", s=2)

        def scratch(s, n):
            return tmp[s][:, n * W4:(n + 1) * W4]

        def hidden(s, f):
            return tmp[s][:, f * NP:(f + 1) * NP]

        def vec(i, c):
            return prm[:, i, c:c + 1]

        OUTS = 16 * 9
        TURNS = PAIRS // 2
        ORDER = ("hot MEAN1 emb VAR1 mean0 NRM1 var0 CMIX nrm0 CR F0 mix F1 k v maxscan ab F2 F3 F4 CGE vevac psum r revac XH F5 F6 s gsp cc den state F7 F8 F9 lden F10 H1 MEAN2 gate gexp num VAR2 x1 Z SCORE ROWS").split()

        def schedule(eng, stages):
            def half(t, t_turn, c, c_turn):
                for name in ORDER:
                    if name in stages:
                        s, it = (c, c_turn) if name.isupper() else (t, t_turn)
                        if s is not None:
                            stages[name](s, it)

            half(0, 0, None, None)
            with eng.Fori(0, TURNS - 1) as it:
                half(1, it, 0, it)
                half(0, it + 1, 1, it)
            half(1, TURNS - 1, 0, TURNS - 1)
            half(None, None, 1, TURNS - 1)

        block = ctx.enter_context(nc.Block())

        @block.sync
        def _(sp):
            sp.dma_start(emb[:], A["emb_t"]).then_inc(s_ld2, 16)
            sp.dma_start(wtxt[:], A["L0_txt_W"].rearrange("(f p) e -> p f e", p=128)).then_inc(s_ld2, 16)
            sp.dma_start(table[VOCAB:VOCAB + 1, :], A["L0_tok_cls_token"].rearrange("(a n) -> a n", a=1)).then_inc(s_ld2, 16)
            sp.dma_start(prm[:], A["prm"]).then_inc(s_ld, 16)
            sp.dma_start(pos[:], A["pos_t"]).then_inc(s_ld, 16)
            sp.dma_start(ident[:], A["ident"]).then_inc(s_ld, 16)
            sp.dma_start(rowid[:], A["rowid"]).then_inc(s_ld, 16)
            sp.dma_start(wtok[:], A["wtok_t"]).then_inc(s_ld, 16)

            def load_pair(i, s):
                sp.dma_start(patch[s][:], A["patches"][bass.ds(i, 1)].rearrange("a p k n -> (a p) k n")).then_inc(s_in[s], 16)
                src = A["x_txt"][bass.ds(2 * i, 2), :].unsqueeze(0).broadcast_to([VOCAB, 2, NTXT])
                sp.dma_start(ids[s][:], src).then_inc(s_in[s], 16)

            for s in range(2):
                load_pair(s, s)
            for w, n in ((wtk, "w_tk"), (wtv, "w_tv"), (wtr, "w_tr"), (wcr, "w_cr"), (wck, "w_ck")):
                sp.dma_start(w[:], A["L0_attn_" + n].rearrange("(a p) n -> p a n", p=128)).then_inc(s_ld, 16)
            sp.dma_start(wcv[:], A["L0_attn_w_cv"].rearrange("(a p) n -> p a n", p=128)).then_inc(s_ld, 16)
            sp.dma_start(wgate[:], A["gate_t"]).then_inc(s_ld, 16)

            sp.wait_ge(s_const, 5)
            for dst in (z_rows, acc_rows):
                sp.dma_start(dst.rearrange("(b t) c -> b t c", t=TD)[:, T:TD, :], zero[:]).then_inc(s_fill, 16)
            sp.dma_start(score_rows.rearrange("e (b t) -> e b t", t=TD)[:, :, T:TD],
                         zero[0:E8, 0:B * (TD - T)].rearrange("e (b t) -> e b t", b=B)).then_inc(s_fill, 16)

            def store_rows(s, it):
                first = (it * 2 + s) * (2 * TD)
                seam = T - ROWT
                sp.wait_ge(s_sce[s], it + 2)
                sp.sem_inc(s_turn, 1)
                sp.dma_start(score_rows[:, bass.ds(first, 2 * TD)].rearrange("e (s t) -> e s t", s=2)[:, :, 0:T],
                             scs[s][:].rearrange("e (s t) -> e s t", s=2)).then_inc(s_out[s], 16)
                sp.wait_ge(s_tre[s], it * 3 + 6)
                sp.sem_inc(s_turn, 1)
                for m, dst in enumerate((z_rows, acc_rows)):
                    for j, p0, n, row in ((0, 0, ROWT, 0), (1, 0, seam, ROWT), (1, seam, ROWT - seam, TD), (2, 0, ROWT, TD + ROWT - seam)):
                        sp.dma_start(dst[bass.ds(first + row, n), :], rows[s][p0:p0 + n, j, m, :]).then_inc(s_out[s], 16)

            with sp.Fori(0, TURNS - 1) as it:
                for s in range(2):
                    sp.wait_ge(s_hot[s], it + 1)
                    sp.sem_inc(s_turn, 1)
                    sp.wait_ge(s_emb[s], it + 1)
                    sp.sem_inc(s_turn, 1)
                    load_pair(it * 2 + (2 + s), s)
                    store_rows(s, it)
            for s in range(2):
                store_rows(s, TURNS - 1)
            sp.wait_ge(s_fill, 48)
            for s in range(2):
                sp.wait_ge(s_out[s], 1 + OUTS * (PAIRS // 2))
                sp.wait_ge(s_in[s], 32 * (PAIRS // 2))

        @block.gpsimd
        def _(pool):
            V = nc.gpsimd
            V.memset(mean_w[:], 1.0 / C).then_inc(s_const, 1)
            for n, v in enumerate((EPS, EPS * EPS, 1.0)):
                V.memset(epsc[:, n:n + 1], v).then_inc(s_const, 1)
            V.memset(zero[:], 0.0).then_inc(s_const, 1)
            for s in range(2):
                pool.sem_inc(s_out[s], 1)
            with pool.Fori(0, PAIRS // 2) as it:
                for s in range(2):
                    for f in range(FT):
                        pool.wait_ge(s_relu[s], it * FT + (f + 1))
                        V.tensor_tensor(hidden(s, f), hidden(s, f), hidden(s, f), ALU.mult).then_inc(s_kk2[s], 1)

        @block.tensor
        def _(pe):
            V = nc.tensor
            pe.wait_ge(s_ld2, 48)
            for f in range(NFREQ):
                last = V.matmul(ps[0][0:VOCAB, 0, 0:C], emb[:, f, :], wtxt[:, f, :], start=f == 0, stop=f == NFREQ - 1)
            last.then_inc(s_tabp, 1)
            pe.wait_ge(s_ld, 16 * 12)
            pe.wait_ge(s_tab, 1)
            pe.wait_ge(s_const, 4)

            def sums(s, b, x, done, compact):
                for c in range(CT):
                    last = V.matmul(ps[s][:, b, 0:NP], mean_w[:], (compc if compact else realc)(x, c),
                                    start=c == 0, stop=c == CT - 1)
                last.then_inc(done, 1)

            def project(s, b, w, x, done):
                for m in range(CT):
                    for c in range(CT):
                        last = V.matmul(ps[s][:, b + m, 0:NP], w[:, c, m * 128:(m + 1) * 128], compc(x, c),
                                        start=c == 0, stop=c == CT - 1)
                last.then_inc(done, 1)

            def embed(s, it):
                pe.wait_ge(s_hot[s], it + 1)
                pe.wait_ge(s_in[s], it * 32 + 32)
                pe.wait_ge(s_tre[s], it * 3 + 1)
                pe.wait_ge(s_sce[s], it + 1)
                for m in range(CT):
                    V.matmul(ps[s][:, m, 0:NP], table[:, m * 128:(m + 1) * 128], hot[s][:].rearrange("p s t -> p (s t)"),
                             start=True, stop=False)
                    out = ps[s][:, m, 0:NP].rearrange("p (s t) -> p s t", s=2)[:, :, 1:1 + NIMG]
                    for k in range(PK):
                        last = V.matmul(out, wtok[:, k, m * 128:(m + 1) * 128],
                                        patch[s][:, k, :].rearrange("p (s t) -> p s t", s=2),
                                        start=False, stop=k == PK - 1)
                last.then_inc(s_emb[s], 1)

            def mean0(s, it):
                pe.wait_ge(s_h0[s], it + 1)
                pe.wait_ge(s_tre[s], it * 3 + 2)
                sums(s, 2, tl[s]["h0"], s_mean[s], False)

            def var0(s, it):
                pe.wait_ge(s_sq[s], it * 3 + 1)
                pe.wait_ge(s_tre[s], it * 3 + 3)
                sums(s, 3, tl[s]["sq"], s_var[s], True)

            def key(s, it):
                pe.wait_ge(s_mix[s], it * 5 + 1)
                project(s, 0, wtk, tl[s]["m0"], s_proj[s])

            def value(s, it):
                pe.wait_ge(s_mix[s], it * 5 + 2)
                project(s, 2, wtv, tl[s]["m1"], s_proj[s])

            def receptance(s, it):
                pe.wait_ge(s_mix[s], it * 5 + 3)
                pe.wait_ge(s_pev[s], it * 4 + 1)
                project(s, 0, wtr, tl[s]["m2"], s_proj[s])

            def mean1(s, it):
                pe.wait_ge(s_x1[s], it + 1)
                sums(s, 2, tl[s]["xa"], s_mean[s], True)

            def var1(s, it):
                pe.wait_ge(s_sq[s], it * 3 + 2)
                sums(s, 3, tl[s]["sq"], s_var[s], True)

            def channel_receptance(s, it):
                pe.wait_ge(s_mix[s], it * 5 + 4)
                project(s, 0, wcr, tl[s]["m1"], s_proj[s])

            def ffn(f):
                def up(s, it, f):
                    if f == 0:
                        pe.wait_ge(s_mix[s], it * 5 + 5)
                    if f >= 2:
                        pe.wait_ge(s_relu[s], it * FT + (f - 1))
                    for c in range(CT):
                        last = V.matmul(ps[s][:, 2 + f % 2, 0:NP], wck[:, c, f * 128:(f + 1) * 128],
                                        compc(tl[s]["m0"], c), start=c == 0, stop=c == CT - 1)
                    last.then_inc(s_ck[s], 1)

                def down(s, it, f):
                    if f == 0:
                        pe.wait_ge(s_pev[s], it * 4 + 4)
                    pe.wait_ge(s_kk2[s], it * FT + (f + 1))
                    for m in range(CT):
                        last = V.matmul(ps[s][:, m, 0:NP], wcv[:, f, m * 128:(m + 1) * 128], hidden(s, f),
                                        start=f == 0, stop=f == FT - 1)
                    if f == FT - 1:
                        last.then_inc(s_cv[s], 1)

                def step(s, it):
                    if f < FT:
                        up(s, it, f)
                    if f >= 3:
                        down(s, it, f - 3)

                return step

            def mean2(s, it):
                pe.wait_ge(s_h1[s], it + 1)
                sums(s, 2, tl[s]["xa"], s_mean[s], True)

            def var2(s, it):
                pe.wait_ge(s_sq[s], it * 3 + 3)
                sums(s, 3, tl[s]["sq"], s_var[s], True)

            def score(s, it):
                pe.wait_ge(s_xf[s], it + 1)
                for c in range(CT):
                    last = V.matmul(ps[s][0:E8, 0, 0:NP], wgate[:, c, :], compc(tl[s]["m0"], c), start=c == 0, stop=c == CT - 1)
                last.then_inc(s_scm[s], 1)

            def to_rows(s, it):
                pe.wait_ge(s_hx[s], it + 1)
                for j in range(RT):
                    for m, x in enumerate((tl[s]["m1"], tl[s]["m2"])):
                        for c in range(CT):
                            src = comp(x)[:, c, :, :].rearrange("p s t -> p (s t)")[:, j * ROWT:(j + 1) * ROWT]
                            last = V.transpose(ps[s][0:ROWT, 1 + j, m * C + c * 128:m * C + (c + 1) * 128], src, ident[:])
                    last.then_inc(s_tr[s], 1)

            stages = {"emb": embed, "mean0": mean0, "var0": var0, "k": key, "v": value, "r": receptance, "MEAN1": mean1, "VAR1": var1,
                      "CR": channel_receptance, "MEAN2": mean2, "VAR2": var2, "SCORE": score, "ROWS": to_rows}
            for f in range(FT + 3):
                stages[f"F{f}"] = ffn(f)
            schedule(pe, stages)

        @block.scalar
        def _(act):
            V = nc.scalar
            one_act_table(nc)
            act.wait_ge(s_tabp, 1)
            V.activation(table[0:VOCAB, :], ps[0][0:VOCAB, 0, 0:C], ACT.Copy).then_inc(s_tab, 1)
            act.wait_ge(s_const, 4)
            act.wait_ge(s_ld, 16 * 12)
            for s in range(2):
                act.sem_inc(s_sce[s], 1)
                act.sem_inc(s_tre[s], 3)
            CHAIN = 9
            RSTD, RGATE, RSTD1, CGATE, RSTD2 = 0, 2, 4, 5, 7

            def link(s, it, n):
                act.wait_ge(s_a[s], it * CHAIN + n)

            def sqr(k):
                def stage(s, it):
                    act.wait_ge(s_xc[s], it * 3 + (k + 1))
                    V.activation(tl[s]["sq"][:, 0:WC], tl[s]["xc"][:, 0:WC], ACT.Square).then_inc(s_sq[s], 1)
                return stage

            def rstd(k, first):
                m = 1 if k == 1 else 2

                def stage(s, it):
                    act.wait_ge(s_var[s], it * 3 + (k + 1))
                    V.activation(half[s][:, 0, :], ps[s][:, 3, 0:NP], ACT.Ln, bias=epsc[:, 0:1]).then_inc(s_a[s], 1)
                    if m == 2:
                        V.activation(half[s][:, 1, :], ps[s][:, 3, 0:NP], ACT.Ln, bias=epsc[:, 1:2], scale=1.0 + EPS).then_inc(s_a[s], 1)
                    link(s, it, first + m)
                    V.activation(half[s][:, 0:m, :], half[s][:, 0:m, :], ACT.Exp, scale=-0.5).then_inc(s_rs[s], 1)
                return stage

            def affine(src, g, b, k):
                def stage(s, it):
                    act.wait_ge(s_hc[s], it * 2 + (k + 1))
                    for c in range(CT):
                        last = V.activation(realc(tl[s]["hh"], c), compc(tl[s][src], c), ACT.Identity, bias=vec(b, c), scale=vec(g, c))
                    last.then_inc(s_h[s], 1)
                return stage

            def k_evac(s, it):
                act.wait_ge(s_proj[s], it * 4 + 1)
                V.activation(real(tl[s]["kk"]), bank2(s, 0), ACT.Copy).then_inc(s_pev[s], 1)

            def v_evac(s, it):
                act.wait_ge(s_proj[s], it * 4 + 2)
                V.activation(comp(tl[s]["vv"]), bank2(s, 2), ACT.Copy).then_inc(s_pev[s], 1)

            def alpha_beta(s, it):
                act.wait_ge(s_t1[s], it + 1)
                V.activation(real(tl[s]["al"]), comp(scratch(s, 0)), ACT.Exp)
                V.activation(real(tl[s]["be"]), comp(scratch(s, 1)), ACT.Exp, scale=-1.0).then_inc(s_ab[s], 1)

            def log_p(s, it):
                act.wait_ge(s_pp[s], it + 1)
                V.activation(comp(scratch(s, 0)), prev(tl[s]["pp"]), ACT.Ln).then_inc(s_lp[s], 1)

            def softplus(s, it, x, y, first, done):
                V.activation(tl[s][y][:, 0:WC], tl[s][x][:, 0:WC], ACT.Abs).then_inc(s_a[s], 1)
                link(s, it, first + 1)
                V.activation(tl[s][y][:, 0:WC], tl[s][y][:, 0:WC], ACT.Exp, scale=-1.0).then_inc(s_a[s], 1)
                link(s, it, first + 2)
                V.activation(tl[s][y][:, 0:WC], tl[s][y][:, 0:WC], ACT.Ln, bias=epsc[:, 2:3]).then_inc(done, 1)

            def r_evac(s, it):
                act.wait_ge(s_proj[s], it * 4 + 3)
                V.activation(comp(tl[s]["m2"]), bank2(s, 0), ACT.Copy).then_inc(s_pev[s], 1)
                act.wait_ge(s_pev[s], it * 4 + 3)
                softplus(s, it, "m2", "m0", RGATE, s_sg[s])

            def cr_evac(s, it):
                act.wait_ge(s_proj[s], it * 4 + 4)
                V.activation(comp(tl[s]["m2"]), bank2(s, 0), ACT.Copy).then_inc(s_pev[s], 1)
                act.wait_ge(s_pev[s], it * 4 + 4)
                softplus(s, it, "m2", "aa", CGATE, s_cg[s])

            def exponents(s, it):
                act.wait_ge(s_s[s], it + 1)
                V.activation(real(tl[s]["ca"]), comp(scratch(s, 0)), ACT.Exp)
                V.activation(comp(scratch(s, 1)), comp(scratch(s, 1)), ACT.Exp, scale=-1.0)
                V.activation(scratch(s, 2)[:, 0:WC], scratch(s, 2)[:, 0:WC], ACT.Exp)
                V.activation(scratch(s, 3)[:, 0:WC], scratch(s, 3)[:, 0:WC], ACT.Exp, scale=-1.0).then_inc(s_cc[s], 1)

            def log_den(s, it):
                act.wait_ge(s_den[s], it + 1)
                V.activation(scratch(s, 0)[:, 0:WC], scratch(s, 0)[:, 0:WC], ACT.Ln).then_inc(s_lden[s], 1)

            def gate_exp(s, it):
                act.wait_ge(s_gate[s], it + 1)
                V.activation(tl[s]["m0"][:, 0:WC], tl[s]["m0"][:, 0:WC], ACT.Exp).then_inc(s_e12[s], 1)

            def cgate_exp(s, it):
                act.wait_ge(s_cge[s], it + 1)
                V.activation(tl[s]["aa"][:, 0:WC], tl[s]["aa"][:, 0:WC], ACT.Exp).then_inc(s_crm2[s], 1)

            def relu(f):
                def stage(s, it):
                    act.wait_ge(s_ck[s], it * FT + (f + 1))
                    V.activation(hidden(s, f), ps[s][:, 2 + f % 2, 0:NP], ACT.Relu).then_inc(s_relu[s], 1)
                return stage

            def score_evac(s, it):
                act.wait_ge(s_scm[s], it + 1)
                act.wait_ge(s_out[s], it * OUTS + 1)
                V.activation(scs[s][:], ps[s][0:E8, 0, 0:NP], ACT.Copy).then_inc(s_sce[s], 1)

            def rows_evac(s, it):
                for j in range(RT):
                    act.wait_ge(s_tr[s], it * 3 + (j + 1))
                    V.activation(rows[s][:, j, :, :].rearrange("p m c -> p (m c)"), ps[s][0:ROWT, 1 + j, :], ACT.Copy).then_inc(s_tre[s], 1)

            stages = {"mean0": sqr(0), "var0": rstd(0, RSTD), "nrm0": affine("m0", G1, B1, 0), "k": k_evac, "vevac": v_evac,
                      "ab": alpha_beta, "psum": log_p, "revac": r_evac, "cc": exponents, "lden": log_den, "gexp": gate_exp,
                      "MEAN1": sqr(1), "VAR1": rstd(1, RSTD1), "NRM1": affine("m2", G2, B2, 1), "CR": cr_evac, "CGE": cgate_exp,
                      "MEAN2": sqr(2), "VAR2": rstd(2, RSTD2), "SCORE": score_evac, "ROWS": rows_evac}
            for f in range(FT):
                stages[f"F{f}"] = relu(f)
            schedule(act, stages)

        @block.vector
        def _(dve):
            V = nc.vector
            dve.wait_ge(s_ld, 16 * 12)
            for c in range(CT):
                V.tensor_scalar(pos[:, c, 1:1 + NIMG], pos[:, c, 1:1 + NIMG], vec(TOKB, c), None, ALU.add)
                V.tensor_scalar(pos[:, c, 1 + NIMG:T], pos[:, c, 1 + NIMG:T], vec(TXTB, c), None, ALU.add)
            pre = Chain(dve, s_pre)
            pre.then(V.memset(wdec[:], 0.0))
            for c in range(CT):
                pre.then(V.tensor_scalar(wdec[:, c * 2 * TP:(c + 1) * 2 * TP], wdec[:, c * 2 * TP:(c + 1) * 2 * TP],
                                         vec(DECAY, c), None, ALU.add))
            pre.then(V.memset(pads(wdec), NEG))
            for s in range(2):
                V.memset(pads(tl[s]["hh"]), 0.0)
                V.memset(pads(tl[s]["kk"]), NEG)
                V.memset(pads(tl[s]["al"]), 0.0)
                V.memset(pads(tl[s]["be"]), 1.0)
                V.memset(pads(tl[s]["ca"]), 0.0)
                V.memset(pads(tl[s]["cv"]), 0.0)
                pre.then(V.memset(hot[s][:], 0.0))
                pre.then(V.memset(hot[s][VOCAB:VOCAB + 1, :, 0:1], 1.0))
            CHAIN = 14
            DIFF, MAXSCAN, S_SUM, GATE, DEN, STATE, OUT, X1, CDIFF, XH, H1 = 0, 1, 3, 4, 5, 6, 7, 10, 11, 12, 13

            def link(s, it, n, ins):
                ins.then_inc(s_v[s], 1)
                dve.wait_ge(s_v[s], it * CHAIN + n)

            def centre(x, k, compact=True):
                def stage(s, it):
                    dve.wait_ge(s_mean[s], it * 3 + (k + 1))
                    V.tensor_tensor(comp(tl[s]["xc"]), (comp if compact else real)(tl[s][x]), both(ps[s][:, 2, 0:NP]), ALU.subtract).then_inc(s_xc[s], 1)
                    dve.wait_ge(s_xc[s], it * 3 + (k + 1))
                return stage

            def mix(s, out, i, done):
                for c in range(CT):
                    last = V.scalar_tensor_tensor(compc(out, c), compc(tl[s]["dd"], c), vec(i, c), prevc(tl[s]["hh"], c), ALU.mult, ALU.add)
                last.then_inc(done, 1)

            def onehot(s, it):
                dve.wait_ge(s_in[s], it * 32 + 32)
                V.tensor_scalar(hot[s][0:VOCAB, :, 1 + NIMG:T], ids[s][:], rowid[:, 0:1], None, ALU.is_equal).then_inc(s_hot[s], 1)

            def h0_ready(s, it):
                dve.wait_ge(s_emb[s], it + 1)
                V.tensor_tensor(real(tl[s]["h0"]), bank2(s, 0), pos[:].unsqueeze(2).broadcast_to([128, CT, 2, T]), ALU.add).then_inc(s_h0[s], 1)
                dve.wait_ge(s_h0[s], it + 1)

            def norm0(s, it):
                dve.wait_ge(s_rs[s], it * 3 + 1)
                V.tensor_tensor(comp(tl[s]["m0"]), comp(tl[s]["xc"]), both(half[s][:, 1, :]), ALU.mult).then_inc(s_hc[s], 1)
                V.tensor_tensor(comp(tl[s]["xa"]), comp(tl[s]["xc"]), both(half[s][:, 0, :]), ALU.mult)

            def mixes(s, it):
                dve.wait_ge(s_h[s], it * 2 + 1)
                link(s, it, DIFF + 1, V.tensor_tensor(comp(tl[s]["dd"]), real(tl[s]["hh"]), prev(tl[s]["hh"]), ALU.subtract))
                mix(s, tl[s]["m0"], MK, s_mix[s])
                mix(s, tl[s]["m1"], MV, s_mix[s])
                mix(s, tl[s]["m2"], MR, s_mix[s])

            def maxscan(s, it):
                dve.wait_ge(s_pev[s], it * 4 + 1)
                link(s, it, MAXSCAN + 1, V.tensor_tensor_scan(tl[s]["mm"][:], tl[s]["kk"][:], wdec[:], NEG, ALU.max, ALU.add))
                link(s, it, MAXSCAN + 2, V.tensor_tensor(comp(tl[s]["dd"]), prev(tl[s]["mm"]), real(tl[s]["kk"]), ALU.subtract))
                V.tensor_scalar(scratch(s, 0)[:, 0:WC], tl[s]["dd"][:, 0:WC], 0.0, None, ALU.min)
                V.tensor_scalar(scratch(s, 1)[:, 0:WC], tl[s]["dd"][:, 0:WC], 0.0, None, ALU.max).then_inc(s_t1[s], 1)

            def weight_sum(s, it):
                dve.wait_ge(s_ab[s], it + 1)
                V.tensor_tensor_scan(tl[s]["pp"][:], tl[s]["al"][:], tl[s]["be"][:], 1.0, ALU.mult, ALU.add).then_inc(s_pp[s], 1)

            def s_sum(s, it):
                dve.wait_ge(s_lp[s], it + 1)
                link(s, it, S_SUM + 1, V.tensor_tensor(tl[s]["dd"][:, 0:WC], tl[s]["dd"][:, 0:WC], scratch(s, 0)[:, 0:WC], ALU.add))
                V.tensor_scalar(scratch(s, 0)[:, 0:WC], tl[s]["dd"][:, 0:WC], 0.0, None, ALU.min)
                V.tensor_scalar(scratch(s, 1)[:, 0:WC], tl[s]["dd"][:, 0:WC], 0.0, None, ALU.max)
                for c in range(CT):
                    V.tensor_scalar(compc(scratch(s, 2), c), compc(tl[s]["dd"], c), vec(FIRST, c), 0.0, ALU.subtract, ALU.min)
                    last = V.tensor_scalar(compc(scratch(s, 3), c), compc(tl[s]["dd"], c), vec(FIRST, c), 0.0, ALU.subtract, ALU.max)
                last.then_inc(s_s[s], 1)

            def gate_log(s, it):
                dve.wait_ge(s_sg[s], it + 1)
                link(s, it, GATE + 1, V.scalar_tensor_tensor(tl[s]["m2"][:, 0:WC], tl[s]["m2"][:, 0:WC], 0.0, tl[s]["m0"][:, 0:WC], ALU.min, ALU.subtract))

            def denominator(s, it):
                dve.wait_ge(s_cc[s], it + 1)
                link(s, it, DEN + 1, V.tensor_tensor(scratch(s, 0)[:, 0:WC], scratch(s, 2)[:, 0:WC], scratch(s, 3)[:, 0:WC], ALU.add))
                dve.sem_inc(s_den[s], 1)

            def state(s, it):
                dve.wait_ge(s_pev[s], it * 4 + 2)
                link(s, it, STATE + 1, V.tensor_tensor(real(tl[s]["cv"]), comp(scratch(s, 1)), comp(tl[s]["vv"]), ALU.mult))
                V.tensor_tensor_scan(tl[s]["aa"][:], tl[s]["ca"][:], tl[s]["cv"][:], 0.0, ALU.mult, ALU.add)

            def gate(s, it):
                dve.wait_ge(s_lden[s], it + 1)
                V.tensor_tensor(tl[s]["m0"][:, 0:WC], tl[s]["m2"][:, 0:WC], scratch(s, 0)[:, 0:WC], ALU.subtract).then_inc(s_gate[s], 1)

            def numerator(s, it):
                link(s, it, OUT + 1, V.tensor_tensor(comp(tl[s]["m1"]), comp(scratch(s, 3)), comp(tl[s]["vv"]), ALU.mult))
                link(s, it, OUT + 2, V.tensor_tensor(comp(tl[s]["dd"]), comp(scratch(s, 2)), prev(tl[s]["aa"]), ALU.mult))
                link(s, it, OUT + 3, V.tensor_tensor(tl[s]["m1"][:, 0:WC], tl[s]["m1"][:, 0:WC], tl[s]["dd"][:, 0:WC], ALU.add))

            def x1_ready(s, it):
                dve.wait_ge(s_e12[s], it + 1)
                link(s, it, X1 + 1, V.tensor_tensor(tl[s]["m1"][:, 0:WC], tl[s]["m1"][:, 0:WC], tl[s]["m0"][:, 0:WC], ALU.mult))
                V.tensor_tensor(tl[s]["xa"][:, 0:WC], tl[s]["xa"][:, 0:WC], tl[s]["m1"][:, 0:WC], ALU.add).then_inc(s_x1[s], 1)
                dve.wait_ge(s_x1[s], it + 1)

            def norm1(s, it):
                dve.wait_ge(s_rs[s], it * 3 + 2)
                V.tensor_tensor(comp(tl[s]["m2"]), comp(tl[s]["xc"]), both(half[s][:, 0, :]), ALU.mult).then_inc(s_hc[s], 1)

            def channel_mixes(s, it):
                dve.wait_ge(s_h[s], it * 2 + 2)
                link(s, it, CDIFF + 1, V.tensor_tensor(comp(tl[s]["dd"]), real(tl[s]["hh"]), prev(tl[s]["hh"]), ALU.subtract))
                mix(s, tl[s]["m1"], CR, s_mix[s])
                mix(s, tl[s]["m0"], CK, s_mix[s])

            def cgate(s, it):
                dve.wait_ge(s_cg[s], it + 1)
                V.scalar_tensor_tensor(tl[s]["aa"][:, 0:WC], tl[s]["m2"][:, 0:WC], 0.0, tl[s]["aa"][:, 0:WC], ALU.min, ALU.subtract).then_inc(s_cge[s], 1)

            def add_h0(s, it):
                V.tensor_tensor(comp(tl[s]["xa"]), comp(tl[s]["xa"]), real(tl[s]["h0"]), ALU.add).then_inc(s_v[s], 1)

            def h1_ready(s, it):
                dve.wait_ge(s_cv[s], it + 1)
                dve.wait_ge(s_crm2[s], it + 1)
                link(s, it, H1 + 1, V.tensor_tensor(comp(tl[s]["m2"]), bank2(s, 0), comp(tl[s]["aa"]), ALU.mult))
                V.tensor_tensor(tl[s]["xa"][:, 0:WC], tl[s]["m2"][:, 0:WC], tl[s]["xa"][:, 0:WC], ALU.add).then_inc(s_h1[s], 1)
                dve.wait_ge(s_h1[s], it + 1)

            def z_ready(s, it):
                dve.wait_ge(s_rs[s], it * 3 + 3)
                V.tensor_tensor(comp(tl[s]["m0"]), comp(tl[s]["xc"]), both(half[s][:, 0, :]), ALU.mult).then_inc(s_xf[s], 1)
                V.tensor_tensor(comp(tl[s]["m1"]), comp(tl[s]["xc"]), both(half[s][:, 1, :]), ALU.mult)
                dve.wait_ge(s_xf[s], it + 1)
                V.tensor_tensor(comp(tl[s]["m2"]), comp(tl[s]["xa"]), comp(tl[s]["m0"]), ALU.add).then_inc(s_hx[s], 1)
                dve.wait_ge(s_hx[s], it + 1)

            schedule(dve, {
                "hot": onehot, "emb": h0_ready, "mean0": centre("h0", 0, False), "nrm0": norm0, "mix": mixes, "maxscan": maxscan,
                "psum": weight_sum, "s": s_sum, "gsp": gate_log, "den": denominator, "state": state, "gate": gate, "num": numerator, "x1": x1_ready, "MEAN1": centre("xa", 1),
                "NRM1": norm1, "CMIX": channel_mixes, "CGE": cgate, "XH": add_h0, "H1": h1_ready, "MEAN2": centre("xa", 2), "Z": z_ready})
    nc.all_engine_barrier()
    nc.clear_and_free_semaphores(sems)
    nc.all_engine_barrier()


u32 = mybir.dt.uint32
SP_P, SP_C = 128, NROW // 128
JT = K_TOP // ROWT
GT = JT // RT
ROUNDS = 13


def phase_experts(nc, A, s_turn, z_rows, acc_rows, score_rows):
    ctx = ExitStack()
    with ctx:
        def sb(name, shape, dt=fp32):
            return ctx.enter_context(nc.sbuf_tensor("e_" + name, shape, dt))

        def sem(name):
            return ctx.enter_context(nc.semaphore("e_" + name))

        score = sb("score", [SP_P, E8, SP_C])
        thr, step = sb("thr", [SP_P, E8]), sb("step", [SP_P, E8])
        mult3 = sb("mult3", [SP_P, 3, E8])
        step3, cand3, cnt3 = (sb(n, [SP_P, 3, E8]) for n in ("step3", "cand3", "cnt3"))
        met, nmet = sb("met", [SP_P, 3, E8]), sb("nmet", [SP_P, E8])
        flag3 = sb("flag3", [SP_P, 3, E8, SP_C])
        flag = sb("flag", [SP_P, E8, SP_C])
        eq = sb("eq", [SP_P, E8, SP_C])
        rank = sb("rank", [SP_P, E8, SP_C])
        cnt, upd, need = sb("cnt", [SP_P, E8]), sb("upd", [SP_P, E8]), sb("need", [SP_P, E8])
        carry = sb("carry", [SP_P, E8, SP_C])
        ones, tri = sb("ones", [SP_P, SP_P]), sb("tri", [SP_P, SP_P])
        ge = sb("ge", [SP_P, E8 * SP_C, JT + 1])
        tile1 = sb("tile1", [SP_P, E8 * SP_C, JT])
        parts = sb("parts", [SP_P, E8 * SP_C, 5, JT], bf16)
        sp3 = sb("sp3", [SP_P, 3, E8, SP_C], bf16)
        rest = sb("rest", [SP_P, 2, E8, SP_C])
        limit = sb("limit", [SP_P, SP_C])
        tokp, tokc = sb("tokp", [SP_P, 1]), sb("tokc", [SP_P, SP_C])
        lo = sb("lo", [SP_P, E8, SP_C])
        lane = sb("lane", [SP_P, ROWT])
        hotlo = [sb(f"hotlo{s}", [SP_P, SP_C, ROWT], bf16) for s in range(2)]
        found = sb("found", [ROWT, E8, 5, JT])
        idxf = sb("idxf", [ROWT, E8, JT])
        idx = sb("idx", [ROWT, E8, JT], u32)
        kept = sb("kept", [ROWT, E8, JT])

        lnv = sb("lnv", [128, 2, CT])
        w1 = [sb(f"w1{s}", [128, CT * F1 + FT]) for s in range(2)]
        w2 = [sb(f"w2{s}", [128, FT, C]) for s in range(2)]
        b2 = [sb(f"b2{s}", [1, C]) for s in range(2)]
        one_row = sb("one_row", [1, ROWT])
        eye = sb("eye", [128, 128])
        cidx = [sb(f"cidx{s}", [ROWT, JT], u32) for s in range(2)]
        ckept = [sb(f"ckept{s}", [ROWT, JT]) for s in range(2)]
        gz = [sb(f"gz{s}", [ROWT, JT, C]) for s in range(2)]
        yt = [sb(f"yt{s}", [128, CT, K_TOP]) for s in range(2)]
        hid = [sb(f"hid{g}", [128, FT, NP]) for g in range(GT)]
        oo = [sb(f"oo{s}", [ROWT, JT, C]) for s in range(2)]
        pt = ctx.enter_context(nc.psum_tensor("e_pt", [128, 2, 512], fp32))
        pu = ctx.enter_context(nc.psum_tensor("e_pu", [128, 3, 512], fp32))
        pd = ctx.enter_context(nc.psum_tensor("e_pd", [128, 3, 512], fp32))

        s_ld, s_v, s_cnt, s_sum = sem("loads"), sem("dve_chain"), sem("counted"), sem("summed")
        s_tanh, s_hl, s_fd = sem("tanh"), sem("onehots"), sem("found")
        s_w = [sem(f"weights{s}") for s in range(2)]
        s_ci, s_g, s_tr, s_yt = sem("indices"), [sem(f"gathered{s}") for s in range(2)], sem("transposed"), sem("y_ready")
        s_up, s_hid, s_dn, s_oo, s_sc = sem("up_done"), sem("hidden_ready"), sem("down_done"), sem("out_ready"), sem("scattered")
        s_cst, s_fin = sem("consts"), sem("lists_ready")
        block = ctx.enter_context(nc.Block())
        LOADS = 7

        @block.sync
        def _(sp):
            sp.dma_start(score[:], score_rows.rearrange("e (p c) -> p e c", c=SP_C)).then_inc(s_ld, 16)
            sp.dma_start(tri[:], A["tri"]).then_inc(s_ld, 16)
            sp.dma_start(limit[:], A["limit"]).then_inc(s_ld, 16)
            sp.dma_start(tokp[:], A["tokp"]).then_inc(s_ld, 16)
            sp.dma_start(tokc[:], A["iota"][0:1, 0:SP_C].broadcast_to([SP_P, SP_C])).then_inc(s_ld, 16)
            sp.dma_start(lane[:], A["iota"][0:1, 0:ROWT].broadcast_to([SP_P, ROWT])).then_inc(s_ld, 16)
            sp.dma_start(eye[:], A["ident"]).then_inc(s_ld, 16)
            sp.dma_start(lnv[:], A["ffn_ln"]).then_inc(s_cst, 16)

            def load_expert(e, s):
                sp.dma_start(w1[s][:], A["w1"][bass.ds(e, 1)].rearrange("a p n -> (a p) n")).then_inc(s_w[s], 16)
                sp.dma_start(w2[s][:], A["w2"][bass.ds(e, 1)].rearrange("a p f n -> (a p) f n")).then_inc(s_w[s], 16)
                sp.dma_start(b2[s][:], A["b2"][bass.ds(e, 1), :]).then_inc(s_w[s], 16)

            for s in range(2):
                load_expert(s, s)
            with sp.Fori(0, E8 // 2 - 1) as it:
                for s in range(2):
                    sp.wait_ge(s_dn, it * 12 + (6 * s + 6))
                    sp.sem_inc(s_turn, 1)
                    sp.wait_ge(s_hid, it * 32 + (16 * s + 16))
                    sp.sem_inc(s_turn, 1)
                    load_expert(it * 2 + (2 + s), s)

        @block.gpsimd
        def _(pool):

            def gather(s, n):
                pool.wait_ge(s_ci, n)
                pool.sem_inc(s_turn, 1)
                for j in range(JT):
                    pool.indirect_dma_start(gz[s][:, j, :], None, z_rows[:, :],
                                            bass.IndirectOffsetOnAxis(ap=cidx[s][:, j:j + 1], axis=0),
                                            bounds_check=NROW - 1).then_inc(s_g[s], 16)

            def scatter(s, n, before):
                pool.wait_ge(s_oo, n * JT)
                if before is not None:
                    pool.wait_ge(s_sc, before)
                pool.sem_inc(s_turn, 1)
                for j in range(JT):
                    pool.indirect_dma_start(acc_rows[:, :], bass.IndirectOffsetOnAxis(ap=cidx[s][:, j:j + 1], axis=0),
                                            oo[s][:, j, :], None, bounds_check=NROW - 1,
                                            compute_op=ALU.add).then_inc(s_sc, 16)

            def pair(it, before):
                gather(1, it * 2 + 2)
                scatter(0, it * 2 + 1, before)
                gather(0, it * 2 + 3)
                scatter(1, it * 2 + 2, it * (32 * JT) + 16 * JT)

            gather(0, 1)
            pair(0, None)
            with pool.Fori(1, E8 // 2 - 1) as it:
                pair(it, it * (32 * JT))
            last = E8 // 2 - 1
            gather(1, E8)
            scatter(0, E8 - 1, last * 32 * JT)
            scatter(1, E8, last * 32 * JT + 16 * JT)
            pool.wait_ge(s_sc, E8 * JT * 16)

        @block.scalar
        def _(act):
            V = nc.scalar
            act.wait_ge(s_ld, 16 * LOADS)
            V.activation(flag[:], score[:], ACT.Tanh).then_inc(s_tanh, 1)
            act.wait_ge(s_cst, 16)

            def norm_affine(s, n0):
                for g in range(GT):
                    act.wait_ge(s_tr, n0 + (g + 1))
                    for c in range(CT):
                        last = V.activation(yt[s][:, c, g * NP:(g + 1) * NP], pt[:, c, 0:NP], ACT.Identity,
                                            scale=lnv[:, 0, c:c + 1], bias=lnv[:, 1, c:c + 1])
                    last.then_inc(s_yt, 1)

            def hidden(s, g, n0):
                for f in range(FT):
                    k = g * FT + f
                    act.wait_ge(s_up, n0 + (k + 1))
                    V.activation(hid[g][:, f, :], pu[:, k % 3, 0:NP], ACT.Gelu_apprx_tanh,
                                 bias=w1[s][:, CT * F1 + f:CT * F1 + f + 1]).then_inc(s_hid, 1)

            def expert(s, it, more):
                for g in range(GT):
                    if g == 0:
                        act.wait_ge(s_w[s], it * 48 + 48)
                    hidden(s, g, it * (4 * FT) + s * 2 * FT)
                if more:
                    norm_affine(1 - s, it * 4 + (2 * s + 2))

            norm_affine(0, 0)
            with act.Fori(0, E8 // 2 - 1) as it:
                for s in range(2):
                    expert(s, it, True)
            for s in range(2):
                expert(s, E8 // 2 - 1, s == 0)

        @block.tensor
        def _(pe):
            V = nc.tensor
            pe.wait_ge(s_ld, 16 * LOADS)
            with pe.Fori(0, ROUNDS) as it:
                pe.wait_ge(s_cnt, it + 1)
                V.matmul(pt[0:SP_P, 0, 0:3 * E8], ones[:], cnt3[:].rearrange("p a e -> p (a e)"), start=True, stop=True).then_inc(s_sum, 1)
            pe.wait_ge(s_cnt, ROUNDS + 1)
            V.matmul(pt[0:SP_P, 0, 0:E8], ones[:], cnt[:], start=True, stop=True).then_inc(s_sum, 1)
            for n in range(2):
                pe.wait_ge(s_cnt, ROUNDS + 2 + n)
                V.matmul(pt[0:SP_P, 0, 0:E8], tri[:], cnt[:], start=True, stop=True).then_inc(s_sum, 1)
            for e in range(E8):
                pe.wait_ge(s_hl, e + 1)
                for c in range(SP_C):
                    last = V.matmul(pt[0:ROWT, 0 if e < 2 else 1, e * 5 * JT:(e + 1) * 5 * JT], hotlo[e % 2][:, c, :],
                                    parts[:, e * SP_C + c, :, :].rearrange("p a b -> p (a b)"),
                                    start=c == 0, stop=c == SP_C - 1)
                last.then_inc(s_fd, 1)
            pe.wait_ge(s_fin, 1)

            def transposes(s, n, yt_before, gathered):
                pe.wait_ge(s_g[s], gathered)
                for g in range(GT):
                    if yt_before is not None or g:
                        pe.wait_ge(s_yt, g if yt_before is None else yt_before + g)
                    for c in range(CT):
                        for j in range(RT):
                            last = V.transpose(pt[:, c, j * ROWT:(j + 1) * ROWT], gz[s][:, g * RT + j, c * 128:(c + 1) * 128],
                                               eye[0:ROWT, 0:ROWT])
                    last.then_inc(s_tr, 1)

            def up(s, g, it, first):
                n0 = it * (4 * FT) + s * 2 * FT
                for f in range(FT):
                    k = g * FT + f
                    if not (first and k < 3):
                        pe.wait_ge(s_hid, n0 + (k - 2))
                    for c in range(CT):
                        last = V.matmul(pu[:, k % 3, 0:NP], w1[s][:, c * F1 + f * 128:c * F1 + (f + 1) * 128],
                                        yt[s][:, c, g * NP:(g + 1) * NP], start=c == 0, stop=c == CT - 1)
                    last.then_inc(s_up, 1)

            def down(s, g, it, first):
                n0 = it * (4 * FT) + s * 2 * FT
                m0 = it * (2 * JT) + s * JT
                pe.wait_ge(s_hid, n0 + (g + 1) * FT)
                for j in range(RT):
                    if not (first and g == 0):
                        pe.wait_ge(s_oo, m0 + (g * RT + j - RT + 1))
                    V.matmul(pd[0:ROWT, j, 0:C], one_row[:], b2[s][:], start=True, stop=False)
                    for f in range(FT):
                        last = V.matmul(pd[0:ROWT, j, 0:C], hid[g][:, f, j * ROWT:(j + 1) * ROWT], w2[s][:, f, :],
                                        start=False, stop=f == FT - 1)
                    last.then_inc(s_dn, 1)

            def expert(s, it, first, more):
                pe.wait_ge(s_w[s], it * 48 + 48)
                n = it * 4 + (2 * s + 1)
                pe.wait_ge(s_yt, n)
                up(s, 0, it, first)
                pe.wait_ge(s_yt, n + 1)
                up(s, 1, it, False)
                down(s, 0, it, first)
                if more:
                    transposes(1 - s, None, it * 4 + (2 * s + 2), (it + s) * (16 * JT) + 16 * JT)
                down(s, 1, it, False)

            transposes(0, 0, None, 16 * JT)
            for s in range(2):
                expert(s, 0, s == 0, True)
            with pe.Fori(1, E8 // 2 - 1) as it:
                for s in range(2):
                    expert(s, it, False, True)
            for s in range(2):
                expert(s, E8 // 2 - 1, False, s == 0)

        @block.vector
        def _(dve):
            V = nc.vector
            V.memset(ones[:], 1.0)
            V.memset(one_row[:], 1.0)
            pre = Chain(dve, s_v)
            pre.then(V.memset(carry[:], 1.0))
            pre.mark(V.memset(thr[:], 0.0))
            pre.mark(V.memset(step[:], 0.5))
            pre.then(V.memset(carry[:, :, 0:1], 0.0))

            dve.wait_ge(s_ld, 16 * LOADS)
            dve.wait_ge(s_tanh, 1)
            pre.then(V.tensor_scalar(score[:], flag[:], 1.0, 0.5, ALU.add, ALU.mult))
            pre.then(V.tensor_tensor(score[:], score[:], limit[:].unsqueeze(1).broadcast_to([SP_P, E8, SP_C]), ALU.min))

            def over(x):
                return x.unsqueeze(2).broadcast_to([SP_P, E8, SP_C])

            def thrice(x):
                return x.unsqueeze(1).broadcast_to([SP_P, 3, E8])

            for n in range(3):
                last = V.memset(mult3[:, n, :], n + 1.0)
            pre.then(last)
            CHAIN = 6
            with dve.Fori(0, ROUNDS) as it:
                ch = Chain(dve, s_v, CHAIN, it, base=pre.n)
                ch.then(V.tensor_tensor(step3[:], mult3[:], thrice(step[:]), ALU.mult))
                ch.then(V.tensor_tensor(cand3[:], step3[:], thrice(thr[:]), ALU.add))
                ch.then(V.tensor_tensor(flag3[:], score[:].unsqueeze(1).broadcast_to([SP_P, 3, E8, SP_C]),
                                        cand3[:].unsqueeze(3).broadcast_to([SP_P, 3, E8, SP_C]), ALU.is_ge))
                V.tensor_reduce(cnt3[:], flag3[:], AX.X, ALU.add).then_inc(s_cnt, 1)
                dve.wait_ge(s_sum, it + 1)
                ch.then(V.scalar_tensor_tensor(met[:], pt[0:SP_P, 0, 0:3 * E8].rearrange("p (a e) -> p a e", a=3), float(K_TOP),
                                               thrice(step[:]), ALU.is_ge, ALU.mult))
                V.tensor_scalar(step[:], step[:], 0.25, None, ALU.mult)
                ch.then(V.tensor_reduce(nmet[:], met[:].rearrange("p a e -> p e a"), AX.X, ALU.add))
                ch.then(V.tensor_tensor(thr[:], thr[:], nmet[:], ALU.add))
                assert ch.n == CHAIN
            po = Chain(dve, s_v, base=pre.n + CHAIN * ROUNDS)
            po.then(V.tensor_tensor(flag[:], score[:], over(thr[:]), ALU.is_gt))
            V.tensor_reduce(cnt[:], flag[:], AX.X, ALU.add).then_inc(s_cnt, 1)
            V.tensor_tensor(eq[:], score[:], over(thr[:]), ALU.is_equal)
            dve.wait_ge(s_sum, ROUNDS + 1)
            po.then(V.tensor_scalar(need[:], pt[0:SP_P, 0, 0:E8], -1.0, float(K_TOP), ALU.mult, ALU.add))

            def flat(x):
                return x.rearrange("p e c -> p (e c)")

            def ranks(x, n):
                po.then(V.tensor_tensor_scan(flat(rank[:]), flat(carry[:]), flat(x[:]), 0.0, ALU.mult, ALU.add))
                V.tensor_copy(cnt[:].unsqueeze(2), rank[:, :, SP_C - 1:SP_C]).then_inc(s_cnt, 1)
                dve.wait_ge(s_sum, n)
                po.then(V.tensor_copy(upd[:], pt[0:SP_P, 0, 0:E8]))
                po.then(V.tensor_tensor(rank[:], rank[:], over(upd[:]), ALU.add))

            ranks(eq, ROUNDS + 2)
            po.then(V.tensor_tensor(rank[:], rank[:], over(need[:]), ALU.is_le))
            po.then(V.tensor_tensor(eq[:], eq[:], rank[:], ALU.mult))
            po.then(V.tensor_tensor(flag[:], flag[:], eq[:], ALU.add))
            ranks(flag, ROUNDS + 3)
            po.then(V.tensor_scalar(flag[:], flag[:], -2.0 * NTOK, 2.0 * NTOK - 1.0, ALU.mult, ALU.add))
            po.then(V.tensor_tensor(rank[:], rank[:], flag[:], ALU.add))
            for j in range(JT + 1):
                last = V.tensor_scalar(ge[:, :, j], flat(rank[:]), float(ROWT * j), None, ALU.is_ge)
            po.then(last)
            po.mark(V.tensor_tensor(tile1[:], ge[:, :, 0:JT], ge[:, :, 1:JT + 1], ALU.subtract))
            po.then(V.tensor_reduce(flat(lo[:]), ge[:, :, 1:JT], AX.X, ALU.add))
            po.then(V.scalar_tensor_tensor(lo[:], lo[:], -float(ROWT), rank[:], ALU.mult, ALU.add))
            po.then(V.tensor_copy(sp3[:, 0], score[:]))
            po.then(V.tensor_tensor(rest[:, 0], score[:], sp3[:, 0], ALU.subtract))
            po.then(V.tensor_copy(sp3[:, 1], rest[:, 0]))
            po.then(V.tensor_tensor(rest[:, 1], rest[:, 0], sp3[:, 1], ALU.subtract))
            po.then(V.tensor_copy(sp3[:, 2], rest[:, 1]))
            V.tensor_scalar(parts[:, :, 0, :], tile1[:], tokp[:, 0:1], None, ALU.mult)
            t4 = tile1[:].rearrange("p (e c) j -> p e c j", e=E8)
            p4 = parts[:].rearrange("p (e c) a j -> p e c a j", e=E8)
            for e in range(E8):
                last = V.tensor_tensor(p4[:, e, :, 1, :], t4[:, e, :, :], tokc[:].unsqueeze(2).broadcast_to([SP_P, SP_C, JT]), ALU.mult)
            for n in range(3):
                last = V.tensor_tensor(parts[:, :, 2 + n, :], tile1[:], sp3[:, n].rearrange("p e c -> p (e c)").unsqueeze(2).broadcast_to([SP_P, E8 * SP_C, JT]), ALU.mult)
            po.then(last)
            def take(s, e):
                V.tensor_copy(ckept[s][:], kept[:, bass.ds(e, 1), :].rearrange("p a j -> p (a j)"))
                V.tensor_copy(cidx[s][:], idx[:, bass.ds(e, 1), :].rearrange("p a j -> p (a j)")).then_inc(s_ci, 1)

            def onehot_lane(e):
                if e >= 2:
                    dve.wait_ge(s_fd, e - 1)
                V.tensor_tensor(hotlo[e % 2][:], lo[:, e, :].unsqueeze(2).broadcast_to([SP_P, SP_C, ROWT]),
                                lane[:].unsqueeze(1).broadcast_to([SP_P, SP_C, ROWT]), ALU.is_equal).then_inc(s_hl, 1)

            def lists(a, b):
                dve.wait_ge(s_fd, b)
                po.then(V.tensor_copy(found[:, a:b].rearrange("p e a j -> p (e a j)"), pt[0:ROWT, 0 if b == 2 else 1, a * 5 * JT:b * 5 * JT]))
                po.then(V.scalar_tensor_tensor(idxf[:, a:b], found[:, a:b, 0, :], float(SP_C), found[:, a:b, 1, :], ALU.mult, ALU.add))
                po.then(V.tensor_copy(idx[:, a:b], idxf[:, a:b]))
                po.then(V.tensor_tensor(kept[:, a:b], found[:, a:b, 2, :], found[:, a:b, 3, :], ALU.add))
                po.then(V.tensor_tensor(kept[:, a:b], kept[:, a:b], found[:, a:b, 4, :], ALU.add))

            for e in range(3):
                onehot_lane(e)
            lists(0, 2)
            for s in range(2):
                take(s, s)
            for e in range(3, E8):
                onehot_lane(e)
            lists(2, E8)
            dve.sem_inc(s_fin, 1)

            def weigh(s, it):
                m0 = it * (2 * JT) + s * JT
                for j in range(JT):
                    dve.wait_ge(s_dn, m0 + (j + 1))
                    V.tensor_scalar(oo[s][:, j, :], pd[0:ROWT, j % RT, 0:C], ckept[s][:, j:j + 1], None, ALU.mult).then_inc(s_oo, 1)

            with dve.Fori(0, E8 // 2 - 1) as it:
                for s in range(2):
                    dve.wait_ge(s_ci, it * 2 + (s + 1))
                    weigh(s, it)
                    dve.wait_ge(s_sc, it * (32 * JT) + 16 * JT * (s + 1))
                    take(s, it * 2 + (s + 2))
            dve.wait_ge(s_ci, E8)
            for s in range(2):
                weigh(s, E8 // 2 - 1)

CH = 12
NCH = TD // CH
TT = 4
NT3 = CH // TT
HG, HH, DH = 4, 4, 16
HD = HH * DH


class Turn:

    def __init__(self, off, it=None):
        self.off, self.it = off, it

    def __add__(self, k):
        return Turn(self.off + k, self.it)

    @property
    def par(self):
        return self.off % 2

    def of(self, k, m):
        return self.off * k + m if self.it is None else self.it * (2 * k) + (self.off * k + m)

    def half(self, k, m):
        return self.off // 2 * k + m if self.it is None else self.it * k + (self.off // 2 * k + m)


def wait(eng, sem, v):
    if not isinstance(v, int) or v > 0:
        eng.wait_ge(sem, v)


def phase_delta(nc, A, s_turn, acc_rows, proj_rows, o_rows, out):
    ctx = ExitStack()
    with ctx:
        def sb(name, shape, dt=fp32):
            return ctx.enter_context(nc.sbuf_tensor("d_" + name, shape, dt))

        def sem(name):
            return ctx.enter_context(nc.semaphore("d_" + name))

        def pb(name, shape):
            return ctx.enter_context(nc.psum_tensor("d_" + name, shape, fp32))

        NB = 4 * C + C + E8
        (B_QKVB, B_OUT, B_RT) = (0, 4 * C, 5 * C)
        wqkvb = sb("wqkvb", [128, CT, 4 * C])
        wout = sb("wout", [128, CT, C])
        wrt = sb("wrt", [128, CT, E8])
        wex = sb("wex", [128, CT, E8 * C])
        bias = sb("bias", [3, NB])
        bpart = [sb(f"bpart{n}", [3, NB], bf16) for n in range(3)]
        brow = sb("brow", [3, NB], bf16)
        ones3 = sb("ones3", [3, 128], bf16)
        ident = sb("ident", [128, 128])
        lnp = sb("lnp", [128, 2, CT])
        epsc = sb("epsc", [128, 3])
        rev = sb("rev", [128, E8])

        h2 = [sb(f"h2{p}", [128, NT3, C]) for p in range(2)]
        st1, mv1, st3, mv3 = sb("st1", [128, NT3, 6]), sb("mv1", [128, NT3, 2]), sb("st3", [128, NT3, 6]), sb("mv3", [128, NT3, 2])
        rs1, rs3 = sb("rs1", [128, 2, NT3]), sb("rs3", [128, NT3])
        negh = sb("negh", [128, 2, NT3])
        onep, shift1, shift3 = sb("onep", [128, NT3]), sb("shift1", [128, 2, NT3]), sb("shift3", [128, NT3])
        hn = sb("hn", [128, NT3, C])
        ntile = [sb(f"nt{i}", [128, CT, 128]) for i in range(NT3)]
        pr = [sb(f"pr{i}", [128, 4 * C]) for i in range(NT3)]
        base = [sb(f"base{p}", [128, NT3, C]) for p in range(2)]
        D = [sb(f"qkvb{p}", [128, CH, 4 * HD]) for p in range(2)]
        O = [sb(f"o{p}", [128, CH, HD]) for p in range(2)]
        ksq, bab = sb("ksq", [128, CH, HD]), sb("bab", [128, CH, HD])
        ss, inv = sb("ss", [128, CH * HH]), sb("inv", [128, CH * HH])
        S, mk, ou = (sb(n, [128, HD * DH]) for n in ("state", "mk", "outer"))
        mqp = [sb(f"mqp{n}", [128, 4, HD * DH]) for n in range(2)]
        brest = [mqp[n][0:3].rearrange("p t n -> p (t n)")[:, 0:NB] for n in range(2)]
        rk, u1, u = sb("rk", [128, HD]), sb("u1", [128, HD]), sb("u", [128, HD])
        otm = sb("otm", [128, NT3, C])
        ott = [sb(f"ot{i}", [128, CT, 128]) for i in range(NT3)]
        wo = sb("wo", [128, NT3, C])
        h3 = [sb(f"h3{p}", [128, NT3, C]) for p in range(2)]
        dd = [sb(f"dd{p}", [128, NT3, C]) for p in range(2)]
        eb = sb("eb", [E8, C])
        wt = sb("wt", [E8, NT3, 128])
        dtile = [sb(f"dt{i}", [128, CT, 128]) for i in range(NT3)]
        mx, lgs, ex, sm, rc = sb("mx", [128, NT3]), sb("lgs", [128, NT3, E8]), sb("ex", [128, NT3, E8]), sb("sm", [128, NT3]), sb("rc", [128, NT3])
        mask, mr, wm = sb("mask", [128, NT3, E8]), sb("mr", [128, NT3]), sb("wm", [128, NT3, E8])
        xw = [sb(f"xw{n}", [128, E8, C]) for n in range(2)]
        xt = [sb(f"xt{n}", [128, 2, CT, 128]) for n in range(2)]
        outb = sb("outb", [128, NT3, C])

        pt = [pb(f"pt{n}", [128, 512]) for n in range(2)]
        pj = pb("pj", [128, 1024])
        pf = [pb(f"pf{n}", [128, 512]) for n in range(2)]
        py, po = pb("py", [128, 512]), pb("po", [128, 512])

        s_ld2, s_bld = sem("late_loads"), sem("bias_load")
        s_ld, s_cst, s_bias, s_v, s_a = sem("loads"), sem("consts"), sem("bias_rows"), sem("dve_chain"), sem("act_chain")
        s_h2 = [sem(f"h2_in{p}") for p in range(2)]
        s_dl = [sem(f"qkvb_in{p}") for p in range(2)]
        s_st1, s_rs1, s_hn, s_nb = sem("stats1"), sem("rstd1"), sem("hn_ready"), sem("base_coeffs")
        s_ntt, s_nte, s_pj, s_pre, s_base = sem("nt_done"), sem("nt_evac"), sem("proj_done"), sem("proj_evac"), sem("base_ready")
        s_pst, s_sq, s_sp, s_ss, s_bl, s_inv, s_beta, s_kn = (sem(n) for n in (
            "proj_stored", "k_squares", "softplus", "k_sums", "beta_log", "k_inv", "beta_ready", "k_ready"))
        s_ost, s_otl = sem("o_stored"), sem("o_in")
        s_ott, s_ote, s_wo, s_woe = sem("ot_done"), sem("ot_evac"), sem("wout_done"), sem("wout_evac")
        s_h3, s_st3, s_rs3, s_ddn, s_dtt, s_dte = (sem(n) for n in ("h3_ready", "stats3", "rstd3", "d_ready", "dt_done", "dt_evac"))
        s_lg, s_ls, s_ex, s_wm = sem("logits"), sem("logits_less_max"), sem("exps"), sem("expert_weights")
        s_xw, s_f, s_fe, s_yd, s_oe, s_od = (sem(n) for n in (
            "weighted", "xt_done", "xt_evac", "out_summed", "out_evac", "out_stored"))

        s_red, s_oev = sem("o_reduced"), sem("o_evac")
        s_l1, s_l3, s_lstep, s_lrt, s_lkb, s_st, s_mq, s_pv, s_pv3, s_nd = (sem(n) for n in (
            "stats1_chain", "stats3_chain", "step_chain", "router_chain", "k_chain", "state_ready", "mq_ready", "rstd1_chain", "rstd3_chain", "norm3_ready"))

        OB = 4
        NOB = CH // OB
        assert NOB == 3

        def steps_of(c):
            return T - (NCH - 1) * CH if c.it is None and c.off == NCH - 1 else CH

        BANKS = 1 + NT3 * E8 // 2
        assert BANKS % 2 == 1
        acc_t = acc_rows.rearrange("(b t) c -> t b c", t=TD)
        out_t = out.rearrange("b t c -> t b c")
        block = ctx.enter_context(nc.Block())

        def schedule(eng, body, prologue):
            prologue()
            for c in range(3):
                body(Turn(c), True, True, c >= 1, c >= 2)
            with eng.Fori(0, (NCH - 1 - 3) // 2) as it:
                for k in range(2):
                    body(Turn(3 + k, it), True, True, True, True)
            body(Turn(NCH - 1), False, True, True, True)
            body(Turn(NCH), False, False, True, True)
            body(Turn(NCH + 1), False, False, False, True)

        assert (NCH - 4) % 2 == 0

        @block.sync
        def _(sp):
            sp.dma_start(bias[:], A["b_row"].broadcast_to([3, NB])).then_inc(s_bld, 16)
            sp.dma_start(ident[:], A["ident"]).then_inc(s_ld, 16)
            sp.dma_start(lnp[:], A["l1_ln"]).then_inc(s_ld, 16)

            def load_h2(k):
                wait(sp, s_base, k.of(1, -1))
                sp.sem_inc(s_turn, 1)
                for i in range(NT3):
                    sp.dma_start(h2[k.par][:, i, :], acc_t[bass.ds(k.of(CH, TT * i), TT)]).then_inc(s_h2[k.par], 16)

            def prologue():
                load_h2(Turn(0))
                sp.dma_start(rev[:], A["rev"].broadcast_to([128, E8])).then_inc(s_ld, 16)
                sp.dma_start(wqkvb[:], A["wqkvb"]).then_inc(s_ld, 16)
                sp.dma_start(wout[:], A["L1_attn_w_out"].rearrange("(a p) n -> p a n", p=128)).then_inc(s_ld2, 16)
                sp.dma_start(wrt[:], A["wrt"]).then_inc(s_ld2, 16)
                sp.dma_start(wex[:], A["wex"]).then_inc(s_ld2, 16)
                sp.dma_start(eb[:], A["L1_ffn_expert_b"]).then_inc(s_ld2, 16)
                project_io(Turn(0))

            def project_io(k):
                for i in range(NT3):
                    sp.wait_ge(s_pre, k.of(NT3, i + 1))
                    sp.sem_inc(s_turn, 1)
                    sp.dma_start(proj_rows[bass.ds(k.of(CH, TT * i), TT)].rearrange("t b n -> (t b) n"), pr[i][:]).then_inc(s_pst, 16)
                sp.wait_ge(s_pst, k.of(16 * NT3, 16 * NT3))
                sp.sem_inc(s_turn, 1)
                wait(sp, s_mq, k.of(CH, -CH))
                sp.sem_inc(s_turn, 1)
                for g in range(HG):
                    sp.dma_start(D[k.par][32 * g:32 * g + 32, :, :],
                                 proj_rows[bass.ds(k.of(CH, 0), CH), :, g * 4 * HD:(g + 1) * 4 * HD].rearrange("t b n -> b t n")).then_inc(s_dl[k.par], 16)

            def body(c, prep, delta, post, routed):
                if prep:
                    load_h2(c + 1)
                if post:
                    k = c + (-1)
                    sp.wait_ge(s_ost, k.of(16 * HG, 16 * HG))
                    sp.sem_inc(s_turn, 1)
                    wait(sp, s_ott, k.of(NT3, 0))
                    sp.sem_inc(s_turn, 1)
                    for i in range(NT3):
                        sp.dma_start(otm[:, i, :], o_rows[bass.ds(k.of(CH, TT * i), TT)].rearrange("t b n -> (t b) n")).then_inc(s_otl, 16)
                if prep:
                    project_io(c + 1)
                if delta:
                    sp.wait_ge(s_oev, c.of(2, 2))
                    sp.sem_inc(s_turn, 1)
                    for g in range(HG):
                        sp.dma_start(o_rows[bass.ds(c.of(CH, 0), CH), :, g * HD:(g + 1) * HD].rearrange("t b n -> b t n"),
                                     O[c.par][32 * g:32 * g + 32, :, :]).then_inc(s_ost, 16)

            schedule(sp, body, prologue)
            sp.wait_ge(s_pst, 16 * NT3 * NCH)
            sp.wait_ge(s_ost, 16 * HG * NCH)
            sp.wait_ge(s_od, 16 * NT3 * NCH)

        @block.gpsimd
        def _(pool):
            V = nc.gpsimd
            for n, v in enumerate((EPS, EPS * EPS, 1.0)):
                V.memset(epsc[:, n:n + 1], v).then_inc(s_cst, 1)
            V.memset(ones3[:], 1.0).then_inc(s_cst, 1)
            V.memset(S[:], 0.0).then_inc(s_cst, 1)
            V.memset(negh[:], -0.5).then_inc(s_cst, 1)
            pool.wait_ge(s_cst, 6)

            def rstd1(k):
                pool.wait_ge(s_st1, k.of(1, 1))
                pool.sem_inc(s_turn, 1)
                V.tensor_scalar(rs1[:, 1, :], mv1[:, :, 1], 1.0 + EPS, EPS * EPS, ALU.mult, ALU.add)
                V.tensor_scalar(rs1[:, 0, :], mv1[:, :, 1], EPS, None, ALU.add).then_inc(s_pv, 1)
                pool.wait_ge(s_pv, k.of(2, 1))
                pool.sem_inc(s_turn, 1)
                V.tensor_tensor(rs1[:], rs1[:], negh[:], ALU.pow).then_inc(s_rs1, 1)
                pool.wait_ge(s_rs1, k.of(1, 1))
                wait(pool, s_base, k.of(1, 0))
                pool.sem_inc(s_turn, 1)
                V.tensor_tensor(shift1[:], rs1[:], mv1[:, :, 0].unsqueeze(1).broadcast_to([128, 2, NT3]), ALU.mult)
                V.tensor_scalar(onep[:], rs1[:, 0, :], 1.0, None, ALU.add).then_inc(s_pv, 1)
                pool.wait_ge(s_pv, k.of(2, 2))
                pool.sem_inc(s_turn, 1)
                V.tensor_scalar(shift1[:], shift1[:], -1.0, None, ALU.mult).then_inc(s_nb, 1)

            def body(c, prep, delta, post, routed):
                if prep:
                    rstd1(c + 1)
                if post:
                    k = c + (-1)
                    pool.wait_ge(s_st3, k.of(1, 1))
                    pool.sem_inc(s_turn, 1)
                    V.tensor_scalar(rs3[:], mv3[:, :, 1], EPS, None, ALU.add).then_inc(s_pv3, 1)
                    pool.wait_ge(s_pv3, k.of(2, 1))
                    pool.sem_inc(s_turn, 1)
                    V.tensor_tensor(rs3[:], rs3[:], negh[:, 0, :], ALU.pow).then_inc(s_rs3, 1)
                    pool.wait_ge(s_rs3, k.of(1, 1))
                    pool.sem_inc(s_turn, 1)
                    V.tensor_tensor(shift3[:], rs3[:], mv3[:, :, 0], ALU.mult).then_inc(s_pv3, 1)
                    pool.wait_ge(s_pv3, k.of(2, 2))
                    pool.sem_inc(s_turn, 1)
                    V.tensor_scalar(shift3[:], shift3[:], -1.0, None, ALU.mult).then_inc(s_nd, 1)

            schedule(pool, body, lambda: rstd1(Turn(0)))

        @block.tensor
        def _(pe):
            V = nc.tensor
            pe.wait_ge(s_ld, 16 * 4)
            pe.wait_ge(s_bias, 1)

            def transposes(bank, src, done):
                for c in range(CT):
                    last = V.transpose(bank[:, c * 128:(c + 1) * 128], src[:, c * 128:(c + 1) * 128], ident[:])
                last.then_inc(done, 1)

            def product(out, x, w, b, n):
                V.matmul(out, ones3[:], brow[:, b:b + n], start=True, stop=False)
                for c in range(CT):
                    last = V.matmul(out, x[:, c, :], w[:, c, :], start=False, stop=c == CT - 1)
                return last

            def staggered(turn_tile, multiply_tile):
                turn_tile(0)
                turn_tile(1)
                multiply_tile(0)
                turn_tile(2)
                multiply_tile(1)
                multiply_tile(2)

            def prep_chunk(k, after_post):
                def turn_tile(i):
                    if i < 2:
                        if after_post:
                            pe.wait_ge(s_ote, k.of(NT3, -2 * NT3 + 2 + i))
                        elif k.off > 0 and i == 0:
                            pe.wait_ge(s_nte, k.of(NT3, 0))
                    else:
                        pe.wait_ge(s_nte, k.of(NT3, 1))
                    pe.wait_ge(s_hn, k.of(NT3, i + 1))
                    transposes(pt[(i + 1) % 2], hn[:, i, :], s_ntt)

                def multiply_tile(i):
                    pe.wait_ge(s_nte, k.of(NT3, i + 1))
                    wait(pe, s_pre, k.of(NT3, i))
                    for n in range(2):
                        last = product(pj[:, n * 512:(n + 1) * 512], ntile[i], wqkvb[:, :, n * 512:(n + 1) * 512], B_QKVB + n * 512, 512)
                    last.then_inc(s_pj, 1)

                staggered(turn_tile, multiply_tile)

            def post_a(k):
                pe.wait_ge(s_otl, k.of(16 * NT3, 16 * NT3))

                def turn_tile(i):
                    if i < 2:
                        pe.wait_ge(s_oev, k.of(2, 2))
                        if k.it is None and k.off == 0:
                            pe.wait_ge(s_nte, 2 * NT3)
                        else:
                            pe.wait_ge(s_dte, k.of(NT3, 0))
                    else:
                        pe.wait_ge(s_ote, k.of(NT3, 1))
                    transposes(pt[i % 2], otm[:, i, :], s_ott)

                def multiply_tile(i):
                    pe.wait_ge(s_ote, k.of(NT3, i + 1))
                    wait(pe, s_woe, k.of(NT3, i))
                    if i == 0:
                        wait(pe, s_ls, k.of(1, 0))
                        wait(pe, s_oe, k.of(NT3, -NT3 + 1))
                    product(py[:, 0:C], ott[i], wout, B_OUT, C).then_inc(s_wo, 1)

                staggered(turn_tile, multiply_tile)

            def post_b(k, prep, ahead):
                def turn_tile(i):
                    if i < 2:
                        if prep:
                            pe.wait_ge(s_nte, k.of(NT3, 2 * NT3 + 2 + i))
                        else:
                            pe.wait_ge(s_ote, k.of(NT3, NT3))
                    else:
                        pe.wait_ge(s_dte, k.of(NT3, 1))
                    pe.wait_ge(s_ddn, k.of(NT3, i + 1))
                    transposes(pt[i % 2], dd[k.par][:, i, :], s_dtt)

                def multiply_tile(i):
                    pe.wait_ge(s_dte, k.of(NT3, i + 1))
                    if i == 0:
                        pe.wait_ge(s_woe, k.of(NT3, NT3))
                        wait(pe, s_oe, k.of(NT3, -ahead))
                    return product(py[:, C + i * E8:C + (i + 1) * E8], dtile[i], wrt, B_RT, E8)

                turn_tile(0)
                turn_tile(1)
                multiply_tile(0)
                turn_tile(2)
                multiply_tile(1)
                multiply_tile(2).then_inc(s_lg, 1)

            def weights(k):
                pe.wait_ge(s_wm, k.of(1, 1))
                wait(pe, s_fe, k.of(BANKS, -1))
                for i in range(NT3):
                    last = V.transpose(pf[k.par][0:E8, i * 128:(i + 1) * 128], wm[:, i, :], ident[:])
                last.then_inc(s_f, 1)

            def routed_tile(k, i, post):
                n0 = 1 + i * E8 // 2
                src = xw[(k.par + i) % 2]

                def turn_pair(q):
                    wait(pe, s_fe, k.of(BANKS, n0 + q - 1))
                    for n in range(2 * CT):
                        e, c = 2 * q + n // CT, n % CT
                        last = V.transpose(pf[(k.par + n0 + q) % 2][:, n * 128:(n + 1) * 128], src[:, e, c * 128:(c + 1) * 128], ident[:])
                    last.then_inc(s_f, 1)

                def multiply_pair(q):
                    pe.wait_ge(s_fe, k.of(BANKS, n0 + q + 1))
                    for n in range(2 * CT):
                        e, c = 2 * q + n // CT, n % CT
                        last = V.matmul(py[:, 0:C], xt[q % 2][:, n // CT, c, :], wex[:, c, e * C:(e + 1) * C],
                                        start=False, stop=q == 3 and n == 2 * CT - 1)
                    return last

                pe.wait_ge(s_xw, k.of(NT3, i + 1))
                turn_pair(0)
                turn_pair(1)
                wait(pe, s_oe, k.of(NT3, i))
                if i == 1 and post:
                    pe.wait_ge(s_woe, k.of(NT3, 2 * NT3))
                if i == 2 and post:
                    pe.wait_ge(s_ls, k.of(1, 2))
                V.matmul(py[:, 0:C], ident[:], h3[k.par][:, i, :], start=True, stop=False)
                pe.wait_ge(s_fe, k.of(BANKS, 1))
                V.matmul(py[:, 0:C], wt[:, i, :], eb[:], start=False, stop=False)
                multiply_pair(0)
                turn_pair(2)
                multiply_pair(1)
                turn_pair(3)
                multiply_pair(2)
                multiply_pair(3).then_inc(s_yd, 1)

            def body(c, prep, delta, post, routed):
                if c.it is None and c.off == 1:
                    pe.wait_ge(s_ld2, 16 * 4)
                if routed:
                    pe.wait_ge(s_h3, c.of(1, -1))
                    weights(c + (-2))
                    routed_tile(c + (-2), 0, post)
                if post:
                    post_a(c + (-1))
                if prep:
                    prep_chunk(c + 1, post)
                if delta:
                    reduce_steps(c, 0)
                if routed:
                    routed_tile(c + (-2), 1, post)
                if prep:
                    reduce_steps(c, 1)
                if post and not delta:
                    post_b(c + (-1), prep, 1)
                if routed:
                    routed_tile(c + (-2), 2, post and not delta)
                if post and delta:
                    post_b(c + (-1), prep, 0)
                if delta and not prep:
                    reduce_steps(c, 1)
                if delta:
                    reduce_steps(c, 2)

            def reduce_steps(c, n):
                pe.wait_ge(s_mq, c.of(CH, min(OB * (n + 1), steps_of(c))))
                if n < 2:
                    out = po[:, n * OB * HD:(n + 1) * OB * HD]
                    wait(pe, s_oev, c.of(2, 0))
                else:
                    out = pt[1][:, OB * HD:2 * OB * HD]
                x = mqp[(c.par + n) % 2][:].rearrange("p t (r j) -> p (t r) j", j=DH)
                for j in range(DH):
                    last = V.matmul(out, ident[:], x[:, :, j], start=j == 0, stop=j == DH - 1)
                last.then_inc(s_red, 1)

            schedule(pe, body, lambda: prep_chunk(Turn(0), False))

        @block.scalar
        def _(act):
            V = nc.scalar
            one_act_table(nc)
            act.wait_ge(s_cst, 6)
            act.wait_ge(s_ld, 16 * 4)

            def norm_rows(k):
                act.wait_ge(s_nb, k.of(1, 1))
                for i in range(NT3):
                    V.activation(hn[:, i, :], h2[k.par][:, i, :], ACT.Identity, scale=rs1[:, 1, i:i + 1], bias=shift1[:, 1, i:i + 1]).then_inc(s_hn, 1)

            def norm_d(k):
                act.wait_ge(s_nd, k.of(1, 1))
                for i in range(NT3):
                    V.activation(dd[k.par][:, i, :], h3[k.par][:, i, :], ACT.Identity, scale=rs3[:, i:i + 1], bias=shift3[:, i:i + 1]).then_inc(s_ddn, 1)

            def staggered(first, second):
                first(0)
                first(1)
                second(0)
                first(2)
                second(1)
                second(2)

            def prep_chunk(k):
                def normed(i):
                    act.wait_ge(s_ntt, k.of(NT3, i + 1))
                    for c in range(CT):
                        last = V.activation(ntile[i][:, c, :], pt[(i + 1) % 2][:, c * 128:(c + 1) * 128], ACT.Identity,
                                            scale=lnp[:, 0, c:c + 1], bias=lnp[:, 1, c:c + 1])
                    last.then_inc(s_nte, 1)

                def projected(i):
                    act.wait_ge(s_pj, k.of(NT3, i + 1))
                    wait(act, s_pst, k.of(16 * NT3, 0))
                    V.activation(pr[i][:], pj[:], ACT.Copy).then_inc(s_pre, 1)

                staggered(normed, projected)
                wait(act, s_h3, k.of(1, -1))
                for i in range(NT3):
                    last = V.activation(base[k.par][:, i, :], h2[k.par][:, i, :], ACT.Identity,
                                        scale=onep[:, i:i + 1], bias=shift1[:, 0, i:i + 1])
                last.then_inc(s_base, 1)

            def keys_and_betas(k):
                d = D[k.par]
                act.wait_ge(s_dl[k.par], k.half(16 * HG, 16 * HG))
                V.activation(ksq[:], d[:, :, HD:2 * HD], ACT.Square).then_inc(s_sq, 1)
                V.activation(bab[:], d[:, :, 3 * HD:4 * HD], ACT.Abs).then_inc(s_a, 1)
                act.wait_ge(s_a, k.of(3, 1))
                V.activation(bab[:], bab[:], ACT.Exp, scale=-1.0).then_inc(s_a, 1)
                act.wait_ge(s_a, k.of(3, 2))
                V.activation(bab[:], bab[:], ACT.Ln, bias=epsc[:, 2:3]).then_inc(s_sp, 1)

            def keys_and_betas_end(k):
                d = D[k.par]
                act.wait_ge(s_ss, k.of(1, 1))
                V.activation(inv[:], ss[:], ACT.Ln).then_inc(s_a, 1)
                act.wait_ge(s_a, k.of(3, 3))
                V.activation(inv[:], inv[:], ACT.Exp, scale=-0.5).then_inc(s_inv, 1)
                act.wait_ge(s_bl, k.of(1, 1))
                V.activation(d[:, :, 3 * HD:4 * HD], d[:, :, 3 * HD:4 * HD], ACT.Exp).then_inc(s_beta, 1)

            def attention_rows(k):
                def turned(i):
                    act.wait_ge(s_ott, k.of(NT3, i + 1))
                    V.activation(ott[i][:].rearrange("p c n -> p (c n)"), pt[i % 2][:, 0:C], ACT.Copy).then_inc(s_ote, 1)

                def multiplied(i):
                    act.wait_ge(s_wo, k.of(NT3, i + 1))
                    if i == 0:
                        wait(act, s_h3, k.of(1, 0))
                    V.activation(wo[:, i, :], py[:, 0:C], ACT.Copy).then_inc(s_woe, 1)

                staggered(turned, multiplied)

            def weights(k):
                act.wait_ge(s_f, k.of(BANKS, 1))
                V.activation(wt[:].rearrange("p i n -> p (i n)"), pf[k.par][0:E8, 0:NT3 * 128], ACT.Copy).then_inc(s_fe, 1)

            def weigh_tile(k, i):
                act.wait_ge(s_wm, k.of(1, 1))
                for e in range(E8):
                    last = V.activation(xw[(k.par + i) % 2][:, e, :], dd[k.par][:, i, :], ACT.Copy, scale=wm[:, i, e:e + 1])
                last.then_inc(s_xw, 1)

            def routed_tile(k, i):
                n0 = 1 + i * E8 // 2
                for q in range(E8 // 2):
                    act.wait_ge(s_f, k.of(BANKS, n0 + q + 1))
                    V.activation(xt[q % 2][:].rearrange("p e c n -> p (e c n)"), pf[(k.par + n0 + q) % 2][:], ACT.Copy).then_inc(s_fe, 1)
                act.wait_ge(s_yd, k.of(NT3, i + 1))
                wait(act, s_od, k.of(16 * NT3, 0))
                V.activation(outb[:, i, :], py[:, 0:C], ACT.Copy).then_inc(s_oe, 1)
                act.wait_ge(s_oe, k.of(NT3, i + 1))
                if k.it is None and k.off == NCH - 1 and i == NT3 - 1:
                    n = T - (NCH * CH - TT)
                    act.dma_start(out_t[T - n:T], outb[0:32 * n, i, :]).then_inc(s_od, 16)
                else:
                    act.dma_start(out_t[bass.ds(k.of(CH, TT * i), TT)], outb[:, i, :]).then_inc(s_od, 16)

            def body(c, prep, delta, post, routed):
                if routed:
                    weights(c + (-2))
                    if post:
                        weigh_tile(c + (-2), 1)
                    routed_tile(c + (-2), 0)
                if post:
                    attention_rows(c + (-1))
                if prep:
                    norm_rows(c + 1)
                    prep_chunk(c + 1)
                if routed:
                    routed_tile(c + (-2), 1)
                    if post:
                        weigh_tile(c + (-2), 2)
                if prep:
                    keys_and_betas(c + 1)
                if post:
                    norm_d(c + (-1))
                if routed and not (post and not delta):
                    routed_tile(c + (-2), 2)
                if post:
                    k = c + (-1)
                    for i in range(NT3):
                        act.wait_ge(s_dtt, k.of(NT3, i + 1))
                        V.activation(dtile[i][:].rearrange("p c n -> p (c n)"), pt[i % 2][:, 0:C], ACT.Copy).then_inc(s_dte, 1)
                    act.wait_ge(s_ls, k.of(1, 1))
                    V.activation(ex[:], lgs[:], ACT.Exp).then_inc(s_ex, 1)
                if routed and post and not delta:
                    routed_tile(c + (-2), 2)
                if prep:
                    keys_and_betas_end(c + 1)
                if post and delta:
                    weigh_tile(c + (-1), 0)
                if delta:
                    wait(act, s_ost, c.of(16 * HG, -16 * HG))
                    for n0, n, src in ((0, 2 * OB, po[:]), (2 * OB, OB, pt[1][:, OB * HD:])):
                        act.wait_ge(s_red, c.of(NOB, (n0 + n) // OB))
                        V.activation(O[c.par][:, n0:n0 + n, :].rearrange("p t n -> p (t n)"), src, ACT.Copy).then_inc(s_oev, 1)

            def prologue():
                norm_rows(Turn(0))
                prep_chunk(Turn(0))
                keys_and_betas(Turn(0))
                keys_and_betas_end(Turn(0))

            schedule(act, body, prologue)

        @block.vector
        def _(dve):
            V = nc.vector
            pre = Chain(dve, s_v)
            dve.wait_ge(s_cst, 6)
            dve.wait_ge(s_bld, 16)
            def split_bias():
                dve.wait_ge(s_ld, 16 * 4)
                pre.then(V.tensor_copy(bpart[0][:], bias[:]))
                pre.then(V.tensor_tensor(brest[0], bias[:], bpart[0][:], ALU.subtract))
                pre.then(V.tensor_copy(bpart[1][:], brest[0]))
                pre.then(V.tensor_tensor(brest[1], brest[0], bpart[1][:], ALU.subtract))
                pre.then(V.tensor_copy(bpart[2][:], brest[1]))
                pre.then(V.tensor_scalar(brest[0], bpart[0][:], ident[0:3, 0:1], None, ALU.mult))
                pre.then(V.scalar_tensor_tensor(brest[1], bpart[1][:], ident[0:3, 1:2], brest[0], ALU.mult, ALU.add))
                V.scalar_tensor_tensor(brow[:], bpart[2][:], ident[0:3, 2:3], brest[1], ALU.mult, ALU.add).then_inc(s_bias, 1)

            class Link:

                def __init__(self, sem_, per):
                    self.sem, self.per = sem_, per

                def start(self, k):
                    self.k, self.n = k, 0

                def mark(self, ins):
                    self.n += 1
                    ins.then_inc(self.sem, 1)

                def wait(self):
                    dve.wait_ge(self.sem, self.k.of(self.per, self.n))

                def then(self, ins):
                    self.mark(ins)
                    self.wait()

                def end(self):
                    assert self.n == self.per, (self.n, self.per)

            l_st1, l_st3, l_step, l_rt, l_kb = Link(s_l1, 1), Link(s_l3, 1), Link(s_lstep, 5 * CH), Link(s_lrt, 7), Link(s_lkb, 1)

            def stats(k, x, st, mv, link, done):
                link.start(k)
                for i in range(NT3):
                    last = V.bn_stats(st[:, i, :], x[:, i, :])
                link.then(last)
                dve.sem_inc(s_turn, 1)
                for i in range(NT3):
                    last = V.bn_aggr(mv[:, i, :], st[:, i, :])
                last.then_inc(done, 1)
                link.end()

            def step(c, t):
                d, s4 = D[c.par], S[:].rearrange("p (h i j) -> p h i j", h=HH, i=DH)

                def col(n):
                    return d[:, t, n * HD:(n + 1) * HD]

                def along_i(x):
                    return x.rearrange("p (h j) -> p h j", h=HH).unsqueeze(2).broadcast_to([128, HH, DH, DH])

                def heads(x):
                    return x[:].rearrange("p (h i j) -> p h i j", h=HH, i=DH)

                def rows(x):
                    return x[:].rearrange("p (r j) -> p r j", j=DH)

                _, k, v, b = (col(n) for n in range(4))
                l_step.mark(V.tensor_tensor(heads(mk), s4, along_i(k), ALU.mult))
                if t > 0:
                    outputs_products(c, t - 1)
                l_step.wait()
                l_step.mark(V.tensor_reduce(rk[:], rows(mk), AX.X, ALU.add))
                l_step.wait()
                l_step.then(V.tensor_tensor(u1[:], v, rk[:], ALU.subtract))
                l_step.then(V.tensor_tensor(u[:], u1[:], b, ALU.mult))
                l_step.then(V.tensor_tensor(heads(ou), u[:].unsqueeze(2).broadcast_to([128, HD, DH]).rearrange("p (h i) j -> p h i j", h=HH), along_i(k), ALU.mult))
                V.tensor_tensor(S[:], S[:], ou[:], ALU.add).then_inc(s_st, 1)
                dve.wait_ge(s_st, c.of(CH, t + 1))

            def outputs_products(c, t):
                d = D[c.par]
                n = t // OB
                wait(dve, s_red, c.of(NOB, n - 1))
                out = mqp[(c.par + n) % 2][:, t % OB, :]
                V.tensor_tensor(out.rearrange("p (h i j) -> p h i j", h=HH, i=DH), S[:].rearrange("p (h i j) -> p h i j", h=HH, i=DH),
                                d[:, t, 0:HD].rearrange("p (h j) -> p h j", h=HH).unsqueeze(2).broadcast_to([128, HH, DH, DH]),
                                ALU.mult).then_inc(s_mq, 1)

            def steps(c, t0, t1):
                if t0 == 0:
                    dve.wait_ge(s_kn, c.of(1, 1))
                    dve.wait_ge(s_beta, c.of(1, 1))
                    l_step.start(c)
                for t in range(t0, min(t1, steps_of(c))):
                    step(c, t)
                if t1 == CH:
                    outputs_products(c, steps_of(c) - 1)

            def keys_sums(k):
                l_kb.start(k)
                dve.wait_ge(s_sq, k.of(1, 1))
                l_kb.then(V.tensor_reduce(ss[:], ksq[:].rearrange("p t (h j) -> p (t h) j", h=HH), AX.X, ALU.add))
                V.tensor_scalar(ss[:], ss[:], 1e-12, None, ALU.max).then_inc(s_ss, 1)
                dve.wait_ge(s_sp, k.of(1, 1))
                b = D[k.par][:, :, 3 * HD:4 * HD]
                V.scalar_tensor_tensor(b, b, 0.0, bab[:], ALU.min, ALU.subtract).then_inc(s_bl, 1)
                l_kb.end()

            def keys_end(k):
                dve.wait_ge(s_inv, k.of(1, 1))
                kk = D[k.par][:, :, HD:2 * HD].rearrange("p t (h j) -> p t h j", h=HH)
                V.tensor_tensor(kk, kk, inv[:].rearrange("p (t h) -> p t h", h=HH).unsqueeze(3).broadcast_to([128, CH, HH, DH]), ALU.mult).then_inc(s_kn, 1)

            def add_base(k):
                dve.wait_ge(s_woe, k.of(NT3, NT3))
                dve.wait_ge(s_base, k.of(1, 1))
                wait(dve, s_yd, k.of(NT3, -NT3))
                V.tensor_tensor(h3[k.par][:], wo[:], base[k.par][:], ALU.add).then_inc(s_h3, 1)
                dve.wait_ge(s_h3, k.of(1, 1))
                stats(k, h3[k.par], st3, mv3, l_st3, s_st3)

            def over8(x):
                return x.unsqueeze(2).broadcast_to([128, NT3, E8])

            def router_a(k):
                l_rt.start(k)
                lg = py[:, C:C + NT3 * E8].rearrange("p (i e) -> p i e", e=E8)
                dve.wait_ge(s_lg, k.of(1, 1))
                l_rt.then(V.tensor_reduce(mx[:], lg, AX.X, ALU.max))
                V.tensor_tensor(lgs[:], lg, over8(mx[:]), ALU.subtract).then_inc(s_ls, 1)

            def router_b(k):
                dve.wait_ge(s_ex, k.of(1, 1))
                l_rt.then(V.tensor_reduce(sm[:], ex[:], AX.X, ALU.add))
                l_rt.then(V.reciprocal(rc[:], sm[:]))
                dve.wait_ge(s_ls, k.of(1, 1))
                l_rt.then(V.tensor_scalar(mask[:], lgs[:], 0.0, None, ALU.is_equal))
                l_rt.then(V.tensor_tensor(mask[:], mask[:], rev[:].unsqueeze(1).broadcast_to([128, NT3, E8]), ALU.mult))
                l_rt.then(V.tensor_reduce(mr[:], mask[:], AX.X, ALU.max))
                l_rt.then(V.tensor_tensor(mask[:], mask[:], over8(mr[:]), ALU.is_equal))
                wait(dve, s_yd, k.of(NT3, 0))
                V.tensor_tensor(wm[:], mask[:], over8(rc[:]), ALU.mult).then_inc(s_wm, 1)
                l_rt.end()

            def stats1(k):
                dve.wait_ge(s_h2[k.par], k.half(16 * NT3, 16 * NT3))
                stats(k, h2[k.par], st1, mv1, l_st1, s_st1)

            def body(c, prep, delta, post, routed):
                if delta:
                    steps(c, 0, 2)
                if prep:
                    stats1(c + 1)
                if delta:
                    steps(c, 2, 5)
                if post:
                    add_base(c + (-1))
                if delta:
                    steps(c, 5, 8)
                if delta:
                    steps(c, 8, 11)
                if prep:
                    keys_sums(c + 1)
                if delta:
                    steps(c, 11, CH)
                if post:
                    router_a(c + (-1))
                if prep:
                    keys_end(c + 1)
                if post:
                    router_b(c + (-1))
                if post and not delta:
                    last_rows(c + (-1))

            def last_rows(k):
                dve.wait_ge(s_wm, k.of(1, 1))
                for i in range(NT3):
                    dve.wait_ge(s_yd, k.of(NT3, i - 1))
                    for e in range(E8):
                        last = V.tensor_scalar(xw[(k.par + i) % 2][:, e, :], dd[k.par][:, i, :], wm[:, i, e:e + 1], None, ALU.mult)
                    last.then_inc(s_xw, 1)

            def prologue():
                stats1(Turn(0))
                split_bias()
                keys_sums(Turn(0))
                keys_end(Turn(0))

            schedule(dve, body, prologue)


def build(nc, A, out):
    def scratch(name, shape):
        return nc.dram_tensor(name, shape, fp32, kind="Internal").ap()

    z_rows, acc_rows = scratch("z_rows", (NROW, C)), scratch("acc_rows", (NROW, C))
    score_rows = scratch("score_rows", (E8, NROW))
    with nc.semaphore("turn") as s_turn:
        phase_tokens(nc, A, s_turn, z_rows, acc_rows, score_rows)
        phase_experts(nc, A, s_turn, z_rows, acc_rows, score_rows)
        phase_delta(nc, A, s_turn, acc_rows, scratch("proj_rows", (TD, B, 4 * C)), scratch("o_rows", (TD, B, C)), out)


def layouts(i):
    def slices(w, n=128):
        return w.reshape(-1, n, *w.shape[1:]).swapaxes(0, 1)

    def by_group(w):
        return w.reshape(*w.shape[:-1], 4, HG, HD).swapaxes(-3, -2).reshape(*w.shape[:-1], 4 * C)

    a, f = "L0_attn_", "L0_ffn_"
    d = {n: i[n] for n in ("x_txt", "L0_txt_W", "L0_tok_cls_token", "L0_attn_w_tk", "L0_attn_w_tv", "L0_attn_w_tr",
                           "L0_attn_w_ck", "L0_attn_w_cv", "L0_attn_w_cr", "L1_attn_w_out", "L1_ffn_expert_b")}
    p = i["x"].reshape(PAIRS, 2, 3, 6, 16, 6, 16).transpose(0, 2, 4, 6, 1, 3, 5).reshape(PAIRS, PK, 128, 2 * NIMG)
    d["patches"] = p.transpose(0, 2, 1, 3)
    d["wtok_t"] = slices(i["L0_tok_w"].T)
    d["emb_t"] = i["L0_txt_emb_tables"].transpose(2, 0, 1)
    d["pos_t"] = slices(np.concatenate([i["L0_tok_pos"], i["L0_txt_pos_table"][:NTXT]], 0).T)
    vectors = [i["L0_tok_b"], i["L0_txt_b"]] + [i[a + n].reshape(-1) for n in (
        "time_decay", "time_first", "ln1_g", "ln1_b", "ln2_g", "ln2_b", "mix_k", "mix_v", "mix_r", "cmix_k", "cmix_r")]
    d["prm"] = np.stack(vectors).reshape(len(vectors), CT, 128).transpose(2, 0, 1)
    d["gate_t"] = slices(i[f + "gate_w"].T)
    w1 = i[f + "fc1s"].transpose(0, 2, 1).reshape(E8, CT, 128, F1).transpose(0, 2, 1, 3).reshape(E8, 128, CT * F1)
    d["w1"] = np.concatenate([w1, i[f + "b1s"].reshape(E8, FT, 128).transpose(0, 2, 1)], 2)
    d["w2"] = i[f + "fc2s"].transpose(0, 2, 1).reshape(E8, FT, 128, C).transpose(0, 2, 1, 3)
    d["b2"] = i[f + "b2s"]
    d["ffn_ln"] = np.stack([i[f + "ln_gamma"], i[f + "ln_beta"]]).reshape(2, CT, 128).transpose(2, 0, 1)
    d["wqkvb"] = slices(by_group(i["L1_attn_w_qkvb"]))
    d["wrt"] = slices(i["L1_ffn_router_w"].T)
    d["wex"] = slices(i["L1_ffn_expert_w"].transpose(2, 0, 1).reshape(C, E8 * C))
    d["b_row"] = np.concatenate([by_group(i["L1_attn_b_qkvb"]), i["L1_attn_b_out"], i["L1_ffn_router_b"]])[None]
    d["l1_ln"] = np.stack([i["L1_attn_ln_g"], i["L1_attn_ln_b"]]).reshape(2, CT, 128).transpose(2, 0, 1)
    f4 = np.float32
    d["ident"], d["tri"] = np.eye(128, dtype=f4), np.triu(np.ones((SP_P, SP_P), f4), 1)
    d["rowid"], d["tokp"] = np.arange(VOCAB, dtype=f4)[:, None], np.arange(SP_P, dtype=f4)[:, None]
    d["iota"], d["rev"] = np.arange(128, dtype=f4)[None], np.arange(E8, 0, -1, dtype=f4)[None]
    d["limit"] = np.where(np.arange(NROW) % TD < T, 2.0, -1.0).astype(f4).reshape(SP_P, SP_C)
    return {n: np.ascontiguousarray(v) for n, v in d.items()}


def kernel(**inputs):
    from concourse.bass_utils import run_bass_kernel_spmd
    import concourse.bacc as bacc

    data = layouts({n: np.asarray(v) for n, v in inputs.items()})
    nc = bacc.Bacc("TRN2", target_bir_lowering=False, num_devices=1)
    A = {n: nc.dram_tensor("in_" + n, v.shape, mybir.dt.from_np(v.dtype), kind="ExternalInput").ap() for n, v in data.items()}
    out = nc.dram_tensor("out_0_dram", (B, T, C), fp32, kind="ExternalOutput").ap()
    build(nc, A, out)
    r = run_bass_kernel_spmd(nc, [{"in_" + n: v for n, v in data.items()}], core_ids=[0])
    return r.results[0]["out_0_dram"]
```
